# Optimizing a Trainium2 kernel written in Bass

```python
import numpy as np
import jax
import jax.numpy as jnp

def _softmax(x, axis=-1):
    return jax.nn.softmax(x, axis=axis)

def _gelu(x):
    return jax.nn.gelu(x, approximate=True)

def _silu(x):
    return jax.nn.silu(x)

def _sigmoid(x):
    return jax.nn.sigmoid(x)

def _layernorm(x, axis=-1, eps=1e-05):
    m = jnp.mean(x, axis=axis, keepdims=True)
    v = jnp.var(x, axis=axis, keepdims=True)
    return (x - m) / jnp.sqrt(v + eps)

def _scatter_add(tgt, idx, src, axis=0):
    return tgt.at[idx].add(src)

def _segment_sum(src, seg, n):
    return jax.ops.segment_sum(src, seg, n)
kernel_name = 'mk_xattn_ffn_d2_seqx_r4_240d0e'

def setup_inputs(seed: int=0):
    np.random.seed(seed)
    _w = jnp.asarray

    def _rec_inputs():
        import jax
        import jax.numpy as jnp
        _rk = jax.random.key(seed)
        x = 7.22e-05 + 1 * jax.random.normal(jax.random.fold_in(_rk, 1), (16, 112, 512), jnp.float32)
        _lenS = 112 - jax.random.randint(jax.random.fold_in(_rk, 7), (16,), 0, max(1, 112 // 4) + 1, jnp.int32)
        _lenS2 = 375 - jax.random.randint(jax.random.fold_in(_rk, 8), (16,), 0, max(1, 375 // 4) + 1, jnp.int32)
        _ctx_1024P = jax.random.normal(jax.random.fold_in(_rk, 11), (16, 16, 256), jnp.float32)
        _ctx_1024c = jax.random.dirichlet(jax.random.fold_in(_rk, 511), 0.3 * jnp.ones((16,), jnp.float32), (16, 375))
        _ctx_1024t = jnp.einsum('bsk,bkd->bsd', _ctx_1024c, _ctx_1024P)
        _ctx_1024t = _ctx_1024t * jax.lax.rsqrt(jnp.mean(jnp.square(_ctx_1024t)) + 1e-12) * 0.953939
        ctx_1024 = -0.000673644 + 1.00013 * (_ctx_1024t + 0.3 * jax.random.normal(jax.random.fold_in(_rk, 611), (16, 375, 256), jnp.float32))
        return (x, ctx_1024)
    x, ctx_1024 = _rec_inputs()

    def _L0_xattn_setup():
        import jax, jax.numpy as jnp
        import numpy as np
        B, S1, S2, DCA = (2, 512, 256, 16)
        QDIM, KDIM, H = (512, 256, 16)
        HD = QDIM // H
        SCALE = HD ** (-0.5)
        EPS = 1e-06
        DCA_WEIGHT = 1.0

        def _ln(t, w, b):
            m = jnp.mean(t, axis=-1, keepdims=True)
            v = jnp.var(t, axis=-1, keepdims=True)
            return (t - m) * jax.lax.rsqrt(v + EPS) * w + b

        def _attn(q, k, v):
            s = jnp.einsum('bhqd,bhkd->bhqk', q, k) * SCALE
            p = jax.nn.softmax(s, axis=-1)
            return jnp.einsum('bhqk,bhkd->bhqd', p, v)
        key = jax.random.key(seed)
        ks = jax.random.split(key, 8)
        w = lambda k, shape: jax.random.normal(k, shape, jnp.float32) * 0.02
        return {'x': jax.random.normal(ks[0], (B, S1, QDIM), jnp.float32), 'y': jax.random.normal(ks[1], (B, S2 + DCA, KDIM), jnp.float32), 'Wq': w(ks[2], (QDIM, QDIM)), 'bq': jnp.zeros((QDIM,), jnp.float32), 'Wk': w(ks[3], (KDIM, QDIM)), 'bk': jnp.zeros((QDIM,), jnp.float32), 'Wv': w(ks[4], (KDIM, QDIM)), 'bv': jnp.zeros((QDIM,), jnp.float32), 'Wkv_dca': w(ks[5], (KDIM, 2 * QDIM)), 'bkv_dca': jnp.zeros((2 * QDIM,), jnp.float32), 'qn_w': jnp.ones((HD,), jnp.float32), 'qn_b': jnp.zeros((HD,), jnp.float32), 'kn_w': jnp.ones((HD,), jnp.float32), 'kn_b': jnp.zeros((HD,), jnp.float32), 'kn_dca_w': jnp.ones((HD,), jnp.float32), 'kn_dca_b': jnp.zeros((HD,), jnp.float32), 'Wo': w(ks[6], (QDIM, QDIM)), 'bo': jnp.zeros((QDIM,), jnp.float32)}
    _L0_xattn_all = _L0_xattn_setup()
    _L0_xattn_in = {k: v for k, v in _L0_xattn_all.items() if k in ('Wq', 'bq', 'Wk', 'bk', 'Wv', 'bv', 'Wkv_dca', 'bkv_dca', 'qn_w', 'qn_b', 'kn_w', 'kn_b', 'kn_dca_w', 'kn_dca_b', 'Wo', 'bo')}
    del _L0_xattn_all

    def _L0_ffn_setup():
        import jax, jax.numpy as jnp
        import numpy as np
        B, T, D = (4, 256, 512)
        N, S, H = (8, 8, 8)
        ETA = 1.0
        key = jax.random.key(seed)
        ks = jax.random.split(key, 9)
        return {'x': jax.random.normal(ks[0], (B, T, D), jnp.float32), 'select_weight': jax.random.normal(ks[1], (N, D, S), jnp.float32) / D, 'select_mean_diff': jax.random.normal(ks[2], (N, D), jnp.float32) / D, 'imp_center': jax.random.normal(ks[3], (N,), jnp.float32), 'imp_slope': jax.random.normal(ks[4], (N,), jnp.float32) * 5.0, 'lora_update': jax.random.normal(ks[5], (N, D, H), jnp.float32) * 0.02, 'lora_degen': jax.random.normal(ks[6], (N, D, H), jnp.float32) * 0.02, 'bias_w': jax.random.normal(ks[7], (N, D), jnp.float32) * 0.02, 'debias_w': jax.random.normal(ks[8], (N, D), jnp.float32) * 0.02}
    _L0_ffn_all = _L0_ffn_setup()
    _L0_ffn_in = {k: v for k, v in _L0_ffn_all.items() if k in ('select_weight', 'select_mean_diff', 'imp_center', 'imp_slope', 'lora_update', 'lora_degen', 'bias_w', 'debias_w')}
    del _L0_ffn_all

    def _L1_xattn_setup():
        import jax, jax.numpy as jnp
        import numpy as np
        EPS = 1e-05

        def rmsnorm(x, g, eps=EPS):
            var = jnp.mean(jnp.square(x), axis=-1, keepdims=True)
            return x * jax.lax.rsqrt(var + eps) * g
        key = jax.random.key(seed)
        ks = jax.random.split(key, 8)
        B, Sq, Skv = (2, 1024, 128)
        dim, cdim, H, D = (512, 256, 16, 128)
        inner = H * D
        s = lambda f: 1.0 / np.sqrt(f)
        return {'hidden_states': jax.random.normal(ks[0], (B, Sq, dim), jnp.float32), 'encoder_hidden_states': jax.random.normal(ks[1], (B, Skv, cdim), jnp.float32), 'Wq': jax.random.normal(ks[2], (dim, inner), jnp.float32) * s(dim), 'Wk': jax.random.normal(ks[3], (cdim, inner), jnp.float32) * s(cdim), 'Wv': jax.random.normal(ks[4], (cdim, inner), jnp.float32) * s(cdim), 'Wo': jax.random.normal(ks[5], (inner, dim), jnp.float32) * s(inner), 'gq': jnp.ones((D,), jnp.float32), 'gk': jnp.ones((D,), jnp.float32)}
    _L1_xattn_all = _L1_xattn_setup()
    _L1_xattn_in = {k: v for k, v in _L1_xattn_all.items() if k in ('Wq', 'Wk', 'Wv', 'Wo', 'gq', 'gk')}
    del _L1_xattn_all

    def _L1_ffn_setup():
        import jax, jax.numpy as jnp
        import numpy as np
        B, L, D = (2, 256, 512)
        E, TOP_K, RANK, DFF = (8, 2, 8, 1376)

        def _lora(x, A, Bm, scale):
            return x @ A @ Bm * scale

        def _expert_lora(x, A, Bm, w, scale):
            xA = jnp.einsum('bld,edr->bler', x, A)
            xAB = jnp.einsum('bler,erd->bled', xA, Bm) * scale
            return (xAB * w).sum(axis=2)
        key = jax.random.key(seed)
        ks = jax.random.split(key, 18)
        r = lambda k, s, sc: jax.random.normal(k, s, dtype=jnp.float32) * sc
        inv_d = 1.0 / np.sqrt(D)
        inv_f = 1.0 / np.sqrt(DFF)
        return {'x': r(ks[0], (B, L, D), 1.0), 'W_router': r(ks[1], (D, E), inv_d), 'W_gate': r(ks[2], (D, DFF), inv_d), 'W_up': r(ks[3], (D, DFF), inv_d), 'W_down': r(ks[4], (DFF, D), inv_f), 'sA_gate': r(ks[5], (D, RANK), inv_d), 'sB_gate': r(ks[6], (RANK, DFF), 0.02), 'sA_up': r(ks[7], (D, RANK), inv_d), 'sB_up': r(ks[8], (RANK, DFF), 0.02), 'sA_down': r(ks[9], (DFF, RANK), inv_f), 'sB_down': r(ks[10], (RANK, D), 0.02), 'A_gate': r(ks[11], (E, D, RANK), inv_d), 'B_gate': r(ks[12], (E, RANK, DFF), 0.02), 'A_up': r(ks[13], (E, D, RANK), inv_d), 'B_up': r(ks[14], (E, RANK, DFF), 0.02), 'A_down': r(ks[15], (E, DFF, RANK), inv_f), 'B_down': r(ks[16], (E, RANK, D), 0.02), 'expert_bias': jnp.zeros((E,), dtype=jnp.float32)}
    _L1_ffn_all = _L1_ffn_setup()
    _L1_ffn_in = {k: v for k, v in _L1_ffn_all.items() if k in ('W_router', 'W_gate', 'W_up', 'W_down', 'sA_gate', 'sB_gate', 'sA_up', 'sB_up', 'sA_down', 'sB_down', 'A_gate', 'B_gate', 'A_up', 'B_up', 'A_down', 'B_down', 'expert_bias')}
    del _L1_ffn_all
    return {'x': x, 'ctx_1024': ctx_1024, 'L0_xattn_Wq': _L0_xattn_in['Wq'], 'L0_xattn_bq': _L0_xattn_in['bq'], 'L0_xattn_Wk': _L0_xattn_in['Wk'], 'L0_xattn_bk': _L0_xattn_in['bk'], 'L0_xattn_Wv': _L0_xattn_in['Wv'], 'L0_xattn_bv': _L0_xattn_in['bv'], 'L0_xattn_Wkv_dca': _L0_xattn_in['Wkv_dca'], 'L0_xattn_bkv_dca': _L0_xattn_in['bkv_dca'], 'L0_xattn_qn_w': _L0_xattn_in['qn_w'], 'L0_xattn_qn_b': _L0_xattn_in['qn_b'], 'L0_xattn_kn_w': _L0_xattn_in['kn_w'], 'L0_xattn_kn_b': _L0_xattn_in['kn_b'], 'L0_xattn_kn_dca_w': _L0_xattn_in['kn_dca_w'], 'L0_xattn_kn_dca_b': _L0_xattn_in['kn_dca_b'], 'L0_xattn_Wo': _L0_xattn_in['Wo'], 'L0_xattn_bo': _L0_xattn_in['bo'], 'L0_ffn_select_weight': _L0_ffn_in['select_weight'], 'L0_ffn_select_mean_diff': _L0_ffn_in['select_mean_diff'], 'L0_ffn_imp_center': _L0_ffn_in['imp_center'], 'L0_ffn_imp_slope': _L0_ffn_in['imp_slope'], 'L0_ffn_lora_update': _L0_ffn_in['lora_update'], 'L0_ffn_lora_degen': _L0_ffn_in['lora_degen'], 'L0_ffn_bias_w': _L0_ffn_in['bias_w'], 'L0_ffn_debias_w': _L0_ffn_in['debias_w'], 'L1_xattn_Wq': _L1_xattn_in['Wq'], 'L1_xattn_Wk': _L1_xattn_in['Wk'], 'L1_xattn_Wv': _L1_xattn_in['Wv'], 'L1_xattn_Wo': _L1_xattn_in['Wo'], 'L1_xattn_gq': _L1_xattn_in['gq'], 'L1_xattn_gk': _L1_xattn_in['gk'], 'L1_ffn_W_router': _L1_ffn_in['W_router'], 'L1_ffn_W_gate': _L1_ffn_in['W_gate'], 'L1_ffn_W_up': _L1_ffn_in['W_up'], 'L1_ffn_W_down': _L1_ffn_in['W_down'], 'L1_ffn_sA_gate': _L1_ffn_in['sA_gate'], 'L1_ffn_sB_gate': _L1_ffn_in['sB_gate'], 'L1_ffn_sA_up': _L1_ffn_in['sA_up'], 'L1_ffn_sB_up': _L1_ffn_in['sB_up'], 'L1_ffn_sA_down': _L1_ffn_in['sA_down'], 'L1_ffn_sB_down': _L1_ffn_in['sB_down'], 'L1_ffn_A_gate': _L1_ffn_in['A_gate'], 'L1_ffn_B_gate': _L1_ffn_in['B_gate'], 'L1_ffn_A_up': _L1_ffn_in['A_up'], 'L1_ffn_B_up': _L1_ffn_in['B_up'], 'L1_ffn_A_down': _L1_ffn_in['A_down'], 'L1_ffn_B_down': _L1_ffn_in['B_down'], 'L1_ffn_expert_bias': _L1_ffn_in['expert_bias']}

def reference(x, ctx_1024, L0_xattn_Wq, L0_xattn_bq, L0_xattn_Wk, L0_xattn_bk, L0_xattn_Wv, L0_xattn_bv, L0_xattn_Wkv_dca, L0_xattn_bkv_dca, L0_xattn_qn_w, L0_xattn_qn_b, L0_xattn_kn_w, L0_xattn_kn_b, L0_xattn_kn_dca_w, L0_xattn_kn_dca_b, L0_xattn_Wo, L0_xattn_bo, L0_ffn_select_weight, L0_ffn_select_mean_diff, L0_ffn_imp_center, L0_ffn_imp_slope, L0_ffn_lora_update, L0_ffn_lora_degen, L0_ffn_bias_w, L0_ffn_debias_w, L1_xattn_Wq, L1_xattn_Wk, L1_xattn_Wv, L1_xattn_Wo, L1_xattn_gq, L1_xattn_gk, L1_ffn_W_router, L1_ffn_W_gate, L1_ffn_W_up, L1_ffn_W_down, L1_ffn_sA_gate, L1_ffn_sB_gate, L1_ffn_sA_up, L1_ffn_sB_up, L1_ffn_sA_down, L1_ffn_sB_down, L1_ffn_A_gate, L1_ffn_B_gate, L1_ffn_A_up, L1_ffn_B_up, L1_ffn_A_down, L1_ffn_B_down, L1_ffn_expert_bias):
    import jax
    import jax.numpy as jnp

    def _L0_xattn_ref(x, y, Wq, bq, Wk, bk, Wv, bv, Wkv_dca, bkv_dca, qn_w, qn_b, kn_w, kn_b, kn_dca_w, kn_dca_b, Wo, bo):
        import jax, jax.numpy as jnp
        import numpy as np
        B, S1, S2, DCA = (2, 512, 256, 16)
        QDIM, KDIM, H = (512, 256, 16)
        HD = QDIM // H
        SCALE = HD ** (-0.5)
        EPS = 1e-06
        DCA_WEIGHT = 1.0

        def _ln(t, w, b):
            m = jnp.mean(t, axis=-1, keepdims=True)
            v = jnp.var(t, axis=-1, keepdims=True)
            return (t - m) * jax.lax.rsqrt(v + EPS) * w + b

        def _attn(q, k, v):
            s = jnp.einsum('bhqd,bhkd->bhqk', q, k) * SCALE
            p = jax.nn.softmax(s, axis=-1)
            return jnp.einsum('bhqk,bhkd->bhqd', p, v)
        b, s1, _ = x.shape
        y_dca = y[:, -DCA:, :]
        y_main = y[:, :-DCA, :]
        kv_dca = (y_dca @ Wkv_dca + bkv_dca).reshape(b, DCA, 2, H, HD)
        k_dca = _ln(kv_dca[:, :, 0], kn_dca_w, kn_dca_b)
        v_dca = kv_dca[:, :, 1]
        s2 = y_main.shape[1]
        q = _ln((x @ Wq + bq).reshape(b, s1, H, HD), qn_w, qn_b)
        kv = jnp.concatenate([y_main @ Wk + bk, y_main @ Wv + bv], axis=-1)
        kv = kv.reshape(b, s2, H, 2 * HD)
        k = _ln(kv[..., :HD], kn_w, kn_b)
        v = kv[..., HD:]
        qT = q.transpose(0, 2, 1, 3)
        ctx = _attn(qT, k.transpose(0, 2, 1, 3), v.transpose(0, 2, 1, 3))
        ctx = ctx.transpose(0, 2, 1, 3).reshape(b, s1, QDIM)
        ctx_dca = _attn(qT, k_dca.transpose(0, 2, 1, 3), v_dca.transpose(0, 2, 1, 3))
        ctx_dca = ctx_dca.transpose(0, 2, 1, 3).reshape(b, s1, QDIM)
        ctx = ctx + DCA_WEIGHT * ctx_dca
        return ctx @ Wo + bo

    def _L0_ffn_ref(x, select_weight, select_mean_diff, imp_center, imp_slope, lora_update, lora_degen, bias_w, debias_w):
        import jax, jax.numpy as jnp
        import numpy as np
        B, T, D = (4, 256, 512)
        N, S, H = (8, 8, 8)
        ETA = 1.0
        x_diff = x[:, None, :, :] - select_mean_diff[None, :, None, :]
        x_diff = x_diff / jnp.linalg.norm(x_diff, axis=3, keepdims=True)
        cont = jnp.einsum('nds,bntd->bnts', select_weight, x_diff) ** 2
        score = cont.sum(axis=-1)
        gate = jax.nn.sigmoid(imp_slope[None, :, None] * (score - imp_center[None, :, None]))
        sel_scale = gate.max(axis=1)[..., None]
        sel_idx = gate.argmax(axis=1)
        debias = jnp.take(debias_w, sel_idx, axis=0)
        bias = jnp.take(bias_w, sel_idx, axis=0)
        upd = jnp.take(lora_update, sel_idx, axis=0)
        dgn = jnp.take(lora_degen, sel_idx, axis=0)
        x_debias = x - debias
        mod_x = jnp.einsum('btdh,btd->bth', upd, x_debias)
        degen_up = jnp.einsum('btdh,bth->btd', dgn, mod_x)
        mod_x_bias = ETA * (bias + degen_up)
        return (1.0 - sel_scale) * x + sel_scale * mod_x_bias

    def _L1_xattn_ref(hidden_states, encoder_hidden_states, Wq, Wk, Wv, Wo, gq, gk):
        import jax, jax.numpy as jnp
        import numpy as np
        EPS = 1e-05

        def rmsnorm(x, g, eps=EPS):
            var = jnp.mean(jnp.square(x), axis=-1, keepdims=True)
            return x * jax.lax.rsqrt(var + eps) * g
        B, Sq, _ = hidden_states.shape
        Skv = encoder_hidden_states.shape[1]
        D = gq.shape[0]
        H = Wq.shape[1] // D
        scale = 1.0 / np.sqrt(D)
        q = (hidden_states @ Wq).reshape(B, Sq, H, D)
        k = (encoder_hidden_states @ Wk).reshape(B, Skv, H, D)
        v = (encoder_hidden_states @ Wv).reshape(B, Skv, H, D)
        q = rmsnorm(q, gq)
        k = rmsnorm(k, gk)
        scores = jnp.einsum('bqhd,bkhd->bhqk', q, k) * scale
        attn = jax.nn.softmax(scores, axis=-1)
        out = jnp.einsum('bhqk,bkhd->bqhd', attn, v)
        out = out.reshape(B, Sq, H * D)
        return out @ Wo

    def _L1_ffn_ref(x, W_router, W_gate, W_up, W_down, sA_gate, sB_gate, sA_up, sB_up, sA_down, sB_down, A_gate, B_gate, A_up, B_up, A_down, B_down, expert_bias):
        import jax, jax.numpy as jnp
        import numpy as np
        B, L, D = (2, 256, 512)
        E, TOP_K, RANK, DFF = (8, 2, 8, 1376)

        def _lora(x, A, Bm, scale):
            return x @ A @ Bm * scale

        def _expert_lora(x, A, Bm, w, scale):
            xA = jnp.einsum('bld,edr->bler', x, A)
            xAB = jnp.einsum('bler,erd->bled', xA, Bm) * scale
            return (xAB * w).sum(axis=2)
        scale = 1.0 / RANK
        logits = x @ W_router
        scores = jax.nn.sigmoid(logits)
        biased = scores + expert_bias
        _, topk_idx = jax.lax.top_k(biased, TOP_K)
        topk_scores = jnp.take_along_axis(scores, topk_idx, axis=-1)
        topk_w = topk_scores / (topk_scores.sum(-1, keepdims=True) + 1e-08)
        one_hot = jax.nn.one_hot(topk_idx, E, dtype=x.dtype)
        expert_weights = (one_hot * topk_w[..., None]).sum(axis=2)
        w = expert_weights[..., None]
        gate = x @ W_gate + _lora(x, sA_gate, sB_gate, scale) + _expert_lora(x, A_gate, B_gate, w, scale)
        up = x @ W_up + _lora(x, sA_up, sB_up, scale) + _expert_lora(x, A_up, B_up, w, scale)
        hidden = jax.nn.silu(gate) * up
        out = hidden @ W_down + _lora(hidden, sA_down, sB_down, scale) + _expert_lora(hidden, A_down, B_down, w, scale)
        return out
    x = x + _L0_xattn_ref(_layernorm(x, axis=-1), ctx_1024, L0_xattn_Wq, L0_xattn_bq, L0_xattn_Wk, L0_xattn_bk, L0_xattn_Wv, L0_xattn_bv, L0_xattn_Wkv_dca, L0_xattn_bkv_dca, L0_xattn_qn_w, L0_xattn_qn_b, L0_xattn_kn_w, L0_xattn_kn_b, L0_xattn_kn_dca_w, L0_xattn_kn_dca_b, L0_xattn_Wo, L0_xattn_bo)
    x = x + _L0_ffn_ref(_layernorm(x, axis=-1), L0_ffn_select_weight, L0_ffn_select_mean_diff, L0_ffn_imp_center, L0_ffn_imp_slope, L0_ffn_lora_update, L0_ffn_lora_degen, L0_ffn_bias_w, L0_ffn_debias_w)
    x = x + _L1_xattn_ref(_layernorm(x, axis=-1), ctx_1024, L1_xattn_Wq, L1_xattn_Wk, L1_xattn_Wv, L1_xattn_Wo, L1_xattn_gq, L1_xattn_gk)
    x = x + _L1_ffn_ref(_layernorm(x, axis=-1), L1_ffn_W_router, L1_ffn_W_gate, L1_ffn_W_up, L1_ffn_W_down, L1_ffn_sA_gate, L1_ffn_sB_gate, L1_ffn_sA_up, L1_ffn_sB_up, L1_ffn_sA_down, L1_ffn_sB_down, L1_ffn_A_gate, L1_ffn_B_gate, L1_ffn_A_up, L1_ffn_B_up, L1_ffn_A_down, L1_ffn_B_down, L1_ffn_expert_bias)
    return x

_drawn_inputs = setup_inputs


def setup_inputs(seed=0):
    import zlib

    import numpy as np

    out = dict(_drawn_inputs(seed))
    spreads = {'L0_xattn_bq': (0.0, 0.7),
     'L0_xattn_bk': (0.0, 0.1),
     'L0_xattn_bv': (0.0, 0.1),
     'L0_xattn_bkv_dca': (0.0, 0.1),
     'L0_xattn_qn_w': (1.0, 0.6),
     'L0_xattn_qn_b': (0.0, 0.8),
     'L0_xattn_kn_w': (1.0, 0.6),
     'L0_xattn_kn_b': (0.0, 2.0),
     'L0_xattn_kn_dca_w': (1.0, 0.6),
     'L0_xattn_kn_dca_b': (0.0, 2.0),
     'L0_xattn_bo': (0.0, 0.1),
     'L1_xattn_gq': (1.0, 0.2),
     'L1_xattn_gk': (1.0, 0.2),
     'L1_ffn_expert_bias': (0.0, 0.8)}
    factors = {'L0_ffn_bias_w': 2.838,
     'L0_ffn_debias_w': 23.045,
     'L1_ffn_W_router': 8.0,
     'L1_ffn_sA_gate': 8.0,
     'L1_ffn_sB_gate': 8.0,
     'L1_ffn_sA_up': 8.0,
     'L1_ffn_sB_up': 8.0,
     'L1_ffn_sA_down': 8.0,
     'L1_ffn_sB_down': 8.0,
     'L1_ffn_A_gate': 8.0,
     'L1_ffn_B_gate': 8.0,
     'L1_ffn_A_up': 8.0,
     'L1_ffn_B_up': 8.0,
     'L1_ffn_A_down': 8.0,
     'L1_ffn_B_down': 8.0}
    for name, (base, spread) in spreads.items():
        noise = np.random.default_rng([zlib.crc32(name.encode()), seed]).standard_normal(out[name].shape)
        drawn = base * np.exp(spread * noise) if base else spread * noise
        out[name] = jnp.asarray(drawn.astype(out[name].dtype))
    for name, factor in factors.items():
        out[name] = (out[name] * factor).astype(out[name].dtype)
    return out
```

```python
import concourse.bass as bass
from concourse import mybir
from contextlib import ExitStack

FP32 = mybir.dt.float32
ALU = mybir.AluOpType
ACT = mybir.ActivationFunctionType
AXX = mybir.AxisListType.X

B, S, D, C = 16, 112, 512, 256
KV, ND = 375, 16
NM = KV - ND
P = 128
DT, CT = D // P, C // P
KR = 125
KT = KV // KR
H = 16
G = 4
NG = H // G
HD0 = D // H
HD1 = 128
LN_EPS, QK_EPS, RMS_EPS = 1e-5, 1e-6, 1e-5


class Links:

    def __init__(self, eng, sem, base):
        self.eng, self.sem, self.base, self.n = eng, sem, base, 0

    def mark(self, ins):
        ins.then_inc(self.sem, 1)
        self.n += 1

    def wait(self):
        self.eng.wait_ge(self.sem, self.base + self.n)

    def __call__(self, ins):
        self.mark(ins)
        self.wait()


def tools(nc, ctx, tag):
    def sb(name, shape):
        return ctx.enter_context(nc.sbuf_tensor(f"{tag}_{name}", shape, FP32))

    def bank(name):
        return ctx.enter_context(nc.psum_tensor(f"{tag}_{name}", [P, 512], FP32))

    def sem(name):
        return ctx.enter_context(nc.semaphore(f"{tag}_{name}"))

    return sb, bank, sem


class TokenNorm:

    LINKS = 2

    def __init__(self, sb, sem, neg_half):
        self.stats, self.mean_var, self.root = sb("stats", [S, 6]), sb("mean_var", [S, 2]), sb("root_x", [S, 1])
        self.neg_half, self.variances, self.roots = neg_half, sem("variances"), sem("x_roots")

    def begin(self, dve, link, x):
        link.mark(dve.bn_stats(self.stats[:, :], x))

    def end(self, dve, link):
        link(dve.bn_aggr(self.mean_var[:, :], self.stats[:, :]))
        dve.tensor_scalar(self.mean_var[:, 1:2], self.mean_var[:, 1:2], LN_EPS, None, ALU.add).then_inc(self.variances, 1)

    def root_of(self, pool, b):
        pool.wait_ge(self.variances, b + 1)
        pool.tensor_tensor(self.root[:, :], self.mean_var[:, 1:2], self.neg_half[0:S, :], ALU.pow).then_inc(self.roots, 1)

    def apply(self, dve, b, x, out):
        dve.wait_ge(self.roots, b + 1)
        return dve.tensor_scalar(out, x, self.mean_var[:, 0:1], self.root[:, :], ALU.subtract, ALU.mult)


def phase_constants(nc, ident, neg_half):
    with ExitStack() as ctx:
        _, _, sem = tools(nc, ctx, "id")
        zeroed, made = sem("zeroed"), sem("made")
        block = ctx.enter_context(nc.Block())

        @block.gpsimd
        def _(pool):
            pool.memset(neg_half[:, :], -0.5).then_inc(zeroed, 1)
            pool.memset(ident[:, :], 0.0).then_inc(zeroed, 1)
            pool.wait_ge(zeroed, 2)
            pool.affine_select(out=ident[:, :], in_=ident[:, :], compare_op=ALU.not_equal, fill=1.0, base=0,
                               pattern=[[-1, P]], channel_multiplier=1).then_inc(made, 1)
            pool.wait_ge(made, 1)


def phase_attention0(nc, A, ident, neg_half, x_all, vd_dram):
    SCALE = float(HD0) ** -0.5
    UP, UB = 7, 10
    EP, EB = 4, 7
    AP_, AB = 3, 3
    with ExitStack() as ctx:
        sb, bank, sem = tools(nc, ctx, "a0")
        wq, wk, wv = sb("wq", [P, DT, D]), sb("wk", [P, CT, D]), sb("wv", [P, CT, D])
        wd, wo = sb("wd", [P, CT, 2 * D]), sb("wo", [P, DT, D])
        bq, bk, bv, bd, bo = (sb(n, [P, w]) for n, w in (("bq", D), ("bk", D), ("bv", D), ("bd", 2 * D), ("bo", D)))
        qw, qb = sb("qw", [P, G]), sb("qb", [P, G])
        kw, kb, dw, db = sb("kw", [P, 1]), sb("kb", [P, 1]), sb("dw", [P, 1]), sb("db", [P, 1])
        dcain, dcaT = sb("dcain", [P, 2, C]), sb("dcaT", [P, CT, 2 * P])
        kdT, vd = sb("kdT", [P, NG, B * ND]), sb("vd", [P, 2, D])
        ctxin, ctxT = sb("ctxin", [KR, KT, C]), sb("ctxT", [P, CT, KV])
        xn, xnT = sb("xn", [S, D]), sb("xnT", [P, DT, S])
        raw, cen, sq = sb("raw", [P, 2, D]), sb("cen", [P, 2, D]), sb("sq", [P, 2, D])
        nmean, msq, rstd = sb("nmean", [P, 2, H]), sb("msq", [P, 2, H]), sb("rstd", [P, 2, H])
        kn, qn = sb("kn", [KR, KT, D]), sb("qn", [S, D])
        keysT, qT = sb("keysT", [P, NG, KV]), sb("qT", [P, H, S])
        vals = sb("vals", [KR, KT, D])
        probs, probsT = sb("probs", [S, 4, KV]), sb("probsT", [KR, KT, G, S])
        nmax, sums, rsum = sb("nmax", [S, 4, 2]), sb("sums", [S, 4, 2]), sb("rsum", [S, 4, 2])
        oT = sb("oT", [P, NG, S])
        tmp = sb("tmp", [S, D])

        proj = [bank("proj0"), bank("proj1")]
        tbank = bank("tbank")
        sbank = [bank("s0"), bank("s1")]
        ptbank, obank, wbank = bank("pt"), bank("o"), bank("w")

        x_first, x_rest, w_k, w_q, w_d, w_vo, params, dca_in = (sem(n) for n in (
            "x_first", "x_rest", "w_k", "w_q", "w_d", "w_vo", "params", "dca_in"))
        ctx_in, vd_out, vd_patch, zero_cols = sem("ctx_in"), sem("vd_out"), sem("vd_patch"), sem("zero_cols")
        units, trs, scores, pts, pvs, wos = (sem(n) for n in ("units", "trs", "scores", "pts", "pvs", "wos"))
        unit_v, unit_a = sem("unit_v"), sem("unit_a")
        centred, squared, msqs, normed = sem("centred"), sem("squared"), sem("msqs"), sem("normed")
        means = sem("means")
        keys_ready, q_ready = sem("keys_ready"), sem("q_ready")
        maxes, exps, rsums, pnorms = sem("maxes"), sem("exps"), sem("rsums"), sem("pnorms")
        pt_even, pt_odd, o_done, xn_ready, x_biased, x_done = (sem(n) for n in (
            "pt_even", "pt_odd", "o_done", "xn_ready", "x_biased", "x_done"))
        vlink, plink = sem("vlink"), sem("plink")
        d_tr, d_tre, d_mm, d_raw, d_knt, d_kn, d_kdt = (sem(n) for n in (
            "d_tr", "d_tre", "d_mm", "d_raw", "d_knt", "d_kn", "d_kdt"))
        tnorm = TokenNorm(sb, sem, neg_half)
        outs_rows = [KR, KR, KR, S]
        block = ctx.enter_context(nc.Block())
        ctx_rows = A["ctx_1024"].rearrange("b (t p) c -> b p t c", p=KR)

        @block.sync
        def _(sp):
            for b in range(B):
                sp.dma_start(dcain[ND * (b % 8):ND * (b % 8 + 1), b // 8, :], A["ctx_1024"][b, NM:KV, :]).then_inc(dca_in, 16)
            sp.dma_start(wd[:, :, :], A["L0_xattn_Wkv_dca"].rearrange("(t p) n -> p t n", p=P)).then_inc(w_d, 16)
            sp.dma_start(x_all[:, 0, :], A["x"][0]).then_inc(x_first, 16)
            sp.dma_start(ctxin[:, :, :], ctx_rows[0]).then_inc(ctx_in, 16)
            def split_columns(w, part, done):
                for i, name in enumerate(("Wk", "Wv")):
                    for t in range(CT):
                        src = A[f"L0_xattn_{name}"][t * P:(t + 1) * P, :].rearrange("p (h two d) -> p h two d", two=2, d=HD0)
                        sp.dma_start(w[:, t, i * D // 2:(i + 1) * D // 2].rearrange("p (h d) -> p h d", d=HD0),
                                     src[:, :, part, :]).then_inc(done, 16)

            split_columns(wk, 0, w_k)
            sp.dma_start(wq[:, :, :], A["L0_xattn_Wq"].rearrange("(t p) n -> p t n", p=P)).then_inc(w_q, 16)
            split_columns(wv, 1, w_vo)
            sp.dma_start(wo[:, :, :], A["L0_xattn_Wo"].rearrange("(t p) n -> p t n", p=P)).then_inc(w_vo, 16)
            sp.dma_start(x_all[:, 1:B, :], A["x"][1:B].rearrange("b s d -> s b d")).then_inc(x_rest, 16)
            sp.wait_ge(d_raw, 4)
            sp.dma_start(vd_dram.rearrange("(t p) n -> p t n", p=P), vd[:, :, :]).then_inc(vd_out, 16)
            sp.wait_ge(vd_out, 16)

            def per_batch(b, last):
                if not last:
                    sp.wait_ge(units, UP + UB * b - 5)
                    sp.dma_start(ctxin[:, :, :], ctx_rows[b + 1]).then_inc(ctx_in, 16)
                sp.wait_ge(unit_v, EP + EB * b + 3)
                sp.dma_start(vals[KR - ND:KR, KT - 1, :], vd_dram[bass.ds(b * ND, ND), :]).then_inc(vd_patch, 16)

            with sp.Fori(0, B - 1) as b:
                per_batch(b, False)
            per_batch(B - 1, True)
            sp.wait_ge(vd_patch, 16 * B)

        @block.gpsimd
        def _(pool):
            pool.memset(qw[:, :], 0.0).then_inc(zero_cols, 1)
            pool.memset(qb[:, :], 0.0).then_inc(zero_cols, 1)
            pool.wait_ge(zero_cols, 2)
            for name, t in (("qn_w", qw), ("qn_b", qb)):
                for j in range(G):
                    pool.dma_start(t[HD0 * j:HD0 * j + HD0, j:j + 1], A[f"L0_xattn_{name}"].rearrange("(n o) -> n o", o=1)).then_inc(params, 16)
            for name, t in (("kn_w", kw), ("kn_b", kb), ("kn_dca_w", dw), ("kn_dca_b", db)):
                for j in range(G):
                    pool.dma_start(t[HD0 * j:HD0 * j + HD0, :], A[f"L0_xattn_{name}"].rearrange("(n o) -> n o", o=1)).then_inc(params, 16)
            for name, t in (("bq", bq), ("bkv_dca", bd), ("bo", bo)):
                pool.dma_start(t[:, :], A[f"L0_xattn_{name}"].partition_broadcast(P)).then_inc(params, 16)
            for part, t in enumerate((bk, bv)):
                for i, name in enumerate(("bk", "bv")):
                    src = A[f"L0_xattn_{name}"].rearrange("(h two d) -> h two d", two=2, d=HD0)[:, part, :]
                    pool.dma_start(t[:, i * D // 2:(i + 1) * D // 2].rearrange("p (h d) -> p h d", d=HD0),
                                   src.partition_broadcast(P)).then_inc(params, 16)

            plinks = Links(pool, plink, 0)

            def centre(k, rows, wait_for):
                pool.wait_ge(means, wait_for)
                pool.tensor_tensor(cen[0:rows, k, :].rearrange("p (h d) -> p h d", h=H),
                                   raw[0:rows, k, :].rearrange("p (h d) -> p h d", h=H),
                                   nmean[0:rows, k, :].unsqueeze(2).broadcast_to([rows, H, HD0]), ALU.add).then_inc(centred, 1)

            def scale(k, rows, out, wait_for):
                pool.wait_ge(msqs, wait_for)
                plinks(pool.tensor_tensor(rstd[0:rows, k, :], msq[0:rows, k, :], neg_half[0:rows, :].broadcast_to([rows, H]), ALU.pow))
                pool.tensor_tensor(out.rearrange("p (h d) -> p h d", h=H),
                                   cen[0:rows, k, :].rearrange("p (h d) -> p h d", h=H),
                                   rstd[0:rows, k, :].unsqueeze(2).broadcast_to([rows, H, HD0]), ALU.mult).then_inc(normed, 1)

            for t in range(2):
                centre(t, P, t + 1)
                scale(t, P, raw[:, t, :], t + 1)
            n0 = 2
            tnorm.root_of(pool, 0)
            outs = [(kn[:, 0, :], KR), (kn[:, 1, :], KR), (kn[:, 2, :], KR), (qn[:, :], S)]

            def project(k, base):
                if k < 4:
                    pool.wait_ge(normed, base + max(k - 1, 0))
                    centre(k % 2, outs[k][1], base + k + 1)
                if k >= 1:
                    scale((k - 1) % 2, outs[k - 1][1], outs[k - 1][0], base + k)

            for k in range(5):
                project(k, n0)
            base0, LINKS = plinks.n, 4

            def body(b, last):
                plinks.base, plinks.n = base0 + LINKS * b, 0
                for h in range(H):
                    n = b * H + h
                    if not last and h == 4:
                        tnorm.root_of(pool, b + 1)
                    if not last and 7 <= h <= 11:
                        project(h - 7, n0 + 4 + 4 * b)
                    if h == 12:
                        pool.tensor_tensor(x_all[:, b, :], x_all[:, b, :], bo[0:S, :], ALU.add).then_inc(x_biased, 1)

            pool.wait_ge(params, 16 * 31)
            with pool.Fori(0, B - 1) as b:
                body(b, False)
            body(B - 1, True)

        @block.scalar
        def _(act):
            def square(k, rows, wait_for):
                act.wait_ge(centred, wait_for)
                act.activation(sq[0:rows, k, :], cen[0:rows, k, :], ACT.Square, scale=HD0 ** -0.5).then_inc(squared, 1)

            for c in range(CT):
                act.wait_ge(d_tr, c + 1)
                act.activation(dcaT[:, c, :], proj[c][:, 0:2 * P], ACT.Copy).then_inc(d_tre, 1)
            for t in range(2):
                square(t, P, t + 1)
            act.wait_ge(params, 16 * 31)
            for t in range(2):
                act.wait_ge(d_knt, t + 1)
                act.activation(kdT[:, :, t * P:(t + 1) * P], tbank[:, :].rearrange("p (g s) -> p g s", g=NG), ACT.Identity,
                               bias=db[:, :], scale=dw[:, :]).then_inc(d_kdt, 1)

            def take(k, base_u, base_a):
                act.wait_ge(units, base_u + k + 1)
                if k < 2:
                    ins = act.activation(ctxT[:, k, :], proj[(k + 1) % 2][:, 0:KV], ACT.Copy)
                else:
                    ins = act.activation(xnT[:, :, :], proj[1][:, 0:DT * S].rearrange("p (t s) -> p t s", t=DT), ACT.Copy)
                ins.then_inc(unit_a, 1)

            def chunk(c, b):
                act.wait_ge(trs, b * NG + c + 1)
                act.activation(keysT[:, c, 0:NM], tbank[:, 0:NM], ACT.Identity, bias=kb[:, :], scale=kw[:, :])
                act.activation(keysT[:, c, NM:KV], kdT[:, c, bass.ds(b * ND, ND)], ACT.Copy).then_inc(keys_ready, 1)
                for j in range(G):
                    ins = act.activation(qT[:, G * c + j, :], tbank[:, KV:KV + S], ACT.Identity, bias=qb[:, j:j + 1], scale=qw[:, j:j + 1])
                ins.then_inc(q_ready, 1)

            def exp(h, n):
                act.wait_ge(maxes, n + 1)
                act.activation(probs[:, h % 4, 0:NM], sbank[h % 2][0:S, 0:NM], ACT.Exp, bias=nmax[:, h % 4, 0:1],
                               accum_out=sums[:, h % 4, 0:1])
                act.activation(probs[:, h % 4, NM:KV], sbank[h % 2][0:S, NM:KV], ACT.Exp, bias=nmax[:, h % 4, 1:2],
                               accum_out=sums[:, h % 4, 1:2]).then_inc(exps, 1)

            for k in range(3):
                take(k, 0, 0)
            for k in range(4):
                square(k % 2, outs_rows[k], 2 + k + 1)
            act.wait_ge(zero_cols, 4)
            act.wait_ge(d_kdt, 2)
            for c in range(NG):
                chunk(c, 0)
            exp(0, 0)

            def pt_out(h, n):
                act.wait_ge(pts, n + 1)
                act.activation(probsT[:, :, h % G, :], ptbank[0:KR, 0:KT * S].rearrange("p (t s) -> p t s", t=KT), ACT.Copy).then_inc(pt_even, 1)

            def body(b, last):
                for h in range(H):
                    n = b * H + h
                    if not (last and h == H - 1):
                        if not (h + 1 < 4 and isinstance(b, int) and b == 0):
                            act.wait_ge(pts, n - 2)
                        exp((h + 1) % H, n + 1)
                    if h % 2 == 1:
                        pt_out(h - 1, n - 1)
                    if not last:
                        if 5 <= h <= 6:
                            if h == 5:
                                take(0, UP + UB * b + 3, 0)
                                take(1, UP + UB * b + 3, 0)
                            else:
                                take(2, UP + UB * b + 3, 0)
                        if 7 <= h <= 10:
                            square((h - 7) % 2, outs_rows[h - 7], 2 + 4 + 4 * b + h - 7 + 1)
                        if h >= 12:
                            chunk(h - 12, b + 1)

            body(0, False)
            with act.Fori(1, B - 1) as b:
                body(b, False)
            body(B - 1, True)

        @block.vector
        def _(dve):
            dve.wait_ge(params, 16 * 31)
            dve.tensor_scalar(qw[:, :], qw[:, :], SCALE, None, ALU.mult).then_inc(zero_cols, 1)
            dve.tensor_scalar(qb[:, :], qb[:, :], SCALE, None, ALU.mult).then_inc(zero_cols, 1)
            link = Links(dve, vlink, 0)

            def part1(k, rows, psum, bias, done):
                dve.tensor_tensor(raw[0:rows, k, :], psum[0:rows, :], bias[0:rows, 0:D], ALU.add).then_inc(done, 1)
                return dve

            def means_of(k, rows):
                link(dve.tensor_reduce(nmean[0:rows, k, :], raw[0:rows, k, :].rearrange("p (h d) -> p h d", h=H), AXX, ALU.add))
                dve.tensor_scalar(nmean[0:rows, k, :], nmean[0:rows, k, :], -1.0 / HD0, None, ALU.mult).then_inc(means, 1)

            def part2(k, rows, wait_for):
                dve.wait_ge(squared, wait_for)
                link(dve.tensor_reduce(msq[0:rows, k, :], sq[0:rows, k, :].rearrange("p (h d) -> p h d", h=H), AXX, ALU.add))
                dve.tensor_scalar(msq[0:rows, k, :], msq[0:rows, k, :], QK_EPS, None, ALU.add).then_inc(msqs, 1)

            for t in range(2):
                dve.wait_ge(d_mm, 2 * t + 1)
                part1(t, P, proj[t], bd, d_raw)
                dve.wait_ge(d_mm, 2 * t + 2)
                dve.tensor_tensor(vd[:, t, :], sbank[t][:, :], bd[:, D:2 * D], ALU.add).then_inc(d_raw, 1)
                dve.wait_ge(d_raw, 2 * t + 1)
                means_of(t, P)
            for t in range(2):
                part2(t, P, t + 1)

            def unit(k, base_u, base_v, wait_raw):
                dve.wait_ge(units, base_u + k + 1)
                if wait_raw:
                    dve.wait_ge(normed, wait_raw)
                part1(k % 2, outs_rows[k], proj[k % 2], bk if k < 3 else bq, unit_v)
                dve.wait_ge(unit_v, base_v + k + 1)
                means_of(k % 2, outs_rows[k])

            dve.wait_ge(x_first, 16)
            tnorm.begin(dve, link, x_all[:, 0, :])
            link.wait()
            tnorm.end(dve, link)
            tnorm.apply(dve, 0, x_all[:, 0, :], xn[:, :]).then_inc(xn_ready, 1)
            for k in range(5):
                if k < 4:
                    if k == 0:
                        dve.wait_ge(d_knt, 2)
                    unit(k, 3, 0, None)
                if k >= 1:
                    part2((k - 1) % 2, outs_rows[k - 1], 2 + k)

            def max_(h, n):
                dve.wait_ge(scores, n + 1)
                dve.tensor_reduce(nmax[:, h % 4, 0:1], sbank[h % 2][0:S, 0:NM], AXX, ALU.max, negate=True)
                dve.tensor_reduce(nmax[:, h % 4, 1:2], sbank[h % 2][0:S, NM:KV], AXX, ALU.max, negate=True).then_inc(maxes, 1)

            max_(0, 0)
            base0 = link.n
            LINKS = TokenNorm.LINKS + 4 * 2

            def pt_out(h, n):
                dve.wait_ge(pts, n + 1)
                dve.tensor_copy(probsT[:, :, h % G, :], ptbank[0:KR, 0:KT * S].rearrange("p (t s) -> p t s", t=KT)).then_inc(pt_odd, 1)

            def o_out(g, n):
                dve.wait_ge(pvs, n + 1)
                for j in range(G):
                    ins = dve.tensor_copy(oT[HD0 * j:HD0 * j + HD0, g, :], obank[HD0 * j:HD0 * j + HD0, j * S:(j + 1) * S])
                ins.then_inc(o_done, 1)

            def x_out(b):
                dve.wait_ge(wos, b + 1)
                dve.wait_ge(x_biased, b + 1)
                dve.tensor_tensor(x_all[:, b, :], wbank[0:S, :], x_all[:, b, :], ALU.add).then_inc(x_done, 1)

            def body(b, first, last):
                link.base, link.n = base0 + LINKS * b, 0
                for h in range(H):
                    n = b * H + h
                    if not (last and h == H - 1):
                        max_((h + 1) % H, n + 1)
                    if h == 4 and not last:
                        if first:
                            dve.wait_ge(x_rest, 16)
                        tnorm.begin(dve, link, x_all[:, b + 1, :])
                        link.wait()
                    dve.wait_ge(exps, n + 1)
                    dve.reciprocal(rsum[:, h % 4, :], sums[:, h % 4, :]).then_inc(rsums, 1)
                    dve.wait_ge(rsums, n + 1)
                    dve.tensor_scalar(probs[:, h % 4, 0:NM], probs[:, h % 4, 0:NM], rsum[:, h % 4, 0:1], None, ALU.mult)
                    dve.tensor_scalar(probs[:, h % 4, NM:KV], probs[:, h % 4, NM:KV], rsum[:, h % 4, 1:2], None, ALU.mult).then_inc(pnorms, 1)
                    if not first:
                        if h == 0:
                            pt_out(H - 1, n - 1)
                        if h == 1:
                            o_out(NG - 1, NG * b - 1)
                        if h == 3:
                            x_out(b - 1)
                    if h % 2 == 0 and h >= 2:
                        pt_out(h - 1, n - 1)
                    if h % G == 1 and h >= 5:
                        o_out(h // G - 1, NG * b + h // G - 1)
                    if 2 <= h <= 4:
                        t = h - 2
                        rows = KR if t < KT - 1 else KR - ND
                        dve.wait_ge(units, UP + UB * b + t + 1)
                        dve.tensor_tensor(vals[0:rows, t, :], proj[t % 2][0:rows, :], bv[0:rows, :], ALU.add).then_inc(unit_v, 1)
                    if not last:
                        if h == 4:
                            tnorm.end(dve, link)
                        if h == 5:
                            tnorm.apply(dve, b + 1, x_all[:, b + 1, :], xn[:, :]).then_inc(xn_ready, 1)
                        if 7 <= h <= 10:
                            k = h - 7
                            unit(k, UP + UB * b + 6, EP + EB * b + 3, None)
                        if 8 <= h <= 11:
                            part2((h - 8) % 2, outs_rows[h - 8], 2 + 4 + 4 * b + h - 8 + 1)
                if not last:
                    assert link.n == LINKS, link.n

            body(0, True, False)
            with dve.Fori(1, B - 1) as b:
                body(b, False, False)
            body(B - 1, False, True)
            pt_out(H - 1, B * H - 1)
            o_out(NG - 1, NG * B - 1)
            x_out(B - 1)
            dve.wait_ge(x_done, B)

        @block.tensor
        def _(pe):
            pe.wait_ge(dca_in, 16 * B)
            for c in range(CT):
                for t in range(2):
                    ins = pe.transpose(proj[c][:, t * P:(t + 1) * P], dcain[:, t, c * P:(c + 1) * P], ident[:, :])
                ins.then_inc(d_tr, 1)
            pe.wait_ge(w_d, 16)
            pe.wait_ge(d_tre, CT)
            for t in range(2):
                for half, dst in enumerate((proj[t], sbank[t])):
                    for c in range(CT):
                        ins = pe.matmul(dst[:, :], dcaT[:, c, t * P:(t + 1) * P], wd[:, c, half * D:(half + 1) * D],
                                        start=c == 0, stop=c == CT - 1)
                    ins.then_inc(d_mm, 1)
            for t in range(2):
                pe.wait_ge(normed, t + 1)
                if t:
                    pe.wait_ge(d_kdt, 1)
                for g in range(NG):
                    ins = pe.transpose(tbank[:, g * P:(g + 1) * P], raw[:, t, g * P:(g + 1) * P], ident[:, :])
                ins.then_inc(d_knt, 1)

            def context_half(c, bank_):
                for t in range(KT):
                    ins = pe.transpose(bank_[:, t * KR:(t + 1) * KR], ctxin[:, t, c * P:(c + 1) * P], ident[0:KR, 0:KR])
                ins.then_inc(units, 1)

            def tokens():
                for t in range(DT):
                    ins = pe.transpose(proj[1][:, t * S:(t + 1) * S], xn[:, t * P:(t + 1) * P], ident[0:S, 0:S])
                ins.then_inc(units, 1)

            def rows_unit(t, w, bank_):
                for c in range(CT):
                    ins = pe.matmul(bank_[0:KR, :], ctxT[:, c, t * KR:(t + 1) * KR], w[:, c, :], start=c == 0, stop=c == CT - 1)
                ins.then_inc(units, 1)

            def q_unit():
                for t in range(DT):
                    ins = pe.matmul(proj[1][0:S, :], xnT[:, t, :], wq[:, t, :], start=t == 0, stop=t == DT - 1)
                ins.then_inc(units, 1)

            def chunk(c, b):
                if c == 0:
                    pe.wait_ge(normed, 2 + 4 + 4 * b)
                if isinstance(b, int) and b == 0 and c == 0:
                    pe.wait_ge(d_kdt, 2)
                else:
                    pe.wait_ge(q_ready, b * NG + c)
                for t in range(KT):
                    pe.transpose(tbank[:, t * KR:(t + 1) * KR], kn[:, t, c * P:(c + 1) * P], ident[0:KR, 0:KR])
                pe.transpose(tbank[:, KV:KV + S], qn[:, c * P:(c + 1) * P], ident[0:S, 0:S]).then_inc(trs, 1)

            def score(h, n, b, free):
                if free:
                    pe.wait_ge(exps, n - 1)
                if h % G == 0:
                    pe.wait_ge(keys_ready, b * NG + h // G + 1)
                    pe.wait_ge(q_ready, b * NG + h // G + 1)
                pe.matmul(sbank[h % 2][0:S, 0:KV], qT[:, h, :], keysT[:, h // G, :], start=True, stop=True).then_inc(scores, 1)

            def pt(h, n, b):
                pe.wait_ge(pnorms, n + 1)
                if not (isinstance(n, int) and n == 0):
                    pe.wait_ge(pt_even if h % 2 else pt_odd, b * 8 + (h + 1) // 2)
                for t in range(KT):
                    ins = pe.transpose(ptbank[0:KR, t * S:(t + 1) * S], probs[:, h % 4, t * KR:(t + 1) * KR], ident[0:S, 0:S])
                ins.then_inc(pts, 1)

            def pv(g, b):
                pe.wait_ge(pt_even, b * 8 + 2 * g + 2)
                pe.wait_ge(pt_odd, b * 8 + 2 * g + 2)
                if not (isinstance(b, int) and b == 0 and g == 0):
                    pe.wait_ge(o_done, b * NG + g)
                if g == 0:
                    pe.wait_ge(unit_v, EP + EB * b + 3)
                    pe.wait_ge(vd_patch, b * 16 + 16)
                for t in range(KT):
                    ins = pe.matmul(obank[:, 0:G * S], vals[:, t, g * P:(g + 1) * P], probsT[:, t, :, :].rearrange("p g s -> p (g s)"),
                                    start=t == 0, stop=t == KT - 1)
                ins.then_inc(pvs, 1)

            def out(b):
                pe.wait_ge(o_done, b * NG + NG)
                if not (isinstance(b, int) and b == 0):
                    pe.wait_ge(x_done, b)
                for g in range(NG):
                    ins = pe.matmul(wbank[0:S, :], oT[:, g, :], wo[:, g, :], start=g == 0, stop=g == NG - 1)
                ins.then_inc(wos, 1)

            pe.wait_ge(ctx_in, 16)
            pe.wait_ge(d_raw, 4)
            context_half(0, proj[1])
            context_half(1, proj[0])
            pe.wait_ge(xn_ready, 1)
            pe.wait_ge(unit_a, 1)
            tokens()
            pe.wait_ge(w_k, 16 * 4)
            pe.wait_ge(unit_a, 2)
            rows_unit(0, wk, proj[0])
            pe.wait_ge(unit_a, 3)
            rows_unit(1, wk, proj[1])
            pe.wait_ge(unit_v, 1)
            rows_unit(2, wk, proj[0])
            pe.wait_ge(w_q, 16)
            pe.wait_ge(unit_v, 2)
            q_unit()
            for c in range(NG):
                chunk(c, 0)
            score(0, 0, 0, False)
            pe.wait_ge(w_vo, 16 * 5)

            def body(b, first, last):
                for h in range(H):
                    n = b * H + h
                    if h < H - 1:
                        score(h + 1, n + 1, b, not (first and h == 0))
                    elif not last:
                        score(0, n + 1, b + 1, True)
                    if not first:
                        if h == 1:
                            pv(NG - 1, b - 1)
                        if h == 2:
                            out(b - 1)
                    if h >= 5 and h % G == 1:
                        pv(h // G - 1, b)
                    if 2 <= h <= 4:
                        pe.wait_ge(unit_v, EP + EB * b + h - 3)
                        rows_unit(h - 2, wv, proj[h % 2])
                    if not last:
                        if h == 5:
                            pe.wait_ge(ctx_in, b * 16 + 32)
                            pe.wait_ge(unit_v, EP + EB * b + 2)
                            context_half(0, proj[1])
                            pe.wait_ge(unit_v, EP + EB * b + 3)
                            context_half(1, proj[0])
                        if h == 6:
                            pe.wait_ge(xn_ready, b + 2)
                            pe.wait_ge(unit_a, AP_ + AB * b + 1)
                            tokens()
                        if h == 7:
                            pe.wait_ge(unit_a, AP_ + AB * b + 2)
                            rows_unit(0, wk, proj[0])
                        if h == 8:
                            pe.wait_ge(unit_a, AP_ + AB * b + 3)
                            rows_unit(1, wk, proj[1])
                        if h == 9:
                            pe.wait_ge(unit_v, EP + EB * b + 4)
                            rows_unit(2, wk, proj[0])
                        if h == 10:
                            pe.wait_ge(unit_v, EP + EB * b + 5)
                            q_unit()
                        if h >= 12:
                            chunk(h - 12, b + 1)
                    if h >= 1:
                        pt(h - 1, n - 1, b)
                    elif not first:
                        pt(H - 1, n - 1, b - 1)

            body(0, True, False)
            with pe.Fori(1, B - 1) as b:
                body(b, False, False)
            body(B - 1, False, True)
            pt(H - 1, B * H - 1, B - 1)
            pv(NG - 1, B - 1)
            out(B - 1)


def one_hot_first_max(dve, link, values, best, rank, keys, out):
    shape = list(values.shape)
    link(dve.tensor_reduce(best, values, AXX, ALU.max))
    link(dve.tensor_tensor(out, values, best.unsqueeze(2).broadcast_to(shape), ALU.is_equal))
    link(dve.tensor_tensor(out, out, rank.unsqueeze(1).broadcast_to(shape), ALU.mult))
    link(dve.tensor_reduce(keys, out, AXX, ALU.max))
    link(dve.tensor_tensor(out, out, keys.unsqueeze(2).broadcast_to(shape), ALU.is_equal))


def phase_select(nc, A, ident, neg_half, x_all):
    N, R = 8, 8
    NR = N * R
    W1 = 2 * NR + N
    W2 = NR + N
    with ExitStack() as ctx:
        sb, bank, sem = tools(nc, ctx, "f0")
        w1, degen, w2 = sb("w1", [P, DT, W1]), sb("degen", [P, DT, NR]), sb("w2", [W2, D])
        md, db, dbT = sb("md", [N, D]), sb("db", [N, D]), sb("dbT", [P, DT, N])
        mdsq, md2, md2d = sb("mdsq", [N, D]), sb("md2", [N, 1]), sb("md2d", [N, N])
        own, ones = sb("own", [N, NR]), sb("ones", [N, P])
        own_sel, own_upd = sb("own_sel", [N, NR]), sb("own_upd", [N, NR])
        c_sel, c_upd, c_md2 = sb("c_sel", [P, NR]), sb("c_upd", [P, NR]), sb("c_md2", [P, N])
        slope, centre, rank = sb("slope", [P, N]), sb("centre", [P, N]), sb("rank", [P, N])
        xn, xn_all, xnT, y = sb("xn", [S, 2, D]), sb("xn_all", [S, B, D]), sb("xnT", [P, 2, DT * S]), sb("y", [S, B, W1])
        xx, sqx = sb("xx", [S, B]), sb("sqx", [S, D])
        z, score, nrm, gate = sb("z", [S, B, NR]), sb("score", [S, B, N]), sb("nrm", [S, B, N]), sb("gate", [S, B, N])
        gmax, keys, hot, rest = sb("gmax", [S, B]), sb("keys", [S, B]), sb("hot", [S, B, N]), sb("rest", [S, B])
        mix, mix2, mixT, upd = sb("mix", [S, B, W2]), sb("mix2", [S, 2, W2]), sb("mixT", [W2, 2, S]), sb("upd", [S, 2, D])
        tb, yb = [bank("t0"), bank("t1")], [bank("y0"), bank("y1")]
        cb, mb, ub = bank("c"), bank("m"), [bank("u0"), bank("u1")]
        loads, setup_p, setup_v, setup_t, pl, vl = (sem(n) for n in ("loads", "setup_p", "setup_v", "setup_t", "pl", "vl"))
        xn_ready, xnT_done, xnT_out, ys, y_out, sq_done = (sem(n) for n in (
            "xn_ready", "xnT_done", "xnT_out", "ys", "y_out", "sq_done"))
        arg_ready, exp_ready, mix_ready, mixT_done, mixT_out, upds, upd_out, x_done = (sem(n) for n in (
            "arg_ready", "exp_ready", "mix_ready", "mixT_done", "mixT_out", "upds", "upd_out", "x_done"))
        block = ctx.enter_context(nc.Block())
        N_LOADS = 3 * N + 5
        xn_kept, mix_at = sem("xn_kept"), sem("mix_at")
        tnorm = TokenNorm(sb, sem, neg_half)

        @block.sync
        def _(sp):
            for i, name in enumerate(("select_weight", "lora_update")):
                for n in range(N):
                    sp.dma_start(w1[:, :, i * NR + n * R:i * NR + n * R + R],
                                 A[f"L0_ffn_{name}"][n].rearrange("(t p) r -> p t r", p=P)).then_inc(loads, 16)
            for n in range(N):
                sp.dma_start(degen[:, :, n * R:n * R + R], A["L0_ffn_lora_degen"][n].rearrange("(t p) r -> p t r", p=P)).then_inc(loads, 16)
            sp.dma_start(md[:, :], A["L0_ffn_select_mean_diff"]).then_inc(loads, 16)
            sp.dma_start(db[:, :], A["L0_ffn_debias_w"]).then_inc(loads, 16)
            sp.dma_start(w2[NR:W2, :], A["L0_ffn_bias_w"]).then_inc(loads, 16)
            sp.dma_start(slope[:, :], A["L0_ffn_imp_slope"].partition_broadcast(P)).then_inc(loads, 16)
            sp.dma_start(centre[:, :], A["L0_ffn_imp_center"].partition_broadcast(P)).then_inc(loads, 16)

        @block.gpsimd
        def _(pool):
            links = Links(pool, pl, 0)
            links(pool.memset(own[:, :], 1.0))
            links(pool.affine_select(out=own[:, :], in_=own[:, :], compare_op=ALU.is_ge, fill=0.0, base=0,
                                     pattern=[[1, NR]], channel_multiplier=-R))
            links(pool.affine_select(out=own[:, :], in_=own[:, :], compare_op=ALU.is_ge, fill=0.0, base=R - 1,
                                     pattern=[[-1, NR]], channel_multiplier=R))
            for n in range(N):
                pool.memset(rank[:, n:n + 1], float(N - n)).then_inc(setup_p, 1)
            pool.memset(ones[:, :], 1.0).then_inc(setup_p, 1)
            pool.wait_ge(setup_p, N + 1)

            with pool.Fori(0, B) as b:
                tnorm.root_of(pool, b)
            with pool.Fori(0, B // 2) as i:
                for u in range(2):
                    b = i * 2 + u
                    pool.wait_ge(upd_out, b + 1)
                    pool.tensor_tensor(x_all[:, b, :], x_all[:, b, :], upd[:, u, :], ALU.add).then_inc(x_done, 1)
            pool.wait_ge(x_done, B)

        @block.scalar
        def _(act):
            act.wait_ge(setup_t, 1)
            act.activation(w2[0:NR, :], cb[0:NR, :], ACT.Copy).then_inc(setup_v, 1)

            with act.Fori(0, B // 2) as i:
                for u in range(2):
                    b = i * 2 + u
                    act.wait_ge(xnT_done, b + 1)
                    act.activation(xnT[:, u, :], tb[u][:, 0:DT * S], ACT.Copy).then_inc(xnT_out, 1)
                    act.wait_ge(xn_ready, b + 1)
                    act.activation(sqx[:, :], xn[:, u, :], ACT.Square, accum_out=xx[:, bass.ds(b, 1)]).then_inc(sq_done, 1)
                    act.wait_ge(sq_done, b + 1)
            act.wait_ge(arg_ready, 1)
            act.activation(gate[:, :, :], gate[:, :, :], ACT.Exp, scale=-1.0).then_inc(exp_ready, 1)
            with act.Fori(0, B // 2) as i:
                for u in range(2):
                    b = i * 2 + u
                    act.wait_ge(mixT_done, b + 1)
                    act.activation(mixT[:, u, :], mb[0:W2, u * S:u * S + S], ACT.Copy).then_inc(mixT_out, 1)

        @block.tensor
        def _(pe):
            pe.wait_ge(loads, 16 * N_LOADS)
            for t in range(DT):
                ins = pe.transpose(cb[0:NR, t * P:(t + 1) * P], degen[:, t, :], ident[:, :])
            ins.then_inc(setup_t, 1)
            for t in range(DT):
                pe.transpose(mb[:, t * N:(t + 1) * N], md[:, t * P:(t + 1) * P], ident[0:N, 0:N])
            for t in range(DT):
                ins = pe.transpose(mb[:, (DT + t) * N:(DT + t + 1) * N], db[:, t * P:(t + 1) * P], ident[0:N, 0:N])
            ins.then_inc(setup_t, 1)
            pe.wait_ge(setup_v, 4)
            for t in range(DT):
                ins = pe.matmul(ub[0][0:N, 0:NR], w1[:, t, 2 * NR:W1], w1[:, t, 0:NR], start=t == 0, stop=t == DT - 1)
            ins.then_inc(setup_t, 1)
            for t in range(DT):
                ins = pe.matmul(ub[1][0:N, 0:NR], dbT[:, t, :], w1[:, t, NR:2 * NR], start=t == 0, stop=t == DT - 1)
            ins.then_inc(setup_t, 1)
            pe.wait_ge(setup_v, 7)
            pe.wait_ge(setup_p, N + 1)
            pe.matmul(cb[:, 0:NR], ones[:, :], own_sel[:, :], start=True, stop=True)
            pe.matmul(cb[:, NR:2 * NR], ones[:, :], own_upd[:, :], start=True, stop=True)
            pe.matmul(cb[:, 2 * NR:W1], ones[:, :], md2d[:, :], start=True, stop=True).then_inc(setup_t, 1)

            def transposes(b, u):
                pe.wait_ge(xn_ready, b + 1)
                for t in range(DT):
                    ins = pe.transpose(tb[u][:, t * S:(t + 1) * S], xn[:, u, t * P:(t + 1) * P], ident[0:S, 0:S])
                ins.then_inc(xnT_done, 1)

            with pe.Fori(0, B // 2) as i:
                for u in range(2):
                    b = i * 2 + u
                    transposes(b, u)
                    pe.wait_ge(xnT_out, b + 1)
                    for t in range(DT):
                        ins = pe.matmul(yb[u][0:S, 0:W1], xnT[:, u, t * S:(t + 1) * S], w1[:, t, :], start=t == 0, stop=t == DT - 1)
                    ins.then_inc(ys, 1)
            with pe.Fori(0, B // 2) as i:
                for u in range(2):
                    b = i * 2 + u
                    pe.wait_ge(mix_at, b + 1)
                    pe.transpose(mb[0:W2, u * S:u * S + S], mix2[:, u, :], ident[0:S, 0:S]).then_inc(mixT_done, 1)
                    pe.wait_ge(mixT_out, b + 1)
                    pe.matmul(ub[u][0:S, :], mixT[:, u, :], w2[:, :], start=True, stop=True).then_inc(upds, 1)

        @block.vector
        def _(dve):
            link = Links(dve, vl, 0)
            dve.wait_ge(setup_t, 2)
            dve.tensor_copy(w1[:, :, 2 * NR:W1], mb[:, 0:DT * N].rearrange("p (t n) -> p t n", t=DT)).then_inc(setup_v, 1)
            dve.tensor_copy(dbT[:, :, :], mb[:, DT * N:2 * DT * N].rearrange("p (t n) -> p t n", t=DT)).then_inc(setup_v, 1)
            link(dve.tensor_tensor(mdsq[:, :], md[:, :], md[:, :], ALU.mult))
            dve.tensor_reduce(md2[:, :], mdsq[:, :], AXX, ALU.add).then_inc(setup_v, 1)
            dve.wait_ge(setup_t, 4)
            dve.wait_ge(pl, 3)
            dve.wait_ge(setup_v, 4)
            dve.tensor_tensor(own_sel[:, :], ub[0][0:N, 0:NR], own[:, :], ALU.mult).then_inc(setup_v, 1)
            dve.tensor_tensor(own_upd[:, :], ub[1][0:N, 0:NR], own[:, :], ALU.mult).then_inc(setup_v, 1)
            dve.tensor_scalar(md2d[:, :], ident[0:N, 0:N], md2[:, :], None, ALU.mult).then_inc(setup_v, 1)
            dve.wait_ge(setup_t, 5)
            dve.wait_ge(setup_p, N + 1)
            link(dve.tensor_copy(c_sel[:, :], cb[:, 0:NR]))
            link(dve.tensor_copy(c_upd[:, :], cb[:, NR:2 * NR]))
            link(dve.tensor_copy(c_md2[:, :], cb[:, 2 * NR:W1]))
            base = link.n
            LINKS = TokenNorm.LINKS

            def step(b, u, first, last):
                link.base, link.n = base + b * LINKS, 0
                if not last:
                    tnorm.begin(dve, link, x_all[:, b, :])
                    link.wait()
                if not first:
                    dve.wait_ge(ys, b)
                    dve.tensor_scalar(y[:, b - 1, :], yb[1 - u][0:S, 0:W1], 1.0, None, ALU.mult).then_inc(y_out, 1)
                if not last:
                    tnorm.end(dve, link)
                    tnorm.apply(dve, b, x_all[:, b, :], xn_all[:, b, :]).then_inc(xn_kept, 1)
                    dve.wait_ge(xn_kept, b + 1)
                    if not (isinstance(b, int) and b < 2):
                        dve.wait_ge(sq_done, b - 1)
                    dve.tensor_scalar(xn[:, u, :], xn_all[:, b, :], 1.0, None, ALU.mult).then_inc(xn_ready, 1)

            step(0, 0, True, False)
            step(1, 1, False, False)
            with dve.Fori(1, B // 2) as i:
                for u in range(2):
                    step(i * 2 + u, u, False, False)
            step(B, 0, False, True)
            link.base, link.n = base + B * LINKS, 0
            dve.wait_ge(y_out, B)
            dve.wait_ge(sq_done, B)
            per_sel = [S, B, N]
            link(dve.tensor_tensor(z[:, :, :], y[:, :, 0:NR], c_sel[0:S, :].unsqueeze(1).broadcast_to([S, B, NR]), ALU.subtract))
            link(dve.tensor_tensor(z[:, :, :], z[:, :, :], z[:, :, :], ALU.mult))
            link(dve.tensor_reduce(score[:, :, :].rearrange("p b n -> p (b n)"), z[:, :, :].rearrange("p b (n r) -> p (b n) r", r=R), AXX, ALU.add))
            link(dve.tensor_scalar(nrm[:, :, :], y[:, :, 2 * NR:W1], -2.0, None, ALU.mult))
            link(dve.tensor_tensor(nrm[:, :, :], nrm[:, :, :], c_md2[0:S, :].unsqueeze(1).broadcast_to(per_sel), ALU.add))
            link(dve.tensor_tensor(nrm[:, :, :], nrm[:, :, :], xx[:, :].unsqueeze(2).broadcast_to(per_sel), ALU.add))
            link(dve.reciprocal(nrm[:, :, :], nrm[:, :, :]))
            link(dve.tensor_tensor(score[:, :, :], score[:, :, :], nrm[:, :, :], ALU.mult))
            link(dve.tensor_tensor(gate[:, :, :], score[:, :, :], centre[0:S, :].unsqueeze(1).broadcast_to(per_sel), ALU.subtract))
            link(dve.tensor_tensor(gate[:, :, :], gate[:, :, :], slope[0:S, :].unsqueeze(1).broadcast_to(per_sel), ALU.mult))
            dve.tensor_scalar(gate[:, :, :], gate[:, :, :], -87.0, None, ALU.max).then_inc(arg_ready, 1)
            dve.wait_ge(exp_ready, 1)
            link(dve.tensor_scalar(gate[:, :, :], gate[:, :, :], 1.0, None, ALU.add))
            link(dve.reciprocal(gate[:, :, :], gate[:, :, :]))
            one_hot_first_max(dve, link, gate[:, :, :], gmax[:, :], rank[0:S, :], keys[:, :], hot[:, :, :])
            link(dve.tensor_tensor(mix[:, :, NR:W2], hot[:, :, :], gmax[:, :].unsqueeze(2).broadcast_to(per_sel), ALU.mult))
            link(dve.tensor_tensor(z[:, :, :], y[:, :, NR:2 * NR], c_upd[0:S, :].unsqueeze(1).broadcast_to([S, B, NR]), ALU.subtract))
            link(dve.tensor_scalar(rest[:, :], gmax[:, :], -1.0, 1.0, ALU.mult, ALU.add))
            for n in range(N):
                ins = dve.tensor_tensor(mix[:, :, n * R:n * R + R], z[:, :, n * R:n * R + R],
                                        mix[:, :, NR + n:NR + n + 1].broadcast_to([S, B, R]), ALU.mult)
                link(ins)

            def hand_over(b, u):
                dve.tensor_scalar(mix2[:, u, :], mix[:, b, :], 1.0, None, ALU.mult).then_inc(mix_at, 1)

            hand_over(0, 0)
            hand_over(1, 1)

            def update(b, u):
                dve.wait_ge(upds, b + 1)
                if not (isinstance(b, int) and b < 2):
                    dve.wait_ge(x_done, b - 1)
                dve.scalar_tensor_tensor(out=upd[:, u, :], in0=xn_all[:, b, :], scalar=rest[:, bass.ds(b, 1)], in1=ub[u][0:S, :],
                                         op0=ALU.mult, op1=ALU.add).then_inc(upd_out, 1)

            for b in (0, 1):
                update(b, b)
                hand_over(b + 2, b)
            with dve.Fori(1, B // 2 - 1) as i:
                for u in range(2):
                    update(i * 2 + u, u)
                    hand_over(i * 2 + u + 2, u)
            for b in (B - 2, B - 1):
                update(b, b % 2)


def phase_attention1(nc, A, ident, neg_half, x_all):
    SCALE = float(HD1) ** -0.5
    INNER = H * HD1
    W = G * HD1
    TP, TB = 17, 19
    with ExitStack() as ctx:
        sb, bank, sem = tools(nc, ctx, "a1")
        wq, wk, wv = sb("wq", [P, DT, INNER]), sb("wk", [P, CT, INNER]), sb("wv", [P, CT, INNER])
        wo = sb("wo", [P, H, D])
        gq, gk, g_col = sb("gq", [P, 1]), sb("gk", [P, 1]), sb("g_col", [P, 1])
        ctxin, ctx_tok, ctxT = sb("ctxin", [KR, KT, C]), sb("ctx_tok", [KR, KT, C]), sb("ctxT", [P, CT, KV])
        xn, xnT = sb("xn", [S, D]), sb("xnT", [P, DT, S])
        sq, msq, root = sb("sq", [P, 2, W]), sb("msq", [P, 2, G]), sb("root", [P, 2, G])
        kn = sb("kn", [P, 2, W])
        keysT, qT = sb("keysT", [P, H, KV]), sb("qT", [P, H, S])
        probs, probsT = sb("probs", [S, 4, KV]), sb("probsT", [KR, KT, G, S])
        nmax, sums, rsum = sb("nmax", [S, 4]), sb("sums", [S, 4]), sb("rsum", [S, 4])
        mixT, oT = sb("mixT", [P, CT, G * S]), sb("oT", [P, H, S])

        proj, tbank = [bank("proj0"), bank("proj1")], bank("t")
        sbank, ptbank = [bank("s0"), bank("s1")], bank("pt")
        mbank = [bank("m0"), bank("m1")]

        w_k, w_q, w_v, w_o, params, ctx_in, ctx_tok_in = (sem(n) for n in (
            "w_k", "w_q", "w_v", "w_o", "params", "ctx_in", "ctx_tok_in"))
        units, trs, scores, pts, mixes, heads_out, wos = (sem(n) for n in (
            "units", "trs", "scores", "pts", "mixes", "heads_out", "wos"))
        squared, msqs, roots, scaled, t_out = (sem(n) for n in ("squared", "msqs", "roots", "scaled", "t_out"))
        maxes, exps, rsums, pnorms, pt_even, pt_odd = (sem(n) for n in (
            "maxes", "exps", "rsums", "pnorms", "pt_even", "pt_odd"))
        mix0_out, mix1_out, o_out, x_done, xn_ready = (sem(n) for n in (
            "mix0_out", "mix1_out", "o_out", "x_done", "xn_ready"))
        gcol_ready, vl = sem("gcol_ready"), sem("vl")
        tnorm = TokenNorm(sb, sem, neg_half)
        block = ctx.enter_context(nc.Block())
        ctx_rows = A["ctx_1024"].rearrange("b (t p) c -> b p t c", p=KR)

        def unit_rows(n):
            return S if n % G == 3 else KR

        @block.sync
        def _(sp):
            sp.dma_start(ctxin[:, :, :], ctx_rows[0]).then_inc(ctx_in, 16)
            for g in range(NG):
                cols = slice(g * W, (g + 1) * W)
                sp.dma_start(wk[:, :, cols], A["L1_xattn_Wk"].rearrange("(t p) n -> p t n", p=P)[:, :, cols]).then_inc(w_k, 16)
                sp.dma_start(wq[:, :, cols], A["L1_xattn_Wq"].rearrange("(t p) n -> p t n", p=P)[:, :, cols]).then_inc(w_q, 16)
            for name, t in (("gq", gq), ("gk", gk)):
                sp.dma_start(t[:, :], A[f"L1_xattn_{name}"].rearrange("(n o) -> n o", o=1)).then_inc(params, 16)
            sp.dma_start(wv[:, :, :], A["L1_xattn_Wv"].rearrange("(t p) n -> p t n", p=P)).then_inc(w_v, 16)
            sp.dma_start(wo[:, :, :], A["L1_xattn_Wo"].rearrange("(t p) n -> p t n", p=P)).then_inc(w_o, 16)

            def body(b, first, last):
                if not last:
                    sp.wait_ge(trs, 2 if first else TP + TB * (b - 1) + 3)
                    sp.dma_start(ctxin[:, :, :], ctx_rows[b + 1]).then_inc(ctx_in, 16)
                if not first:
                    sp.wait_ge(mixes, b * NG)
                sp.dma_start(ctx_tok[:, :, :], ctx_rows[b]).then_inc(ctx_tok_in, 16)

            body(0, True, False)
            with sp.Fori(1, B - 1) as b:
                body(b, False, False)
            body(B - 1, False, True)

        @block.gpsimd
        def _(pool):
            def root_of(n, m):
                rows = unit_rows(n)
                pool.wait_ge(msqs, m + 1)
                pool.tensor_tensor(root[0:rows, n % 2, :], msq[0:rows, n % 2, :], neg_half[0:rows, :].broadcast_to([rows, G]), ALU.pow).then_inc(roots, 1)

            tnorm.root_of(pool, 0)
            for n in range(H):
                root_of(n, n)
            with pool.Fori(0, B - 1) as b:
                tnorm.root_of(pool, b + 1)
                for n in range(H):
                    root_of(n, b * H + H + n)

        @block.scalar
        def _(act):
            def square(n, m):
                rows = unit_rows(n)
                act.wait_ge(units, m + 1)
                act.activation(sq[0:rows, n % 2, :], proj[n % 2][0:rows, :], ACT.Square, scale=SCALE).then_inc(squared, 1)

            def take_context(c, use):
                act.wait_ge(trs, use + 1)
                act.activation(ctxT[:, c, :], tbank[:, 0:KV], ACT.Copy).then_inc(t_out, 1)

            def take_tokens(use):
                act.wait_ge(trs, use + 1)
                act.activation(xnT[:, :, :], tbank[:, 0:DT * S].rearrange("p (t s) -> p t s", t=DT), ACT.Copy).then_inc(t_out, 1)

            def take_unit(n, use):
                g, t = n // G, n % G
                act.wait_ge(trs, use + 1)
                if t == 3:
                    ins = act.activation(qT[:, g * G:g * G + G, :], tbank[:, 0:G * S].rearrange("p (h s) -> p h s", h=G), ACT.Copy, scale=g_col[:, :])
                else:
                    ins = act.activation(keysT[:, g * G:g * G + G, t * KR:(t + 1) * KR],
                                         tbank[:, 0:G * KR].rearrange("p (h s) -> p h s", h=G), ACT.Copy)
                ins.then_inc(t_out, 1)

            def exp(h, n):
                act.wait_ge(maxes, n + 1)
                act.activation(probs[:, h % 4, :], sbank[h % 2][0:S, 0:KV], ACT.Exp, bias=nmax[:, h % 4:h % 4 + 1],
                               accum_out=sums[:, h % 4:h % 4 + 1]).then_inc(exps, 1)

            def pt_out(h, n):
                act.wait_ge(pts, n + 1)
                act.activation(probsT[:, :, h % G, :], ptbank[0:KR, 0:KT * S].rearrange("p (t s) -> p t s", t=KT), ACT.Copy).then_inc(pt_even, 1)

            def mix1(m):
                act.wait_ge(mixes, m + 1)
                act.activation(mixT[:, 1, :], mbank[1][:, 0:G * S], ACT.Copy).then_inc(mix1_out, 1)

            def o_of(g, m):
                act.wait_ge(heads_out, m + 1)
                act.activation(oT[:, g * G:g * G + G, :], mbank[0][:, 0:G * S].rearrange("p (h s) -> p h s", h=G), ACT.Copy).then_inc(o_out, 1)

            take_context(0, 0)
            take_context(1, 1)
            take_tokens(2)
            act.wait_ge(gcol_ready, 1)
            for n in range(H):
                square(n, n)
                if n >= 2:
                    take_unit(n - 2, n + 1)
            exp(0, 0)

            def body(b, first, last):
                use = TP + TB * b
                for h in range(H):
                    n = b * H + h
                    if h < H - 1 or not last:
                        if not (first and h < 3):
                            act.wait_ge(pts, n - 2)
                        exp((h + 1) % H, n + 1)
                    if h % 2 == 1:
                        pt_out(h - 1, n - 1)
                    if h == 0:
                        take_unit(H - 2, use)
                        if not last:
                            take_context(0, use + 1)
                            take_context(1, use + 2)
                    if h == 1:
                        take_unit(H - 1, use + (1 if last else 3))
                    if not last:
                        if h >= 2:
                            take_unit(h - 2, use + (4 if h == 2 else h + 3))
                        if h == 2:
                            take_tokens(use + 5)
                    if h == 1 and not first:
                        mix1(b * NG - 1)
                    if h == 2 and not first:
                        o_of(NG - 1, b * NG - 1)
                    if h >= 5 and h % G == 1:
                        mix1(b * NG + h // G - 1)
                    if h >= 6 and h % G == 2:
                        o_of(h // G - 1, b * NG + h // G - 1)
                    if not last:
                        square(h, n + H)

            body(0, True, False)
            with act.Fori(1, B - 1) as b:
                body(b, False, False)
            body(B - 1, False, True)
            mix1(B * NG - 1)
            o_of(NG - 1, B * NG - 1)

        @block.vector
        def _(dve):
            link = Links(dve, vl, 0)
            dve.wait_ge(params, 32)
            link(dve.tensor_tensor(g_col[:, :], gq[:, :], gk[:, :], ALU.mult))
            dve.tensor_scalar(g_col[:, :], g_col[:, :], SCALE, None, ALU.mult).then_inc(gcol_ready, 1)

            def reduce(n, m):
                rows = unit_rows(n)
                dve.wait_ge(squared, m + 1)
                link(dve.tensor_reduce(msq[0:rows, n % 2, :], sq[0:rows, n % 2, :].rearrange("p (h d) -> p h d", h=G), AXX, ALU.add))
                dve.tensor_scalar(msq[0:rows, n % 2, :], msq[0:rows, n % 2, :], RMS_EPS, None, ALU.add).then_inc(msqs, 1)

            def scale(n, m, wait):
                rows = unit_rows(n)
                dve.wait_ge(roots, m + 1)
                if wait is not None:
                    dve.wait_ge(trs, wait)
                dve.tensor_tensor(kn[0:rows, n % 2, :].rearrange("p (h d) -> p h d", h=G),
                                  proj[n % 2][0:rows, :].rearrange("p (h d) -> p h d", h=G),
                                  root[0:rows, n % 2, :].unsqueeze(2).broadcast_to([rows, G, HD1]), ALU.mult).then_inc(scaled, 1)

            def max_(h, n):
                dve.wait_ge(scores, n + 1)
                dve.tensor_reduce(nmax[:, h % 4:h % 4 + 1], sbank[h % 2][0:S, 0:KV], AXX, ALU.max, negate=True).then_inc(maxes, 1)

            def pt_out(h, n):
                dve.wait_ge(pts, n + 1)
                dve.tensor_copy(probsT[:, :, h % G, :], ptbank[0:KR, 0:KT * S].rearrange("p (t s) -> p t s", t=KT)).then_inc(pt_odd, 1)

            def mix0(m):
                dve.wait_ge(mixes, m + 1)
                dve.tensor_copy(mixT[:, 0, :], mbank[0][:, 0:G * S]).then_inc(mix0_out, 1)

            def x_out(b):
                dve.wait_ge(wos, b + 1)
                dve.tensor_tensor(x_all[:, b, :], mbank[1][0:S, :], x_all[:, b, :], ALU.add).then_inc(x_done, 1)

            tnorm.begin(dve, link, x_all[:, 0, :])
            link.wait()
            tnorm.end(dve, link)
            tnorm.apply(dve, 0, x_all[:, 0, :], xn[:, :]).then_inc(xn_ready, 1)
            for n in range(H):
                reduce(n, n)
                if n >= 1:
                    scale(n - 1, n - 1, n + 1 if n >= 3 else None)
            max_(0, 0)
            base, LINKS = link.n, TokenNorm.LINKS + H

            def body(b, first, last):
                link.base, link.n = base + b * LINKS, 0
                use = TP + TB * b
                for h in range(H):
                    n = b * H + h
                    if h < H - 1 or not last:
                        max_((h + 1) % H, n + 1)
                    if h == 0 and not last:
                        tnorm.begin(dve, link, x_all[:, b + 1, :])
                        link.wait()
                    dve.wait_ge(exps, n + 1)
                    dve.reciprocal(rsum[:, h % 4:h % 4 + 1], sums[:, h % 4:h % 4 + 1]).then_inc(rsums, 1)
                    dve.wait_ge(rsums, n + 1)
                    dve.tensor_scalar(probs[:, h % 4, :], probs[:, h % 4, :], rsum[:, h % 4:h % 4 + 1], None, ALU.mult).then_inc(pnorms, 1)
                    if h == 0:
                        scale(H - 1, b * H + H - 1, use)
                        if not last:
                            tnorm.end(dve, link)
                    if h == 1 and not last:
                        tnorm.apply(dve, b + 1, x_all[:, b + 1, :], xn[:, :]).then_inc(xn_ready, 1)
                    if not first:
                        if h == 0:
                            pt_out(H - 1, n - 1)
                        if h == 1:
                            mix0(b * NG - 1)
                        if h == 4:
                            x_out(b - 1)
                    if h % 2 == 0 and h >= 2:
                        pt_out(h - 1, n - 1)
                    if h >= 5 and h % G == 1:
                        mix0(b * NG + h // G - 1)
                    if not last:
                        if h >= 1:
                            scale(h - 1, n + H - 1, use + (1 if h == 1 else 4 if h == 2 else 5 if h == 3 else h + 3))
                        reduce(h, n + H)

            body(0, True, False)
            with dve.Fori(1, B - 1) as b:
                body(b, False, False)
            body(B - 1, False, True)
            pt_out(H - 1, B * H - 1)
            mix0(B * NG - 1)
            x_out(B - 1)
            dve.wait_ge(x_done, B)

        @block.tensor
        def _(pe):
            def bank_free(use):
                if not (isinstance(use, int) and use == 0):
                    pe.wait_ge(t_out, use)

            def context_half(c, use):
                bank_free(use)
                for t in range(KT):
                    ins = pe.transpose(tbank[:, t * KR:(t + 1) * KR], ctxin[:, t, c * P:(c + 1) * P], ident[0:KR, 0:KR])
                ins.then_inc(trs, 1)

            def tokens(use):
                bank_free(use)
                for t in range(DT):
                    ins = pe.transpose(tbank[:, t * S:(t + 1) * S], xn[:, t * P:(t + 1) * P], ident[0:S, 0:S])
                ins.then_inc(trs, 1)

            def unit(n, m):
                g, t = n // G, n % G
                cols = slice(g * W, (g + 1) * W)
                if not (isinstance(m, int) and m < 2):
                    pe.wait_ge(scaled, m - 1)
                rows = unit_rows(n)
                tiles = [(xnT[:, k, :], wq[:, k, cols]) for k in range(DT)] if t == 3 else \
                        [(ctxT[:, k, t * KR:(t + 1) * KR], wk[:, k, cols]) for k in range(CT)]
                for k, (rows_, w) in enumerate(tiles):
                    ins = pe.matmul(proj[n % 2][0:rows, :], rows_, w, start=k == 0, stop=k == len(tiles) - 1)
                ins.then_inc(units, 1)

            def unit_T(n, m, use):
                rows = unit_rows(n)
                pe.wait_ge(scaled, m + 1)
                bank_free(use)
                for j in range(G):
                    ins = pe.transpose(tbank[:, j * rows:(j + 1) * rows], kn[0:rows, n % 2, j * P:(j + 1) * P], ident[0:rows, 0:rows])
                ins.then_inc(trs, 1)

            def score(h, n, b):
                if not (isinstance(n, int) and n < 2):
                    pe.wait_ge(exps, n - 1)
                if h % G == 0:
                    c = h // G
                    pe.wait_ge(t_out, TP - TB + TB * b + G * c + 9 if c < 3 else TP + TB * b + (2 if isinstance(b, int) and b == B - 1 else 4))
                pe.matmul(sbank[h % 2][0:S, 0:KV], qT[:, h, :], keysT[:, h, :], start=True, stop=True).then_inc(scores, 1)

            def pt(h, n, b):
                pe.wait_ge(pnorms, n + 1)
                if not (isinstance(n, int) and n == 0):
                    pe.wait_ge(pt_even if h % 2 else pt_odd, b * 8 + (h + 1) // 2)
                for t in range(KT):
                    ins = pe.transpose(ptbank[0:KR, t * S:(t + 1) * S], probs[:, h % 4, t * KR:(t + 1) * KR], ident[0:S, 0:S])
                ins.then_inc(pts, 1)

            def mix(g, b):
                m = b * NG + g
                pe.wait_ge(pt_even, b * 8 + 2 * g + 2)
                pe.wait_ge(pt_odd, b * 8 + 2 * g + 2)
                if not (isinstance(m, int) and m == 0):
                    pe.wait_ge(o_out, m)
                    pe.wait_ge(mix1_out, m)
                if g == 0:
                    pe.wait_ge(ctx_tok_in, b * 16 + 16)
                    if not (isinstance(b, int) and b == 0):
                        pe.wait_ge(x_done, b)
                for c in range(CT):
                    for t in range(KT):
                        ins = pe.matmul(mbank[c][:, 0:G * S], ctx_tok[:, t, c * P:(c + 1) * P],
                                        probsT[:, t, :, :].rearrange("p g s -> p (g s)"), start=t == 0, stop=t == KT - 1)
                ins.then_inc(mixes, 1)

            def head_values(g, b):
                m = b * NG + g
                pe.wait_ge(mix0_out, m + 1)
                pe.wait_ge(mix1_out, m + 1)
                for j in range(G):
                    h = g * G + j
                    for c in range(CT):
                        ins = pe.matmul(mbank[0][:, j * S:(j + 1) * S], wv[:, c, h * HD1:(h + 1) * HD1],
                                        mixT[:, c, j * S:(j + 1) * S], start=c == 0, stop=c == CT - 1)
                ins.then_inc(heads_out, 1)

            def out(b):
                pe.wait_ge(o_out, b * NG + NG)
                for h in range(H):
                    ins = pe.matmul(mbank[1][0:S, :], oT[:, h, :], wo[:, h, :], start=h == 0, stop=h == H - 1)
                ins.then_inc(wos, 1)

            pe.wait_ge(ctx_in, 16)
            context_half(0, 0)
            context_half(1, 1)
            pe.wait_ge(xn_ready, 1)
            tokens(2)
            pe.wait_ge(w_k, 16 * NG)
            pe.wait_ge(w_q, 16 * NG)
            pe.wait_ge(t_out, 3)
            for n in range(H):
                unit(n, n)
                if n >= 2:
                    unit_T(n - 2, n - 2, n + 1)
            score(0, 0, 0)
            pe.wait_ge(w_v, 16)
            pe.wait_ge(w_o, 16)

            def body(b, first, last):
                use = TP + TB * b
                for h in range(H):
                    n = b * H + h
                    if h < H - 1:
                        score(h + 1, n + 1, b)
                    elif not last:
                        score(0, n + 1, b + 1)
                    if not first:
                        if h == 1:
                            mix(NG - 1, b - 1)
                        if h == 2:
                            head_values(NG - 1, b - 1)
                        if h == 3:
                            out(b - 1)
                    if h >= 5 and h % G == 1:
                        mix(h // G - 1, b)
                    if h >= 6 and h % G == 2:
                        head_values(h // G - 1, b)
                    if h == 0:
                        unit_T(H - 2, n + H - 2, use)
                        if not last:
                            pe.wait_ge(ctx_in, b * 16 + 32)
                            context_half(0, use + 1)
                            context_half(1, use + 2)
                    if h == 1:
                        unit_T(H - 1, b * H + H - 1, use + (1 if last else 3))
                    if not last and h >= 2:
                        unit_T(h - 2, n + H - 2, use + (4 if h == 2 else h + 3))
                    if not last and h == 2:
                        pe.wait_ge(xn_ready, b + 2)
                        tokens(use + 5)
                    if h >= 1:
                        pt(h - 1, n - 1, b)
                    elif not first:
                        pt(H - 1, n - 1, b - 1)
                    if not last:
                        if h == 0:
                            pe.wait_ge(t_out, use + 3)
                        if h == 3:
                            pe.wait_ge(t_out, use + 6)
                        unit(h, n + H)

            body(0, True, False)
            with pe.Fori(1, B - 1) as b:
                body(b, False, False)
            body(B - 1, False, True)
            pt(H - 1, B * H - 1, B - 1)
            mix(NG - 1, B - 1)
            head_values(NG - 1, B - 1)
            out(B - 1)


def phase_experts(nc, A, ident, neg_half, x_all, out):
    E, R, F = 8, 8, A["L1_ffn_W_gate"].shape[1]
    L = (E + 1) * R
    FC = -(-F // P)
    FR = F - (FC - 1) * P
    SG = 4
    T, J = SG * S, B // SG
    with ExitStack() as ctx:
        sb, bank, sem = tools(nc, ctx, "f1")
        w_gate, w_up, w_down = sb("w_gate", [P, DT, F]), sb("w_up", [P, DT, F]), sb("w_down", [P, FC, D])
        a_gate, a_up, a_down = sb("a_gate", [P, DT, L]), sb("a_up", [P, DT, L]), sb("a_down", [P, FC, L])
        b_gate, b_up, b_down = sb("b_gate", [L, F]), sb("b_up", [L, F]), sb("b_down", [L, D])
        w_router, bias, rank = sb("w_router", [P, DT, E]), sb("bias", [P, E]), sb("rank", [P, E])
        xn, xs, xnT = sb("xn", [S, 2, D]), sb("xs", [P, 2, DT * S]), sb("xnT", [P, DT, B * S])
        score, biased = sb("score", [S, B, E]), sb("biased", [S, B, E])
        hot, hot2, best, keys = sb("hot", [S, B, E]), sb("hot2", [S, B, E]), sb("best", [S, B]), sb("keys", [S, B])
        wexp, wexp2, wexpT = sb("wexp", [S, B, L]), sb("wexp2", [S, 2, L]), sb("wexpT", [L, B * S])
        ug, uu, vT = sb("ug", [L, B * S]), sb("uu", [L, B * S]), sb("vT", [L, T])
        sg, hT = sb("sg", [P, 2, T]), sb("hT", [P, FC, T])
        gb, upb = [bank("g0"), bank("g1")], [bank("u0"), bank("u1")]
        tb, ob = [bank("t0"), bank("t1")], [bank("o0"), bank("o1")]
        lb, mb = ob, gb[0]

        l_router, l_small, l_gate, l_down = sem("l_router"), sem("l_small"), sem("l_gate"), sem("l_down")
        rank_set, vl = sem("rank_set"), sem("vl")
        tnorm = TokenNorm(sb, sem, neg_half)
        xn_ready, xT_done, xs_out, xnT_out, logits, logits_out = (sem(n) for n in (
            "xn_ready", "xT_done", "xs_out", "xnT_out", "logits", "logits_out"))
        w_at, wT_done, wT_out, uls, us_out = (sem(n) for n in (
            "w_at", "wT_done", "wT_out", "uls", "us_out"))
        gates, ups, sigs, gs_done, h_ready, vs, v_ready, outs, res_done = (sem(n) for n in (
            "gates", "ups", "sigs", "gs_done", "h_ready", "vs", "v_ready", "outs", "res_done"))
        stored = [sem(f"stored{i}") for i in range(SG)]
        block = ctx.enter_context(nc.Block())
        N_SMALL = 1 + 2 * (E + 3) + 2 * (E + 1) + 2

        @block.sync
        def _(sp):
            def rows(name):
                return A[f"L1_ffn_{name}"]

            sp.dma_start(w_router[:, :, :], rows("W_router").rearrange("(t p) e -> p t e", p=P)).then_inc(l_router, 16)
            sp.dma_start(bias[:, :], rows("expert_bias").partition_broadcast(P)).then_inc(l_small, 16)
            for kind, a, b_ in (("gate", a_gate, b_gate), ("up", a_up, b_up)):
                for e in range(E):
                    sp.dma_start(a[:, :, e * R:(e + 1) * R], rows(f"A_{kind}")[e].rearrange("(t p) r -> p t r", p=P)).then_inc(l_small, 16)
                sp.dma_start(a[:, :, E * R:L], rows(f"sA_{kind}").rearrange("(t p) r -> p t r", p=P)).then_inc(l_small, 16)
                sp.dma_start(b_[0:E * R, :], rows(f"B_{kind}").rearrange("e r f -> (e r) f")).then_inc(l_small, 16)
                sp.dma_start(b_[E * R:L, :], rows(f"sB_{kind}")).then_inc(l_small, 16)
            sp.dma_start(w_gate[:, :, :], rows("W_gate").rearrange("(t p) f -> p t f", p=P)).then_inc(l_gate, 16)
            sp.dma_start(w_up[:, :, :], rows("W_up").rearrange("(t p) f -> p t f", p=P)).then_inc(l_gate, 16)
            full = (FC - 1) * P
            for e in range(E + 1):
                src = rows("A_down")[e] if e < E else rows("sA_down")
                sp.dma_start(a_down[:, 0:FC - 1, e * R:(e + 1) * R], src[0:full, :].rearrange("(c p) r -> p c r", p=P)).then_inc(l_small, 16)
                sp.dma_start(a_down[0:FR, FC - 1, e * R:(e + 1) * R], src[full:F, :]).then_inc(l_small, 16)
            sp.dma_start(b_down[0:E * R, :], rows("B_down").rearrange("e r d -> (e r) d")).then_inc(l_small, 16)
            sp.dma_start(b_down[E * R:L, :], rows("sB_down")).then_inc(l_small, 16)
            sp.dma_start(w_down[:, 0:FC - 1, :], rows("W_down")[0:full, :].rearrange("(c p) d -> p c d", p=P)).then_inc(l_down, 16)
            sp.dma_start(w_down[0:FR, FC - 1, :], rows("W_down")[full:F, :]).then_inc(l_down, 16)
            with sp.Fori(0, J) as j:
                for i in range(SG):
                    sp.wait_ge(res_done, j * SG + i + 1)
                    sp.dma_start(out[j * SG + i], x_all[:, j * SG + i, :]).then_inc(stored[i], 16)
            for i in range(SG):
                sp.wait_ge(stored[i], 16 * J)

        @block.gpsimd
        def _(pool):
            for e in range(E):
                pool.memset(rank[:, e:e + 1], float(E - e)).then_inc(rank_set, 1)
            pool.memset(wexp[:, :, E * R:L], 1.0 / R).then_inc(rank_set, 1)

            with pool.Fori(0, B) as b:
                tnorm.root_of(pool, b)

        @block.scalar
        def _(act):
            with act.Fori(0, B // 2) as i:
                for u in range(2):
                    b = i * 2 + u
                    act.wait_ge(xT_done, b + 1)
                    act.activation(xs[:, u, :], tb[u][:, 0:DT * S], ACT.Copy).then_inc(xs_out, 1)
                    act.wait_ge(logits, b + 1)
                    act.activation(score[:, b, :], lb[u][0:S, 0:E], ACT.Sigmoid).then_inc(logits_out, 1)
            with act.Fori(0, J) as j:
                act.wait_ge(wT_done, j * SG + SG)
                act.activation(wexpT[:, bass.ds(j * T, T)], mb[0:L, 0:T], ACT.Copy).then_inc(wT_out, 1)
            with act.Fori(0, J) as j:
                for c in range(FC):
                    rows = P if c < FC - 1 else FR
                    act.wait_ge(gates, j * FC + c + 1)
                    act.activation(sg[0:rows, c % 2, :], gb[c % 2][0:rows, 0:T], ACT.Sigmoid).then_inc(sigs, 1)

        @block.tensor
        def _(pe):
            pe.wait_ge(l_router, 16)
            with pe.Fori(0, B // 2) as i:
                for u in range(2):
                    b = i * 2 + u
                    pe.wait_ge(xn_ready, b + 1)
                    for t in range(DT):
                        ins = pe.transpose(tb[u][:, t * S:(t + 1) * S], xn[:, u, t * P:(t + 1) * P], ident[0:S, 0:S])
                    ins.then_inc(xT_done, 1)
                    pe.wait_ge(xs_out, b + 1)
                    for t in range(DT):
                        ins = pe.matmul(lb[u][0:S, 0:E], xs[:, u, t * S:(t + 1) * S], w_router[:, t, :], start=t == 0, stop=t == DT - 1)
                    ins.then_inc(logits, 1)

            def weights_T(j, first):
                for i in range(SG):
                    pe.wait_ge(w_at, j * SG + i + 1)
                    if i == 0 and not first:
                        pe.wait_ge(wT_out, j)
                    ins = pe.transpose(mb[0:L, i * S:(i + 1) * S], wexp2[:, i % 2, :], ident[0:S, 0:S])
                    ins.then_inc(wT_done, 1)

            weights_T(0, True)
            with pe.Fori(1, J) as j:
                weights_T(j, False)
            pe.wait_ge(l_small, 16 * N_SMALL)

            def lora_in(j, first):
                for k, a in enumerate((a_gate, a_up)):
                    if not first:
                        pe.wait_ge(us_out, j * 2 + k - 1)
                    for t in range(DT):
                        ins = pe.matmul(tb[k][0:L, 0:T], a[:, t, :], xnT[:, t, bass.ds(j * T, T)], start=t == 0, stop=t == DT - 1)
                    ins.then_inc(uls, 1)

            pe.wait_ge(xnT_out, B)
            lora_in(0, True)
            with pe.Fori(1, J) as j:
                lora_in(j, False)
            pe.wait_ge(l_gate, 32)
            pe.wait_ge(us_out, 2 * J)

            def one_pass(j, first):
                for c in range(FC):
                    rows = P if c < FC - 1 else FR
                    if c >= 2:
                        pe.wait_ge(h_ready, j * FC + c - 1)
                    elif c == 0 and not first:
                        pe.wait_ge(h_ready, j * FC)
                    for dst, w, b_, u_, done in ((gb, w_gate, b_gate, ug, gates), (upb, w_up, b_up, uu, ups)):
                        for t in range(DT):
                            pe.matmul(dst[c % 2][0:rows, 0:T], w[:, t, c * P:c * P + rows], xnT[:, t, bass.ds(j * T, T)], start=t == 0, stop=False)
                        pe.matmul(dst[c % 2][0:rows, 0:T], b_[:, c * P:c * P + rows], u_[:, bass.ds(j * T, T)], start=False, stop=True).then_inc(done, 1)
                if first:
                    pe.wait_ge(l_down, 32)
                pe.wait_ge(h_ready, j * FC + FC)
                for c in range(FC):
                    rows = P if c < FC - 1 else FR
                    ins = pe.matmul(tb[0][0:L, 0:T], a_down[0:rows, c, :], hT[0:rows, c, :], start=c == 0, stop=c == FC - 1)
                ins.then_inc(vs, 1)
                for i in range(SG):
                    if i >= 2:
                        pe.wait_ge(res_done, j * SG + i - 1)
                    for c in range(FC):
                        rows = P if c < FC - 1 else FR
                        pe.matmul(ob[i % 2][0:S, :], hT[0:rows, c, i * S:(i + 1) * S], w_down[0:rows, c, :], start=c == 0, stop=False)
                    if i == 0:
                        pe.wait_ge(v_ready, j + 1)
                    pe.matmul(ob[i % 2][0:S, :], vT[:, i * S:(i + 1) * S], b_down[:, :], start=False, stop=True).then_inc(outs, 1)

            one_pass(0, True)
            with pe.Fori(1, J) as j:
                one_pass(j, False)

        @block.vector
        def _(dve):
            link = Links(dve, vl, 0)

            LINKS = TokenNorm.LINKS

            def step(b, u, first, last):
                link.base, link.n = b * LINKS, 0
                if not last:
                    tnorm.begin(dve, link, x_all[:, b, :])
                    link.wait()
                if not first:
                    dve.wait_ge(xs_out, b)
                    dve.tensor_scalar(xnT[:, :, bass.ds((b - 1) * S, S)], xs[:, 1 - u, :].rearrange("p (t s) -> p t s", t=DT), 1.0, None, ALU.mult).then_inc(xnT_out, 1)
                if not last:
                    tnorm.end(dve, link)
                    tnorm.apply(dve, b, x_all[:, b, :], xn[:, u, :]).then_inc(xn_ready, 1)

            step(0, 0, True, False)
            step(1, 1, False, False)
            with dve.Fori(1, B // 2) as i:
                for u in range(2):
                    step(i * 2 + u, u, False, False)
            step(B, 0, False, True)
            link.base, link.n = B * LINKS, 0
            dve.wait_ge(logits_out, B)
            dve.wait_ge(l_small, 16 * N_SMALL)
            dve.wait_ge(rank_set, E + 1)
            per = [S, B, E]
            link(dve.tensor_tensor(biased[:, :, :], score[:, :, :], bias[0:S, :].unsqueeze(1).broadcast_to(per), ALU.add))
            one_hot_first_max(dve, link, biased[:, :, :], best[:, :], rank[0:S, :], keys[:, :], hot[:, :, :])
            link(dve.tensor_scalar(hot2[:, :, :], hot[:, :, :], -1e30, None, ALU.mult))
            link(dve.tensor_tensor(biased[:, :, :], biased[:, :, :], hot2[:, :, :], ALU.add))
            one_hot_first_max(dve, link, biased[:, :, :], best[:, :], rank[0:S, :], keys[:, :], hot2[:, :, :])
            link(dve.tensor_tensor(hot[:, :, :], hot[:, :, :], hot2[:, :, :], ALU.add))
            link(dve.tensor_tensor(hot[:, :, :], hot[:, :, :], score[:, :, :], ALU.mult))
            link(dve.tensor_reduce(best[:, :], hot[:, :, :], AXX, ALU.add))
            link(dve.tensor_scalar(best[:, :], best[:, :], 1e-8, None, ALU.add))
            link(dve.reciprocal(best[:, :], best[:, :]))
            link(dve.tensor_scalar(best[:, :], best[:, :], 1.0 / R, None, ALU.mult))
            link(dve.tensor_tensor(hot[:, :, :], hot[:, :, :], best[:, :].unsqueeze(2).broadcast_to(per), ALU.mult))
            for e in range(E):
                link(dve.tensor_copy(wexp[:, :, e * R:(e + 1) * R], hot[:, :, e:e + 1].broadcast_to([S, B, R])))

            def hand_over(b, u, wait):
                if wait:
                    dve.wait_ge(wT_done, b - 1)
                dve.tensor_scalar(wexp2[:, u, :], wexp[:, b, :], 1.0, None, ALU.mult).then_inc(w_at, 1)

            hand_over(0, 0, False)
            hand_over(1, 1, False)
            with dve.Fori(1, B // 2) as i:
                for u in range(2):
                    hand_over(i * 2 + u, u, True)
            with dve.Fori(0, J) as j:
                cols = bass.ds(j * T, T)
                dve.wait_ge(wT_out, j + 1)
                for k, u_ in enumerate((ug, uu)):
                    dve.wait_ge(uls, j * 2 + k + 1)
                    dve.tensor_tensor(u_[:, cols], tb[k][0:L, 0:T], wexpT[:, cols], ALU.mult).then_inc(us_out, 1)

            def one_pass(j, first):
                for c in range(FC):
                    rows = P if c < FC - 1 else FR
                    m = j * FC + c
                    dve.wait_ge(sigs, m + 1)
                    dve.tensor_tensor(sg[0:rows, c % 2, :], gb[c % 2][0:rows, 0:T], sg[0:rows, c % 2, :], ALU.mult).then_inc(gs_done, 1)
                    dve.wait_ge(gs_done, m + 1)
                    dve.wait_ge(ups, m + 1)
                    dve.tensor_tensor(hT[0:rows, c, :], upb[c % 2][0:rows, 0:T], sg[0:rows, c % 2, :], ALU.mult).then_inc(h_ready, 1)
                dve.wait_ge(vs, j + 1)
                dve.tensor_tensor(vT[:, :], tb[0][0:L, 0:T], wexpT[:, bass.ds(j * T, T)], ALU.mult).then_inc(v_ready, 1)
                for i in range(SG):
                    dve.wait_ge(outs, j * SG + i + 1)
                    dve.tensor_tensor(x_all[:, j * SG + i, :], ob[i % 2][0:S, :], x_all[:, j * SG + i, :], ALU.add).then_inc(res_done, 1)

            one_pass(0, True)
            with dve.Fori(1, J) as j:
                one_pass(j, False)


def build(nc, A, out):
    with ExitStack() as ctx:
        x_all = ctx.enter_context(nc.sbuf_tensor("x_all", [S, B, D], FP32))
        ident = ctx.enter_context(nc.sbuf_tensor("ident", [P, P], FP32))
        neg_half = ctx.enter_context(nc.sbuf_tensor("neg_half", [P, 1], FP32))
        vd_dram = nc.dram_tensor("vd_rows", [B * ND, D], FP32, kind="Internal").ap()
        phase_constants(nc, ident, neg_half)
        phase_attention0(nc, A, ident, neg_half, x_all, vd_dram)
        phase_select(nc, A, ident, neg_half, x_all)
        phase_attention1(nc, A, ident, neg_half, x_all)
        phase_experts(nc, A, ident, neg_half, x_all, out)


def kernel(**inputs):
    import numpy as _np
    import concourse.bacc as _bacc
    from concourse.bass_utils import run_bass_kernel_spmd as _run

    nc = _bacc.Bacc("TRN2", target_bir_lowering=False, num_devices=1)
    arrays, A = {}, {}
    for name, a in inputs.items():
        a = _np.ascontiguousarray(a)
        arrays[f"in_{name}"] = a
        A[name] = nc.dram_tensor(f"in_{name}", a.shape, FP32, kind="ExternalInput").ap()
    out = nc.dram_tensor("out", (B, S, D), FP32, kind="ExternalOutput").ap()
    build(nc, A, out)
    r = _run(nc, [arrays], core_ids=[0])
    return r.results[0]["out"]
```

```python
import concourse.bass as bass
from concourse import mybir
from contextlib import ExitStack

FP32, FP32R = mybir.dt.float32, mybir.dt.float32r
ALU = mybir.AluOpType
ACT = mybir.ActivationFunctionType
AXX = mybir.AxisListType.X

B, S, D, C = 16, 112, 512, 256
KV, ND = 375, 16
NM = KV - ND
P = 128
DT, CT = D // P, C // P
KR = 125
KT = KV // KR
H = 16
G = 4
NG = H // G
HD0 = D // H
HD1 = 128
LN_EPS, QK_EPS, RMS_EPS = 1e-5, 1e-6, 1e-5


class Links:

    def __init__(self, eng, sem, base):
        self.eng, self.sem, self.base, self.n = eng, sem, base, 0

    def mark(self, ins):
        ins.then_inc(self.sem, 1)
        self.n += 1

    def wait(self):
        self.eng.wait_ge(self.sem, self.base + self.n)

    def __call__(self, ins):
        self.mark(ins)
        self.wait()


def tools(nc, ctx, tag):
    def sb(name, shape):
        return ctx.enter_context(nc.sbuf_tensor(f"{tag}_{name}", shape, FP32))

    def bank(name):
        return ctx.enter_context(nc.psum_tensor(f"{tag}_{name}", [P, 512], FP32))

    def sem(name):
        return ctx.enter_context(nc.semaphore(f"{tag}_{name}"))

    return sb, bank, sem


class TokenNorm:

    LINKS = 2

    def __init__(self, sb, sem, neg_half):
        self.stats, self.mean_var, self.root = sb("stats", [S, 6]), sb("mean_var", [S, 2]), sb("root_x", [S, 1])
        self.neg_half, self.variances, self.roots = neg_half, sem("variances"), sem("x_roots")

    def begin(self, dve, link, x):
        link.mark(dve.bn_stats(self.stats[:, :], x))

    def end(self, dve, link):
        link(dve.bn_aggr(self.mean_var[:, :], self.stats[:, :]))
        dve.tensor_scalar(self.mean_var[:, 1:2], self.mean_var[:, 1:2], LN_EPS, None, ALU.add).then_inc(self.variances, 1)

    def root_of(self, pool, b):
        pool.wait_ge(self.variances, b + 1)
        pool.tensor_tensor(self.root[:, :], self.mean_var[:, 1:2], self.neg_half[0:S, :], ALU.pow).then_inc(self.roots, 1)

    def apply(self, dve, b, x, out):
        dve.wait_ge(self.roots, b + 1)
        return dve.tensor_scalar(out, x, self.mean_var[:, 0:1], self.root[:, :], ALU.subtract, ALU.mult)


class AllTokensNorm:

    def __init__(self, sb, sem, neg_half):
        self.stats, self.mean_var, self.root = sb("stats", [S, B, 6]), sb("mean_var", [S, B, 2]), sb("root_x", [S, B])
        self.neg_half, self.steps, self.variances, self.roots = neg_half, sem("norm_steps"), sem("variances"), sem("x_roots")

    def statistics(self, dve, x_all):
        with dve.Fori(0, B) as b:
            dve.bn_stats(self.stats[:, b, :], x_all[:, b, :]).then_inc(self.steps, 1)
        dve.wait_ge(self.steps, B)
        for b in range(B):
            dve.bn_aggr(self.mean_var[:, b, :], self.stats[:, b, :]).then_inc(self.steps, 1)
        dve.wait_ge(self.steps, 2 * B)
        dve.tensor_scalar(self.mean_var[:, :, 1:2], self.mean_var[:, :, 1:2], LN_EPS, None, ALU.add).then_inc(self.variances, 1)

    def root_of(self, pool):
        pool.wait_ge(self.variances, 1)
        pool.tensor_tensor(self.root[:, :].unsqueeze(2), self.mean_var[:, :, 1:2], self.neg_half[0:S, :].unsqueeze(1).broadcast_to([S, B, 1]),
                           ALU.pow).then_inc(self.roots, 1)

    def apply(self, dve, b, x, out):
        return dve.tensor_scalar(out, x, self.mean_var[:, b, 0:1], self.root[:, bass.ds(b, 1)], ALU.subtract, ALU.mult)


def phase_constants(nc, ident, neg_half):
    with ExitStack() as ctx:
        _, _, sem = tools(nc, ctx, "id")
        zeroed, made = sem("zeroed"), sem("made")
        block = ctx.enter_context(nc.Block())

        @block.gpsimd
        def _(pool):
            pool.memset(neg_half[:, :], -0.5).then_inc(zeroed, 1)
            pool.memset(ident[:, :], 0.0).then_inc(zeroed, 1)
            pool.wait_ge(zeroed, 2)
            pool.affine_select(out=ident[:, :], in_=ident[:, :], compare_op=ALU.not_equal, fill=1.0, base=0,
                               pattern=[[-1, P]], channel_multiplier=1).then_inc(made, 1)
            pool.wait_ge(made, 1)


def phase_attention0(nc, A, ident, neg_half, x_all, vd_dram):
    SCALE = float(HD0) ** -0.5
    UB, AB, EB = 10, 3, 7
    with ExitStack() as ctx:
        sb, bank, sem = tools(nc, ctx, "a0")
        wq, wk, wv = sb("wq", [P, DT, D]), sb("wk", [P, CT, D]), sb("wv", [P, CT, D])
        wd, wo = sb("wd", [P, CT, 2 * D]), sb("wo", [P, DT, D])
        bq, bk, bv, bd, bo = (sb(n, [P, w]) for n, w in (("bq", D), ("bk", D), ("bv", D), ("bd", 2 * D), ("bo", D)))
        qw, qb, head_rows = sb("qw", [P, 1]), sb("qb", [P, 1]), sb("head_rows", [P, G])
        q_all = sb("q_all", [P, 2, S])
        kw, kb, dw, db = sb("kw", [P, 1]), sb("kb", [P, 1]), sb("dw", [P, 1]), sb("db", [P, 1])
        dcain, dcaT = sb("dcain", [P, 2, C]), sb("dcaT", [P, CT, 2 * P])
        kdT, vd = sb("kdT", [P, NG, B * ND]), sb("vd", [P, 2, D])
        ctxin, ctxT = sb("ctxin", [KR, KT, C]), sb("ctxT", [P, CT, KV])
        xn, xnT = sb("xn", [S, D]), sb("xnT", [P, DT, S])
        raw, cen, sq = sb("raw", [P, 2, D]), sb("cen", [P, KT + 1, D]), sb("sq", [P, 2, D])
        nmean, msq, rstd = sb("nmean", [P, 2, H]), sb("msq", [P, KT + 1, H]), sb("rstd", [P, KT + 1, H])
        kn, qn = sb("kn", [KR, KT, D]), sb("qn", [S, D])
        keysT, qT = sb("keysT", [P, NG, KV]), sb("qT", [P, H, S])
        vals_next, vals = sb("vals_next", [KR, KT, D]), sb("vals", [KR, KT, D])
        probs, probsT = sb("probs", [S, 4, KV]), sb("probsT", [KR, KT, G, S])
        nmax, sums, rsum = sb("nmax", [S, 4, 2]), sb("sums", [S, 4, 2]), sb("rsum", [S, 4, 2])
        oT = sb("oT", [P, NG, S])

        proj = [bank("proj0"), bank("proj1")]
        tbank = bank("tbank")
        sbank = [bank("s0"), bank("s1")]
        ptbank, obank, wbank = bank("pt"), bank("o"), bank("w")

        x_first, x_rest, w_k, w_q, w_d, w_vo, params, dca_in = (sem(n) for n in (
            "x_first", "x_rest", "w_k", "w_q", "w_d", "w_vo", "params", "dca_in"))
        ctx_in, vd_out, vd_patch, columns = sem("ctx_in"), sem("vd_out"), sem("vd_patch"), sem("columns")
        units, trs, scores, pts, pvs, wos = (sem(n) for n in ("units", "trs", "scores", "pts", "pvs", "wos"))
        unit_v, unit_a = sem("unit_v"), sem("unit_a")
        centred, squared, msqs, normed = sem("centred"), sem("squared"), sem("msqs"), sem("normed")
        keys_ready, q_affine, q_ready, vals_ready = sem("keys_ready"), sem("q_affine"), sem("q_ready"), sem("vals_ready")
        maxes, exps, rsums, pnorms = sem("maxes"), sem("exps"), sem("rsums"), sem("pnorms")
        pt_even, pt_odd, o_done, xn_ready, x_biased, x_done = (sem(n) for n in (
            "pt_even", "pt_odd", "o_done", "xn_ready", "x_biased", "x_done"))
        vlink, plink = sem("vlink"), sem("plink")
        d_tr, d_tre, d_mm, d_raw, d_knt, d_kdt = (sem(n) for n in (
            "d_tr", "d_tre", "d_mm", "d_raw", "d_knt", "d_kdt"))
        tnorm = TokenNorm(sb, sem, neg_half)
        outs_rows = [KR, KR, KR, S]
        block = ctx.enter_context(nc.Block())
        ctx_rows = A["ctx_1024"].rearrange("b (t p) c -> b p t c", p=KR)

        @block.sync
        def _(sp):
            for b in range(B):
                sp.dma_start(dcain[ND * (b % 8):ND * (b % 8 + 1), b // 8, :], A["ctx_1024"][b, NM:KV, :]).then_inc(dca_in, 16)
            sp.dma_start(wd[:, :, :], A["L0_xattn_Wkv_dca"].rearrange("(t p) n -> p t n", p=P)).then_inc(w_d, 16)
            sp.dma_start(x_all[:, 0:2, :], A["x"][0:2].rearrange("b s d -> s b d")).then_inc(x_first, 16)
            sp.dma_start(ctxin[:, :, :], ctx_rows[0]).then_inc(ctx_in, 16)
            def split_columns(w, part, done):
                for i, name in enumerate(("Wk", "Wv")):
                    for t in range(CT):
                        src = A[f"L0_xattn_{name}"][t * P:(t + 1) * P, :].rearrange("p (h two d) -> p h two d", two=2, d=HD0)
                        sp.dma_start(w[:, t, i * D // 2:(i + 1) * D // 2].rearrange("p (h d) -> p h d", d=HD0),
                                     src[:, :, part, :]).then_inc(done, 16)

            split_columns(wk, 0, w_k)
            sp.dma_start(wq[:, :, :], A["L0_xattn_Wq"].rearrange("(t p) n -> p t n", p=P)).then_inc(w_q, 16)
            split_columns(wv, 1, w_vo)
            sp.dma_start(wo[:, :, :], A["L0_xattn_Wo"].rearrange("(t p) n -> p t n", p=P)).then_inc(w_vo, 16)
            sp.dma_start(x_all[:, 2:B, :], A["x"][2:B].rearrange("b s d -> s b d")).then_inc(x_rest, 16)
            sp.wait_ge(d_raw, 4)
            sp.dma_start(vd_dram.rearrange("(t p) n -> p t n", p=P), vd[:, :, :]).then_inc(vd_out, 16)
            sp.wait_ge(vd_out, 16)

            def per_batch(b, last):
                if not last:
                    sp.wait_ge(units, UB * b + 2)
                    sp.dma_start(ctxin[:, :, :], ctx_rows[b + 1]).then_inc(ctx_in, 16)
                sp.wait_ge(unit_v, EB * b + EB)
                sp.dma_start(vals_next[KR - ND:KR, KT - 1, :], vd_dram[bass.ds(b * ND, ND), :]).then_inc(vd_patch, 16)

            with sp.Fori(0, B - 1) as b:
                per_batch(b, False)
            per_batch(B - 1, True)
            sp.wait_ge(vd_patch, 16 * B)

        @block.gpsimd
        def _(pool):
            pool.memset(head_rows[:, :], 0.0).then_inc(columns, 1)
            for j in range(G):
                pool.wait_ge(columns, 1 + j)
                pool.memset(head_rows[HD0 * j:HD0 * j + HD0, j:j + 1], 1.0).then_inc(columns, 1)
            pool.wait_ge(columns, 1 + G)
            plinks = Links(pool, plink, 0)

            def scale(k, rows, out, wait_for):
                pool.wait_ge(msqs, wait_for)
                plinks(pool.tensor_tensor(rstd[0:rows, k, :], msq[0:rows, k, :], neg_half[0:rows, :].broadcast_to([rows, H]), ALU.pow))
                pool.tensor_tensor(out.rearrange("p (h d) -> p h d", h=H),
                                   cen[0:rows, k, :].rearrange("p (h d) -> p h d", h=H),
                                   rstd[0:rows, k, :].unsqueeze(2).broadcast_to([rows, H, HD0]), ALU.mult).then_inc(normed, 1)

            for t in range(2):
                scale(t, P, raw[:, t, :], t + 1)
            n0 = 2
            tnorm.root_of(pool, 0)
            outs = [(kn[:, 0, :], KR), (kn[:, 1, :], KR), (kn[:, 2, :], KR), (qn[:, :], S)]

            def project(k, base):
                scale(k, outs[k][1], outs[k][0], base + k + 1)

            for k in range(4):
                project(k, n0)

            def queries(c, b):
                pool.wait_ge(q_affine, b * NG + c + 1)
                pool.tensor_tensor(qT[:, G * c:G * c + G, :], q_all[:, c % 2, :].unsqueeze(1).broadcast_to([P, G, S]),
                                   head_rows[:, :].unsqueeze(2).broadcast_to([P, G, S]), ALU.mult).then_inc(q_ready, 1)

            for c in range(NG):
                queries(c, 0)
            base0, LINKS = plinks.n, 4

            def body(b, last):
                plinks.base, plinks.n = base0 + LINKS * b, 0
                for h in range(H):
                    n = b * H + h
                    if not last and h == 0:
                        tnorm.root_of(pool, b + 1)
                    if not last and 4 <= h <= 7:
                        project(h - 4, n0 + 4 + 4 * b)
                    if h == 8:
                        pool.tensor_tensor(x_all[:, b, :], x_all[:, b, :], bo[0:S, :], ALU.add).then_inc(x_biased, 1)
                    if not last and h >= 12:
                        queries(h - 12, b + 1)

            pool.wait_ge(params, 16 * 31)
            with pool.Fori(0, B - 1) as b:
                body(b, False)
            body(B - 1, True)

        @block.scalar
        def _(act):
            for name, t in (("qn_w", qw), ("qn_b", qb)):
                for j in range(G):
                    act.dma_start(t[HD0 * j:HD0 * j + HD0, :], A[f"L0_xattn_{name}"].rearrange("(n o) -> n o", o=1)).then_inc(params, 16)
            for name, t in (("kn_w", kw), ("kn_b", kb), ("kn_dca_w", dw), ("kn_dca_b", db)):
                for j in range(G):
                    act.dma_start(t[HD0 * j:HD0 * j + HD0, :], A[f"L0_xattn_{name}"].rearrange("(n o) -> n o", o=1)).then_inc(params, 16)
            for name, t in (("bq", bq), ("bkv_dca", bd), ("bo", bo)):
                act.dma_start(t[:, :], A[f"L0_xattn_{name}"].partition_broadcast(P)).then_inc(params, 16)
            for part, t in enumerate((bk, bv)):
                for i, name in enumerate(("bk", "bv")):
                    src = A[f"L0_xattn_{name}"].rearrange("(h two d) -> h two d", two=2, d=HD0)[:, part, :]
                    act.dma_start(t[:, i * D // 2:(i + 1) * D // 2].rearrange("p (h d) -> p h d", d=HD0),
                                   src.partition_broadcast(P)).then_inc(params, 16)

            def square(k, rows, wait_for):
                act.wait_ge(centred, wait_for)
                act.activation(sq[0:rows, k % 2, :], cen[0:rows, k, :], ACT.Square, scale=HD0 ** -0.5).then_inc(squared, 1)

            for c in range(CT):
                act.wait_ge(d_tr, c + 1)
                act.activation(dcaT[:, c, :], proj[c][:, 0:2 * P], ACT.Copy).then_inc(d_tre, 1)
            for t in range(2):
                square(t, P, t + 1)
            act.wait_ge(params, 16 * 31)
            for t in range(2):
                act.wait_ge(d_knt, t + 1)
                act.activation(kdT[:, :, t * P:(t + 1) * P], tbank[:, :].rearrange("p (g s) -> p g s", g=NG), ACT.Identity,
                               bias=db[:, :], scale=dw[:, :]).then_inc(d_kdt, 1)

            def take(k, base):
                act.wait_ge(units, base + k + 1)
                if k < 2:
                    ins = act.activation(ctxT[:, k, :], proj[(k + 1) % 2][:, 0:KV], ACT.Copy)
                else:
                    ins = act.activation(xnT[:, :, :], proj[1][:, 0:DT * S].rearrange("p (t s) -> p t s", t=DT), ACT.Copy)
                ins.then_inc(unit_a, 1)

            def chunk(c, b):
                act.wait_ge(trs, b * NG + c + 1)
                act.activation(keysT[:, c, 0:NM], tbank[:, 0:NM], ACT.Identity, bias=kb[:, :], scale=kw[:, :])
                act.activation(keysT[:, c, NM:KV], kdT[:, c, bass.ds(b * ND, ND)], ACT.Copy).then_inc(keys_ready, 1)
                if not (isinstance(b, int) and b == 0 and c < 2):
                    act.wait_ge(q_ready, b * NG + c - 1)
                act.activation(q_all[:, c % 2, :], tbank[:, KV:KV + S], ACT.Identity, bias=qb[:, :], scale=qw[:, :]).then_inc(q_affine, 1)

            def exp(h, n):
                act.wait_ge(maxes, n + 1)
                act.activation(probs[:, h % 4, 0:NM], sbank[h % 2][0:S, 0:NM], ACT.Exp, bias=nmax[:, h % 4, 0:1],
                               accum_out=sums[:, h % 4, 0:1])
                act.activation(probs[:, h % 4, NM:KV], sbank[h % 2][0:S, NM:KV], ACT.Exp, bias=nmax[:, h % 4, 1:2],
                               accum_out=sums[:, h % 4, 1:2]).then_inc(exps, 1)

            for k in range(3):
                take(k, 0)
            for k in range(4):
                square(k, outs_rows[k], 2 + k + 1)
            act.wait_ge(vlink, 2)
            act.wait_ge(d_kdt, 2)
            for c in range(NG):
                chunk(c, 0)
            exp(0, 0)

            def pt_out(h, n):
                act.wait_ge(pts, n + 1)
                act.activation(probsT[:, :, h % G, :], ptbank[0:KR, 0:KT * S].rearrange("p (t s) -> p t s", t=KT), ACT.Copy).then_inc(pt_even, 1)

            def values(b):
                act.wait_ge(unit_v, EB * b + EB)
                act.wait_ge(vd_patch, b * 16 + 16)
                if not (isinstance(b, int) and b == 0):
                    act.wait_ge(pvs, b * NG)
                act.activation(vals[:, :, :], vals_next[:, :, :], ACT.Copy).then_inc(vals_ready, 1)

            def body(b, last):
                for h in range(H):
                    n = b * H + h
                    if h % G == 3:
                        pt_out(h - 1, n - 1)
                    if not (last and h == H - 1):
                        if not (h + 1 < 4 and isinstance(b, int) and b == 0):
                            act.wait_ge(pts, n - 2)
                        exp((h + 1) % H, n + 1)
                    if h % G == 1:
                        if not (h == 1 and isinstance(b, int) and b == 0):
                            act.wait_ge(pvs, NG * b + h // G)
                        pt_out(h - 1, n - 1)
                    if h == 2:
                        values(b)
                    if not last:
                        if h == 0:
                            take(0, UB * b + UB)
                            take(1, UB * b + UB)
                        if h == 2:
                            take(2, UB * b + UB)
                        if 3 <= h <= 6:
                            square(h - 3, outs_rows[h - 3], 2 + 4 + 4 * b + h - 3 + 1)
                        if h >= 12:
                            chunk(h - 12, b + 1)

            body(0, False)
            with act.Fori(1, B - 1) as b:
                body(b, False)
            body(B - 1, True)

        @block.vector
        def _(dve):
            dve.wait_ge(params, 16 * 31)
            link = Links(dve, vlink, 0)
            link.mark(dve.tensor_scalar(qw[:, :], qw[:, :], SCALE, None, ALU.mult))
            link.mark(dve.tensor_scalar(qb[:, :], qb[:, :], SCALE, None, ALU.mult))

            def part1(k, rows, psum, bias, done):
                dve.tensor_tensor(raw[0:rows, k, :], psum[0:rows, :], bias[0:rows, 0:D], ALU.add).then_inc(done, 1)

            def centre(k, rows, free):
                link(dve.tensor_reduce(nmean[0:rows, k % 2, :], raw[0:rows, k % 2, :].rearrange("p (h d) -> p h d", h=H), AXX, ALU.add))
                link(dve.tensor_scalar(nmean[0:rows, k % 2, :], nmean[0:rows, k % 2, :], -1.0 / HD0, None, ALU.mult))
                if free is not None:
                    dve.wait_ge(normed, free)
                dve.tensor_tensor(cen[0:rows, k, :].rearrange("p (h d) -> p h d", h=H),
                                  raw[0:rows, k % 2, :].rearrange("p (h d) -> p h d", h=H),
                                  nmean[0:rows, k % 2, :].unsqueeze(2).broadcast_to([rows, H, HD0]), ALU.add).then_inc(centred, 1)

            def part2(k, rows, wait_for):
                dve.wait_ge(squared, wait_for)
                link(dve.tensor_reduce(msq[0:rows, k, :], sq[0:rows, k % 2, :].rearrange("p (h d) -> p h d", h=H), AXX, ALU.add))
                dve.tensor_scalar(msq[0:rows, k, :], msq[0:rows, k, :], QK_EPS, None, ALU.add).then_inc(msqs, 1)

            for t in range(2):
                dve.wait_ge(d_mm, 2 * t + 1)
                part1(t, P, proj[t], bd, d_raw)
                dve.wait_ge(d_mm, 2 * t + 2)
                dve.tensor_tensor(vd[:, t, :], sbank[t][:, :], bd[:, D:2 * D], ALU.add).then_inc(d_raw, 1)
                dve.wait_ge(d_raw, 2 * t + 1)
                centre(t, P, None)
            for t in range(2):
                part2(t, P, t + 1)

            def unit(k, base_u, base_v, base_n):
                dve.wait_ge(units, base_u + k + 1)
                part1(k % 2, outs_rows[k], proj[k % 2], bk if k < 3 else bq, unit_v)
                dve.wait_ge(unit_v, base_v + k + 1)
                centre(k, outs_rows[k], base_n)

            dve.wait_ge(x_first, 16)
            tnorm.begin(dve, link, x_all[:, 0, :])
            link.wait()
            tnorm.end(dve, link)
            tnorm.apply(dve, 0, x_all[:, 0, :], xn[:, :]).then_inc(xn_ready, 1)
            for k in range(5):
                if k < 4:
                    if k == 0:
                        dve.wait_ge(d_knt, 2)
                    unit(k, 3, 0, 2)
                if k >= 1:
                    part2(k - 1, outs_rows[k - 1], 2 + k)

            def max_(h, n):
                dve.wait_ge(scores, n + 1)
                dve.tensor_reduce(nmax[:, h % 4, 0:1], sbank[h % 2][0:S, 0:NM], AXX, ALU.max, negate=True)
                dve.tensor_reduce(nmax[:, h % 4, 1:2], sbank[h % 2][0:S, NM:KV], AXX, ALU.max, negate=True).then_inc(maxes, 1)

            max_(0, 0)

            def values(t, b):
                rows = KR if t < KT - 1 else KR - ND
                dve.wait_ge(units, UB * b + 8 + t)
                if not (isinstance(b, int) and b == 0):
                    dve.wait_ge(vals_ready, b)
                dve.tensor_tensor(vals_next[0:rows, t, :], proj[t % 2][0:rows, :], bv[0:rows, :], ALU.add).then_inc(unit_v, 1)

            for t in range(KT):
                values(t, 0)
            base0 = link.n
            LINKS = TokenNorm.LINKS + 4 * 3

            def pt_out(h, n):
                dve.wait_ge(pts, n + 1)
                dve.tensor_copy(probsT[:, :, h % G, :], ptbank[0:KR, 0:KT * S].rearrange("p (t s) -> p t s", t=KT)).then_inc(pt_odd, 1)

            def o_out(g, n):
                dve.wait_ge(pvs, n + 1)
                for j in range(G):
                    ins = dve.tensor_copy(oT[HD0 * j:HD0 * j + HD0, g, :], obank[HD0 * j:HD0 * j + HD0, j * S:(j + 1) * S])
                ins.then_inc(o_done, 1)

            def x_out(b):
                dve.wait_ge(wos, b + 1)
                dve.wait_ge(x_biased, b + 1)
                dve.tensor_tensor(x_all[:, b, :], wbank[0:S, :], x_all[:, b, :], ALU.add).then_inc(x_done, 1)

            def body(b, first, last):
                link.base, link.n = base0 + LINKS * b, 0
                for h in range(H):
                    n = b * H + h
                    if not (last and h == H - 1):
                        max_((h + 1) % H, n + 1)
                    if first and h == H - 1:
                        dve.wait_ge(x_rest, 16)
                    if h == 0 and not last:
                        tnorm.begin(dve, link, x_all[:, b + 1, :])
                        link.wait()
                    if h % 2 == 0 and h >= 2:
                        pt_out(h - 1, n - 1)
                    dve.wait_ge(exps, n + 1)
                    dve.reciprocal(rsum[:, h % 4, :], sums[:, h % 4, :]).then_inc(rsums, 1)
                    dve.wait_ge(rsums, n + 1)
                    dve.tensor_scalar(probs[:, h % 4, 0:NM], probs[:, h % 4, 0:NM], rsum[:, h % 4, 0:1], None, ALU.mult)
                    dve.tensor_scalar(probs[:, h % 4, NM:KV], probs[:, h % 4, NM:KV], rsum[:, h % 4, 1:2], None, ALU.mult).then_inc(pnorms, 1)
                    if not first:
                        if h == 0:
                            pt_out(H - 1, n - 1)
                        if h == 1:
                            o_out(NG - 1, NG * b - 1)
                        if h == 3:
                            x_out(b - 1)
                    if h % G == 1 and h >= 5:
                        o_out(h // G - 1, NG * b + h // G - 1)
                    if not last:
                        if h == 0:
                            tnorm.end(dve, link)
                        if h == 1:
                            tnorm.apply(dve, b + 1, x_all[:, b + 1, :], xn[:, :]).then_inc(xn_ready, 1)
                        if 3 <= h <= 6:
                            unit(h - 3, UB * b + UB + 3, EB * b + EB, 2 + 4 + 4 * b)
                        if 4 <= h <= 7:
                            part2(h - 4, outs_rows[h - 4], 2 + 4 + 4 * b + h - 4 + 1)
                        if 7 <= h <= 9:
                            values(h - 7, b + 1)
                if not last:
                    assert link.n == LINKS, link.n

            body(0, True, False)
            with dve.Fori(1, B - 1) as b:
                body(b, False, False)
            body(B - 1, False, True)
            pt_out(H - 1, B * H - 1)
            o_out(NG - 1, NG * B - 1)
            x_out(B - 1)
            dve.wait_ge(x_done, B)

        @block.tensor
        def _(pe):
            pe.wait_ge(dca_in, 16 * B)
            for c in range(CT):
                for t in range(2):
                    ins = pe.transpose(proj[c][:, t * P:(t + 1) * P], dcain[:, t, c * P:(c + 1) * P], ident[:, :])
                ins.then_inc(d_tr, 1)
            pe.wait_ge(w_d, 16)
            pe.wait_ge(d_tre, CT)
            for t in range(2):
                for half, dst in enumerate((proj[t], sbank[t])):
                    for c in range(CT):
                        ins = pe.matmul(dst[:, :], dcaT[:, c, t * P:(t + 1) * P], wd[:, c, half * D:(half + 1) * D],
                                        start=c == 0, stop=c == CT - 1)
                    ins.then_inc(d_mm, 1)
            for t in range(2):
                pe.wait_ge(normed, t + 1)
                if t:
                    pe.wait_ge(d_kdt, 1)
                for g in range(NG):
                    ins = pe.transpose(tbank[:, g * P:(g + 1) * P], raw[:, t, g * P:(g + 1) * P], ident[:, :])
                ins.then_inc(d_knt, 1)

            def context_half(c, bank_):
                for t in range(KT):
                    ins = pe.transpose(bank_[:, t * KR:(t + 1) * KR], ctxin[:, t, c * P:(c + 1) * P], ident[0:KR, 0:KR])
                ins.then_inc(units, 1)

            def tokens():
                for t in range(DT):
                    ins = pe.transpose(proj[1][:, t * S:(t + 1) * S], xn[:, t * P:(t + 1) * P], ident[0:S, 0:S])
                ins.then_inc(units, 1)

            def rows_unit(t, w, bank_):
                for c in range(CT):
                    ins = pe.matmul(bank_[0:KR, :], ctxT[:, c, t * KR:(t + 1) * KR], w[:, c, :], start=c == 0, stop=c == CT - 1)
                ins.then_inc(units, 1)

            def q_unit():
                for t in range(DT):
                    ins = pe.matmul(proj[1][0:S, :], xnT[:, t, :], wq[:, t, :], start=t == 0, stop=t == DT - 1)
                ins.then_inc(units, 1)

            def chunk(c, b):
                if c == 0:
                    pe.wait_ge(normed, 2 + 4 + 4 * b)
                if isinstance(b, int) and b == 0 and c == 0:
                    pe.wait_ge(d_kdt, 2)
                else:
                    pe.wait_ge(q_affine, b * NG + c)
                for t in range(KT):
                    pe.transpose(tbank[:, t * KR:(t + 1) * KR], kn[:, t, c * P:(c + 1) * P], ident[0:KR, 0:KR])
                pe.transpose(tbank[:, KV:KV + S], qn[:, c * P:(c + 1) * P], ident[0:S, 0:S]).then_inc(trs, 1)

            def score(h, n, b, free):
                if free:
                    pe.wait_ge(exps, n - 1)
                if h % G == 0:
                    pe.wait_ge(keys_ready, b * NG + h // G + 1)
                    pe.wait_ge(q_ready, b * NG + h // G + 1)
                pe.matmul(sbank[h % 2][0:S, 0:KV], qT[:, h, :], keysT[:, h // G, :], start=True, stop=True).then_inc(scores, 1)

            def pt(h, n, b):
                pe.wait_ge(pnorms, n + 1)
                if not (isinstance(n, int) and n == 0):
                    pe.wait_ge(pt_even if h % 2 else pt_odd, b * 8 + (h + 1) // 2)
                for t in range(KT):
                    ins = pe.transpose(ptbank[0:KR, t * S:(t + 1) * S], probs[:, h % 4, t * KR:(t + 1) * KR], ident[0:S, 0:S])
                ins.then_inc(pts, 1)

            def pv(g, b):
                pe.wait_ge(pt_even, b * 8 + 2 * g + 2)
                pe.wait_ge(pt_odd, b * 8 + 2 * g + 2)
                if not (isinstance(b, int) and b == 0 and g == 0):
                    pe.wait_ge(o_done, b * NG + g)
                if g == 0:
                    pe.wait_ge(vals_ready, b + 1)
                for t in range(KT):
                    ins = pe.matmul(obank[:, 0:G * S], vals[:, t, g * P:(g + 1) * P], probsT[:, t, :, :].rearrange("p g s -> p (g s)"),
                                    start=t == 0, stop=t == KT - 1)
                ins.then_inc(pvs, 1)

            def out(b):
                pe.wait_ge(o_done, b * NG + NG)
                for g in range(NG):
                    ins = pe.matmul(wbank[0:S, :], oT[:, g, :], wo[:, g, :], start=g == 0, stop=g == NG - 1)
                ins.then_inc(wos, 1)

            pe.wait_ge(ctx_in, 16)
            pe.wait_ge(d_raw, 4)
            context_half(0, proj[1])
            context_half(1, proj[0])
            pe.wait_ge(xn_ready, 1)
            pe.wait_ge(unit_a, 1)
            tokens()
            pe.wait_ge(w_k, 16 * 4)
            pe.wait_ge(unit_a, 2)
            rows_unit(0, wk, proj[0])
            pe.wait_ge(unit_a, 3)
            rows_unit(1, wk, proj[1])
            pe.wait_ge(unit_v, 1)
            rows_unit(2, wk, proj[0])
            pe.wait_ge(w_q, 16)
            pe.wait_ge(unit_v, 2)
            q_unit()
            for c in range(NG):
                chunk(c, 0)
            score(0, 0, 0, False)
            pe.wait_ge(w_vo, 16 * 5)
            for t in range(KT):
                pe.wait_ge(unit_v, 3 + t)
                rows_unit(t, wv, proj[t % 2])

            def body(b, first, last):
                for h in range(H):
                    n = b * H + h
                    if h < H - 1:
                        score(h + 1, n + 1, b, not (first and h == 0))
                    elif not last:
                        score(0, n + 1, b + 1, True)
                    if h >= 1:
                        pt(h - 1, n - 1, b)
                    elif not first:
                        pt(H - 1, n - 1, b - 1)
                    if not first:
                        if h == 1:
                            pv(NG - 1, b - 1)
                        if h == 2:
                            out(b - 1)
                    if h >= 5 and h % G == 1:
                        pv(h // G - 1, b)
                    if not last:
                        s, v = AB * b + AB, EB * b + EB
                        if h == 0:
                            pe.wait_ge(ctx_in, b * 16 + 32)
                            pe.wait_ge(unit_v, v - 1)
                            context_half(0, proj[1])
                            pe.wait_ge(unit_v, v)
                            context_half(1, proj[0])
                        if h == 2:
                            pe.wait_ge(xn_ready, b + 2)
                            pe.wait_ge(unit_a, s + 1)
                            tokens()
                        if h == 3:
                            pe.wait_ge(unit_a, s + 2)
                            rows_unit(0, wk, proj[0])
                        if h == 4:
                            pe.wait_ge(unit_a, s + 3)
                            rows_unit(1, wk, proj[1])
                        if h == 5:
                            pe.wait_ge(unit_v, v + 1)
                            rows_unit(2, wk, proj[0])
                        if h == 6:
                            pe.wait_ge(unit_v, v + 2)
                            q_unit()
                        if 7 <= h <= 9:
                            pe.wait_ge(unit_v, v + h - 4)
                            rows_unit(h - 7, wv, proj[(h - 7) % 2])
                        if h >= 12:
                            chunk(h - 12, b + 1)

            body(0, True, False)
            with pe.Fori(1, B - 1) as b:
                body(b, False, False)
            body(B - 1, False, True)
            pt(H - 1, B * H - 1, B - 1)
            pv(NG - 1, B - 1)
            out(B - 1)


def one_hot_first_max(dve, link, values, best, rank, keys, out):
    shape = list(values.shape)
    link(dve.tensor_reduce(best, values, AXX, ALU.max))
    link(dve.tensor_tensor(out, values, best.unsqueeze(2).broadcast_to(shape), ALU.is_equal))
    link(dve.tensor_tensor(out, out, rank.unsqueeze(1).broadcast_to(shape), ALU.mult))
    link(dve.tensor_reduce(keys, out, AXX, ALU.max))
    link(dve.tensor_tensor(out, out, keys.unsqueeze(2).broadcast_to(shape), ALU.is_equal))


def phase_select(nc, A, ident, neg_half, x_all):
    N, R = 8, 8
    NR = N * R
    W1 = 2 * NR + N
    W2 = NR + N
    with ExitStack() as ctx:
        sb, bank, sem = tools(nc, ctx, "f0")
        w1, degen, w2 = sb("w1", [P, DT, W1]), sb("degen", [P, DT, NR]), sb("w2", [W2, D])
        md, db, dbT = sb("md", [N, D]), sb("db", [N, D]), sb("dbT", [P, DT, N])
        mdsq, md2, md2d = sb("mdsq", [N, D]), sb("md2", [N, 1]), sb("md2d", [N, N])
        own, ones = sb("own", [N, NR]), sb("ones", [N, P])
        own_sel, own_upd = sb("own_sel", [N, NR]), sb("own_upd", [N, NR])
        c_sel, c_upd, c_md2 = sb("c_sel", [P, NR]), sb("c_upd", [P, NR]), sb("c_md2", [P, N])
        slope, centre, rank = sb("slope", [P, N]), sb("centre", [P, N]), sb("rank", [P, N])
        xn, xn_all, xnT, y = sb("xn", [S, 2, D]), sb("xn_all", [S, B, D]), sb("xnT", [P, 2, DT * S]), sb("y", [S, B, W1])
        xx, sqx = sb("xx", [S, B]), sb("sqx", [S, D])
        z, score, nrm, gate = sb("z", [S, B, NR]), sb("score", [S, B, N]), sb("nrm", [S, B, N]), sb("gate", [S, B, N])
        gmax, keys, hot, rest = sb("gmax", [S, B]), sb("keys", [S, B]), sb("hot", [S, B, N]), sb("rest", [S, B])
        mix, mix2, mixT, upd = sb("mix", [S, B, W2]), sb("mix2", [S, 2, W2]), sb("mixT", [W2, 2, S]), sb("upd", [S, 2, D])
        tb, yb = [bank("t0"), bank("t1")], [bank("y0"), bank("y1")]
        cb, mb, ub = bank("c"), bank("m"), [bank("u0"), bank("u1")]
        loads, setup_p, setup_v, setup_t, pl, vl = (sem(n) for n in ("loads", "setup_p", "setup_v", "setup_t", "pl", "vl"))
        xn_ready, xnT_done, xnT_out, ys, y_out, sq_done = (sem(n) for n in (
            "xn_ready", "xnT_done", "xnT_out", "ys", "y_out", "sq_done"))
        arg_ready, exp_ready, mixT_done, mixT_out, upds, upd_out, x_done = (sem(n) for n in (
            "arg_ready", "exp_ready", "mixT_done", "mixT_out", "upds", "upd_out", "x_done"))
        block = ctx.enter_context(nc.Block())
        N_LOADS = 3 * N + 5
        xn_kept, mix_at = sem("xn_kept"), sem("mix_at")
        tnorm = AllTokensNorm(sb, sem, neg_half)

        @block.sync
        def _(sp):
            for i, name in enumerate(("select_weight", "lora_update")):
                for n in range(N):
                    sp.dma_start(w1[:, :, i * NR + n * R:i * NR + n * R + R],
                                 A[f"L0_ffn_{name}"][n].rearrange("(t p) r -> p t r", p=P)).then_inc(loads, 16)
            for n in range(N):
                sp.dma_start(degen[:, :, n * R:n * R + R], A["L0_ffn_lora_degen"][n].rearrange("(t p) r -> p t r", p=P)).then_inc(loads, 16)
            sp.dma_start(md[:, :], A["L0_ffn_select_mean_diff"]).then_inc(loads, 16)
            sp.dma_start(db[:, :], A["L0_ffn_debias_w"]).then_inc(loads, 16)
            sp.dma_start(w2[NR:W2, :], A["L0_ffn_bias_w"]).then_inc(loads, 16)
            sp.dma_start(slope[:, :], A["L0_ffn_imp_slope"].partition_broadcast(P)).then_inc(loads, 16)
            sp.dma_start(centre[:, :], A["L0_ffn_imp_center"].partition_broadcast(P)).then_inc(loads, 16)

        @block.gpsimd
        def _(pool):
            links = Links(pool, pl, 0)
            links(pool.memset(own[:, :], 1.0))
            links(pool.affine_select(out=own[:, :], in_=own[:, :], compare_op=ALU.is_ge, fill=0.0, base=0,
                                     pattern=[[1, NR]], channel_multiplier=-R))
            links(pool.affine_select(out=own[:, :], in_=own[:, :], compare_op=ALU.is_ge, fill=0.0, base=R - 1,
                                     pattern=[[-1, NR]], channel_multiplier=R))
            for n in range(N):
                pool.memset(rank[:, n:n + 1], float(N - n)).then_inc(setup_p, 1)
            pool.memset(ones[:, :], 1.0).then_inc(setup_p, 1)
            pool.wait_ge(setup_p, N + 1)

            tnorm.root_of(pool)
            with pool.Fori(0, B // 2) as i:
                for u in range(2):
                    b = i * 2 + u
                    pool.wait_ge(upd_out, b + 1)
                    pool.tensor_tensor(x_all[:, b, :], x_all[:, b, :], upd[:, u, :], ALU.add).then_inc(x_done, 1)
            pool.wait_ge(x_done, B)

        @block.scalar
        def _(act):
            act.wait_ge(setup_t, 1)
            act.activation(w2[0:NR, :], cb[0:NR, :], ACT.Copy).then_inc(setup_v, 1)

            with act.Fori(0, B // 2) as i:
                for u in range(2):
                    b = i * 2 + u
                    act.wait_ge(xnT_done, b + 1)
                    act.activation(xnT[:, u, :], tb[u][:, 0:DT * S], ACT.Copy).then_inc(xnT_out, 1)
                    act.wait_ge(xn_ready, b + 1)
                    act.activation(sqx[:, :], xn[:, u, :], ACT.Square, accum_out=xx[:, bass.ds(b, 1)]).then_inc(sq_done, 1)
                    act.wait_ge(sq_done, b + 1)
            act.wait_ge(arg_ready, 1)
            act.activation(gate[:, :, :], gate[:, :, :], ACT.Exp, scale=-1.0).then_inc(exp_ready, 1)
            with act.Fori(0, B // 2) as i:
                for u in range(2):
                    b = i * 2 + u
                    act.wait_ge(mixT_done, b + 1)
                    act.activation(mixT[:, u, :], tb[u][0:W2, 0:S], ACT.Copy).then_inc(mixT_out, 1)

        @block.tensor
        def _(pe):
            pe.wait_ge(loads, 16 * N_LOADS)
            for t in range(DT):
                ins = pe.transpose(cb[0:NR, t * P:(t + 1) * P], degen[:, t, :], ident[:, :])
            ins.then_inc(setup_t, 1)
            for t in range(DT):
                pe.transpose(mb[:, t * N:(t + 1) * N], md[:, t * P:(t + 1) * P], ident[0:N, 0:N])
            for t in range(DT):
                ins = pe.transpose(mb[:, (DT + t) * N:(DT + t + 1) * N], db[:, t * P:(t + 1) * P], ident[0:N, 0:N])
            ins.then_inc(setup_t, 1)
            pe.wait_ge(setup_v, 4)
            for t in range(DT):
                ins = pe.matmul(ub[0][0:N, 0:NR], w1[:, t, 2 * NR:W1], w1[:, t, 0:NR], start=t == 0, stop=t == DT - 1)
            ins.then_inc(setup_t, 1)
            for t in range(DT):
                ins = pe.matmul(ub[1][0:N, 0:NR], dbT[:, t, :], w1[:, t, NR:2 * NR], start=t == 0, stop=t == DT - 1)
            ins.then_inc(setup_t, 1)
            pe.wait_ge(setup_v, 7)
            pe.wait_ge(setup_p, N + 1)
            pe.matmul(cb[:, 0:NR], ones[:, :], own_sel[:, :], start=True, stop=True)
            pe.matmul(cb[:, NR:2 * NR], ones[:, :], own_upd[:, :], start=True, stop=True)
            pe.matmul(cb[:, 2 * NR:W1], ones[:, :], md2d[:, :], start=True, stop=True).then_inc(setup_t, 1)

            def transposes(b, u):
                pe.wait_ge(xn_ready, b + 1)
                for t in range(DT):
                    ins = pe.transpose(tb[u][:, t * S:(t + 1) * S], xn[:, u, t * P:(t + 1) * P], ident[0:S, 0:S])
                ins.then_inc(xnT_done, 1)

            def products(b, u):
                pe.wait_ge(xnT_out, b + 1)
                if not (isinstance(b, int) and b < 2):
                    pe.wait_ge(y_out, b - 1)
                for t in range(DT):
                    ins = pe.matmul(yb[u][0:S, 0:W1], xnT[:, u, t * S:(t + 1) * S], w1[:, t, :], start=t == 0, stop=t == DT - 1)
                ins.then_inc(ys, 1)

            def mix_transpose(b, u):
                pe.wait_ge(mix_at, b + 1)
                pe.transpose(tb[u][0:W2, 0:S], mix2[:, u, :], ident[0:S, 0:S]).then_inc(mixT_done, 1)

            def update(b, u):
                pe.wait_ge(mixT_out, b + 1)
                if not (isinstance(b, int) and b < 2):
                    pe.wait_ge(upd_out, b - 1)
                pe.matmul(ub[u][0:S, :], mixT[:, u, :], w2[:, :], start=True, stop=True).then_inc(upds, 1)

            for ahead, then in ((transposes, products), (mix_transpose, update)):
                ahead(0, 0)
                for b in (0, 1):
                    ahead(b + 1, 1 - b)
                    then(b, b)
                with pe.Fori(1, B // 2 - 1) as i:
                    for u in range(2):
                        ahead(i * 2 + u + 1, 1 - u)
                        then(i * 2 + u, u)
                ahead(B - 1, 1)
                then(B - 2, 0)
                then(B - 1, 1)

        @block.vector
        def _(dve):
            link = Links(dve, vl, 0)
            tnorm.statistics(dve, x_all)
            dve.wait_ge(setup_t, 2)
            dve.tensor_copy(w1[:, :, 2 * NR:W1], mb[:, 0:DT * N].rearrange("p (t n) -> p t n", t=DT)).then_inc(setup_v, 1)
            dve.tensor_copy(dbT[:, :, :], mb[:, DT * N:2 * DT * N].rearrange("p (t n) -> p t n", t=DT)).then_inc(setup_v, 1)
            link(dve.tensor_tensor(mdsq[:, :], md[:, :], md[:, :], ALU.mult))
            dve.tensor_reduce(md2[:, :], mdsq[:, :], AXX, ALU.add).then_inc(setup_v, 1)
            dve.wait_ge(setup_t, 4)
            dve.wait_ge(pl, 3)
            dve.wait_ge(setup_v, 4)
            dve.tensor_tensor(own_sel[:, :], ub[0][0:N, 0:NR], own[:, :], ALU.mult).then_inc(setup_v, 1)
            dve.tensor_tensor(own_upd[:, :], ub[1][0:N, 0:NR], own[:, :], ALU.mult).then_inc(setup_v, 1)
            dve.tensor_scalar(md2d[:, :], ident[0:N, 0:N], md2[:, :], None, ALU.mult).then_inc(setup_v, 1)
            dve.wait_ge(setup_t, 5)
            dve.wait_ge(setup_p, N + 1)
            link(dve.tensor_copy(c_sel[:, :], cb[:, 0:NR]))
            link(dve.tensor_copy(c_upd[:, :], cb[:, NR:2 * NR]))
            link(dve.tensor_copy(c_md2[:, :], cb[:, 2 * NR:W1]))

            def step(b, u, first, last):
                if not last:
                    if not (isinstance(b, int) and b < 2):
                        dve.wait_ge(sq_done, b - 1)
                    tnorm.apply(dve, b, x_all[:, b, :], xn[:, u, :]).then_inc(xn_ready, 1)
                    tnorm.apply(dve, b, x_all[:, b, :], xn_all[:, b, :]).then_inc(xn_kept, 1)
                if not first:
                    dve.wait_ge(ys, b - 1)
                    dve.tensor_scalar(y[:, b - 2, :], yb[u][0:S, 0:W1], 1.0, None, ALU.mult).then_inc(y_out, 1)

            dve.wait_ge(tnorm.roots, 1)
            step(0, 0, True, False)
            step(1, 1, True, False)
            with dve.Fori(1, B // 2) as i:
                for u in range(2):
                    step(i * 2 + u, u, False, False)
            step(B, 0, False, True)
            step(B + 1, 1, False, True)
            dve.wait_ge(xn_kept, B)
            dve.wait_ge(y_out, B)
            dve.wait_ge(sq_done, B)
            per_sel = [S, B, N]
            link(dve.tensor_tensor(z[:, :, :], y[:, :, 0:NR], c_sel[0:S, :].unsqueeze(1).broadcast_to([S, B, NR]), ALU.subtract))
            link(dve.tensor_tensor(z[:, :, :], z[:, :, :], z[:, :, :], ALU.mult))
            link(dve.tensor_reduce(score[:, :, :].rearrange("p b n -> p (b n)"), z[:, :, :].rearrange("p b (n r) -> p (b n) r", r=R), AXX, ALU.add))
            link(dve.tensor_scalar(nrm[:, :, :], y[:, :, 2 * NR:W1], -2.0, None, ALU.mult))
            link(dve.tensor_tensor(nrm[:, :, :], nrm[:, :, :], c_md2[0:S, :].unsqueeze(1).broadcast_to(per_sel), ALU.add))
            link(dve.tensor_tensor(nrm[:, :, :], nrm[:, :, :], xx[:, :].unsqueeze(2).broadcast_to(per_sel), ALU.add))
            link(dve.reciprocal(nrm[:, :, :], nrm[:, :, :]))
            link(dve.tensor_tensor(score[:, :, :], score[:, :, :], nrm[:, :, :], ALU.mult))
            link(dve.tensor_tensor(gate[:, :, :], score[:, :, :], centre[0:S, :].unsqueeze(1).broadcast_to(per_sel), ALU.subtract))
            link(dve.tensor_tensor(gate[:, :, :], gate[:, :, :], slope[0:S, :].unsqueeze(1).broadcast_to(per_sel), ALU.mult))
            dve.tensor_scalar(gate[:, :, :], gate[:, :, :], -87.0, None, ALU.max).then_inc(arg_ready, 1)
            dve.wait_ge(exp_ready, 1)
            link(dve.tensor_scalar(gate[:, :, :], gate[:, :, :], 1.0, None, ALU.add))
            link(dve.reciprocal(gate[:, :, :], gate[:, :, :]))
            one_hot_first_max(dve, link, gate[:, :, :], gmax[:, :], rank[0:S, :], keys[:, :], hot[:, :, :])
            link(dve.tensor_tensor(mix[:, :, NR:W2], hot[:, :, :], gmax[:, :].unsqueeze(2).broadcast_to(per_sel), ALU.mult))
            link(dve.tensor_tensor(z[:, :, :], y[:, :, NR:2 * NR], c_upd[0:S, :].unsqueeze(1).broadcast_to([S, B, NR]), ALU.subtract))
            link(dve.tensor_scalar(rest[:, :], gmax[:, :], -1.0, 1.0, ALU.mult, ALU.add))
            for n in range(N):
                ins = dve.tensor_tensor(mix[:, :, n * R:n * R + R], z[:, :, n * R:n * R + R],
                                        mix[:, :, NR + n:NR + n + 1].broadcast_to([S, B, R]), ALU.mult)
                link(ins)

            def hand_over(b, u):
                if not (isinstance(b, int) and b < 2):
                    dve.wait_ge(mixT_done, b - 1)
                dve.tensor_scalar(mix2[:, u, :], mix[:, b, :], 1.0, None, ALU.mult).then_inc(mix_at, 1)

            hand_over(0, 0)
            hand_over(1, 1)

            def update(b, u):
                dve.wait_ge(upds, b + 1)
                if not (isinstance(b, int) and b < 2):
                    dve.wait_ge(x_done, b - 1)
                dve.scalar_tensor_tensor(out=upd[:, u, :], in0=xn_all[:, b, :], scalar=rest[:, bass.ds(b, 1)], in1=ub[u][0:S, :],
                                         op0=ALU.mult, op1=ALU.add).then_inc(upd_out, 1)

            for b in (0, 1):
                hand_over(b + 2, b)
                update(b, b)
            with dve.Fori(1, B // 2 - 1) as i:
                for u in range(2):
                    hand_over(i * 2 + u + 2, u)
                    update(i * 2 + u, u)
            for b in (B - 2, B - 1):
                update(b, b % 2)


def phase_attention1(nc, A, ident, neg_half, x_all, part_dram):
    SCALE = float(HD1) ** -0.5
    HH, HALVES = H // 2, 2
    GH = HH // G
    W, WH = G * HD1, HH * HD1
    KE = KV + 1
    TP, TB = HH - 1, HH + 1
    with ExitStack() as ctx:
        sb, bank, sem = tools(nc, ctx, "a1")

        def split_sb(name, shape):
            return sb(f"{name}_hi", shape), sb(f"{name}_lo", shape)

        def loaded_sb(name, shape):
            with nc.sbuf_tensor(f"a1_{name}_loaded", shape, FP32) as loaded:
                pass
            lo = sb(f"{name}_lo", shape)
            return loaded, sb(f"{name}_hi", shape), lo

        (wq_rows, *wq), (wk_rows, *wk), (wo_rows, *wo) = loaded_sb("wq", [P, DT, WH]), loaded_sb("wk", [P, CT, WH]), loaded_sb("wo", [P, HH, D])
        wv = sb("wv", [P, CT, WH])
        gq, gk, g_col, eps = sb("gq", [P, 1]), sb("gk", [P, 1]), sb("g_col", [P, 1]), sb("eps", [P, G])
        ctxin, (tok_rows, *ctx_tok), ctxT = sb("ctxin", [KR, KT, C]), loaded_sb("ctx_tok", [KR, KT, C]), split_sb("ctxT", [P, CT, KV])
        xn, xnT = sb("xn", [S, D]), split_sb("xnT", [P, DT, S])
        squares = ctx.enter_context(nc.sbuf_tensor("a1_squares", [P, 2, W], mybir.dt.bfloat16))
        msq, root = sb("msq", [P, 2, G]), sb("root", [P, 2, G])
        kn = sb("kn", [P, 2, W])
        keysT, qT = split_sb("keysT", [P, HH, KE]), split_sb("qT", [P, HH, S])
        probs, probsT = sb("probs", [S, 4, KV]), split_sb("probsT", [KR, KT, G, S])
        nmax, sums, rsum = sb("nmax", [S, 4]), sb("sums", [S, 4]), sb("rsum", [S, 4])
        mixT, oT = sb("mixT", [P, CT, G * S]), split_sb("oT", [P, HH, S])
        part = sb("part", [S, D])

        proj, tbank = [bank("proj0"), bank("proj1")], bank("t")
        sbank, ptbank = [bank("s0"), bank("s1")], bank("pt")
        mbank = [bank("m0"), bank("m1")]

        w_in = [sem(f"w_in{i}") for i in range(2 * GH)]
        wv_in, wo_in, params, ctx_in, ctx_tok_in = (sem(n) for n in ("wv_in", "wo_in", "params", "ctx_in", "ctx_tok_in"))
        part_out, part_in, part_used = sem("part_out"), sem("part_in"), sem("part_used")
        w_hi, w_split, wo_hi, wo_split, ctx_hi, ctx_split = (sem(n) for n in (
            "w_hi", "w_split", "wo_hi", "wo_split", "ctx_hi", "ctx_split"))
        units, trs, scores, pts, mixes, heads_out, wos = (sem(n) for n in (
            "units", "trs", "scores", "pts", "mixes", "heads_out", "wos"))
        t_hi, t_out = sem("t_hi"), sem("t_out")
        ctx_T, ctxT_hi, ctxT_out = sem("ctx_T"), sem("ctxT_hi"), sem("ctxT_out")
        msqs, with_eps, roots, scaled = (sem(n) for n in ("msqs", "with_eps", "roots", "scaled"))
        maxes, exps, rsums, pnorms, pt_hi, pt_out = (sem(n) for n in ("maxes", "exps", "rsums", "pnorms", "pt_hi", "pt_out"))
        mix0_out, mix1_out, o_hi, o_out, x_done, xn_ready = (sem(n) for n in (
            "mix0_out", "mix1_out", "o_hi", "o_out", "x_done", "xn_ready"))
        constants, gcol_ready, vl = sem("constants"), sem("gcol_ready"), sem("vl")
        tnorm = AllTokensNorm(sb, sem, neg_half)
        block = ctx.enter_context(nc.Block())
        ctx_rows = A["ctx_1024"].rearrange("b (t p) c -> b p t c", p=KR)
        LAST = HALVES * B - 1

        def unit_rows(n):
            return S if n % G == 3 else KR

        def halves(eng, lead_in, step, lead_out):
            for f in range(HALVES):
                v0 = f * B
                lead_in(f, v0)
                step(f, v0, 0, True, False)
                with eng.Fori(v0 + 1, v0 + B - 1) as v:
                    step(f, v, v - v0, False, False)
                step(f, v0 + B - 1, B - 1, False, True)
                lead_out(f, v0 + B - 1)

        @block.sync
        def _(sp):
            def load_tokens(v, b):
                sp.dma_start(tok_rows[0:S, :, :], ctx_rows[b][0:S]).then_inc(ctx_tok_in, 16)
                sp.dma_start(tok_rows[S:KR, :, :], ctx_rows[b][S:KR]).then_inc(ctx_tok_in, 16)

            def lead_in(f, v0):
                if f:
                    sp.wait_ge(units, HH * v0)
                else:
                    sp.dma_start(ctxin[:, :, :], ctx_rows[0]).then_inc(ctx_in, 16)
                for g in range(GH):
                    cols, own = slice(f * WH + g * W, f * WH + (g + 1) * W), slice(g * W, (g + 1) * W)
                    sp.dma_start(wk_rows[:, :, own], A["L1_xattn_Wk"].rearrange("(t p) n -> p t n", p=P)[:, :, cols]).then_inc(w_in[2 * g], 16)
                    sp.dma_start(wq_rows[:, :, own], A["L1_xattn_Wq"].rearrange("(t p) n -> p t n", p=P)[:, :, cols]).then_inc(w_in[2 * g + 1], 16)
                if f:
                    sp.wait_ge(heads_out, GH * v0)
                else:
                    for name, t in (("gq", gq), ("gk", gk)):
                        sp.dma_start(t[:, :], A[f"L1_xattn_{name}"].rearrange("(n o) -> n o", o=1)).then_inc(params, 16)
                sp.dma_start(wv[:, :, :], A["L1_xattn_Wv"].rearrange("(t p) n -> p t n", p=P)[:, :, f * WH:(f + 1) * WH]).then_inc(wv_in, 16)
                if f:
                    sp.wait_ge(wos, v0)
                sp.dma_start(wo_rows[:, :, :], A["L1_xattn_Wo"].rearrange("(h p) n -> p h n", p=P)[:, f * HH:(f + 1) * HH, :]).then_inc(wo_in, 16)

            def step(f, v, b, first, last):
                if f:
                    if first:
                        sp.wait_ge(part_out, 16 * B + 16)
                    else:
                        sp.wait_ge(part_used, b)
                    sp.dma_start(part[:, :], part_dram[b]).then_inc(part_in, 16)
                if not (f and last):
                    sp.wait_ge(ctx_T, v * 2 + 2)
                    sp.dma_start(ctxin[:, :, :], ctx_rows[0 if last else b + 1]).then_inc(ctx_in, 16)
                if not (first and not f):
                    sp.wait_ge(mixes, v * GH)
                load_tokens(v, b)
                if not f and not first:
                    sp.wait_ge(x_done, v)
                    sp.dma_start(part_dram[b - 1], part[:, :]).then_inc(part_out, 16)

            def lead_out(f, v):
                if not f:
                    sp.wait_ge(x_done, B)
                    sp.dma_start(part_dram[B - 1], part[:, :]).then_inc(part_out, 16)

            halves(sp, lead_in, step, lead_out)

        @block.gpsimd
        def _(pool):
            pool.memset(eps[:, :], RMS_EPS).then_inc(constants, 1)
            pool.wait_ge(constants, 1)
            pool.memset(part[:, :], 0.0).then_inc(part_out, 16)

            def root_of(n, m):
                rows = unit_rows(n)
                pool.wait_ge(msqs, m + 1)
                pool.tensor_tensor(msq[0:rows, n % 2, :], msq[0:rows, n % 2, :], eps[0:rows, :], ALU.add).then_inc(with_eps, 1)
                pool.wait_ge(with_eps, m + 1)
                pool.tensor_tensor(root[0:rows, n % 2, :], msq[0:rows, n % 2, :], neg_half[0:rows, :].broadcast_to([rows, G]), ALU.pow).then_inc(roots, 1)

            def lead_in(f, v0):
                if not f:
                    tnorm.root_of(pool)
                for n in range(HH):
                    root_of(n, HH * v0 + n)

            def step(f, v, b, first, last):
                for n in range(HH):
                    if not last:
                        root_of(n, v * HH + HH + n)
                    if n == 2:
                        pool.wait_ge(ctx_hi, v + 1)
                        pool.tensor_tensor(ctx_tok[1][:, :, :].bitcast(FP32R), tok_rows[:, :, :], ctx_tok[0][:, :, :], ALU.subtract).then_inc(ctx_split, 1)
                    if n == 5 and f:
                        pool.wait_ge(part_in, b * 16 + 16)
                        pool.wait_ge(xn_ready, v + 1)
                        pool.tensor_tensor(x_all[:, b, :], x_all[:, b, :], part[:, :], ALU.add).then_inc(part_used, 1)

            halves(pool, lead_in, step, lambda f, v: None)

        @block.scalar
        def _(act):
            def square(n, m):
                rows = unit_rows(n)
                act.wait_ge(units, m + 1)
                for j in range(G):
                    cols = slice(j * HD1, (j + 1) * HD1)
                    ins = act.activation(squares[0:rows, n % 2, cols], proj[n % 2][0:rows, cols], ACT.Square, scale=SCALE,
                                         accum_out=msq[0:rows, n % 2, j:j + 1])
                ins.then_inc(msqs, 1)

            def take(out, src, use, scale=1.0):
                act.wait_ge(trs, use + 1)
                act.activation(out.bitcast(FP32R), src, ACT.Copy, scale=scale).then_inc(t_hi, 1)

            def exp(h, n):
                act.wait_ge(maxes, n + 1)
                act.activation(probs[:, h % 4, :], sbank[h % 2][0:S, 0:KV], ACT.Exp, bias=nmax[:, h % 4:h % 4 + 1],
                               accum_out=sums[:, h % 4:h % 4 + 1]).then_inc(exps, 1)

            def probs_hi(h, n):
                act.wait_ge(pts, n + 1)
                act.activation(probsT[0][:, :, h % G, :].bitcast(FP32R), ptbank[0:KR, 0:KT * S].rearrange("p (t s) -> p t s", t=KT),
                               ACT.Copy).then_inc(pt_hi, 1)

            def mix1(m):
                act.wait_ge(mixes, m + 1)
                act.activation(mixT[:, 1, :], mbank[1][:, 0:G * S], ACT.Copy).then_inc(mix1_out, 1)

            def heads_hi(g, m):
                act.wait_ge(heads_out, m + 1)
                act.activation(oT[0][:, g * G:g * G + G, :].bitcast(FP32R), mbank[0][:, 0:G * S].rearrange("p (h s) -> p h s", h=G),
                               ACT.Copy).then_inc(o_hi, 1)

            def weights_hi(f, g):
                for i, (loaded, w) in enumerate(((wk_rows, wk), (wq_rows, wq))):
                    act.wait_ge(w_in[2 * g + i], 16 * f + 16)
                    act.activation(w[0][:, :, g * W:(g + 1) * W].bitcast(FP32R), loaded[:, :, g * W:(g + 1) * W], ACT.Copy).then_inc(w_hi, 1)

            def lead_in(f, v0):
                use = TB * v0
                weights_hi(f, 0)
                context_hi(v0)
                take(*tokens(), use)
                act.wait_ge(gcol_ready, 1)
                for n in range(HH):
                    if n == 2:
                        weights_hi(f, 1)
                    square(n, HH * v0 + n)
                    if n >= 2:
                        take(*unit_part(n - 2), use + n - 1, unit_scale(n - 2))
                exp(0, HH * v0)

            def context_hi(v):
                for c in range(CT):
                    act.wait_ge(ctx_T, v * 2 + c + 1)
                    act.activation(ctxT[0][:, c, :].bitcast(FP32R), mbank[c][:, 0:KV], ACT.Copy).then_inc(ctxT_hi, 1)

            def tokens():
                return xnT[0][:, :, :], tbank[:, 0:DT * S].rearrange("p (t s) -> p t s", t=DT)

            def unit_part(n):
                return unit_out(0, n)

            def unit_scale(n):
                return g_col[:, :] if n % G == 3 else 1.0

            def unit_out(part_, n):
                g, t = n // G, n % G
                if t == 3:
                    return qT[part_][:, g * G:g * G + G, :], tbank[:, 0:G * S].rearrange("p (h s) -> p h s", h=G)
                return keysT[part_][:, g * G:g * G + G, t * KR:(t + 1) * KR], tbank[:, 0:G * KR].rearrange("p (h s) -> p h s", h=G)

            def step(f, v, b, first, last):
                use = TP + TB * v
                for h in range(HH):
                    n = v * HH + h
                    if h == 0 and not last:
                        context_hi(v + 1)
                    if h == 0:
                        take(*unit_part(HH - 2), use)
                    elif h > 1 and not last:
                        take(*unit_part(h - 2), use + (2 if h == 2 else h + 1), unit_scale(h - 2))
                    if h % G != 1 and (h or not first):
                        probs_hi((h - 1) % HH, n - 1)
                    if h < HH - 1 or not last:
                        if not (first and not f and h < 3):
                            act.wait_ge(pts, n - 2)
                        exp((h + 1) % HH, n + 1)
                    if h == 1:
                        if not last:
                            square(0, v * HH + HH)
                        take(*unit_part(HH - 1), use + 1, unit_scale(HH - 1))
                    if h % G == 1:
                        if f or not first or h > 1:
                            act.wait_ge(mixes, v * GH + h // G)
                        probs_hi((h - 1) % HH, n - 1)
                    if h == 1 and not first:
                        mix1(v * GH - 1)
                    if h == 2 and not first:
                        heads_hi(GH - 1, v * GH - 1)
                    if h == 3:
                        act.wait_ge(ctx_tok_in, v * 32 + 32)
                        act.activation(ctx_tok[0][:, :, :].bitcast(FP32R), tok_rows[:, :, :], ACT.Copy).then_inc(ctx_hi, 1)
                    if h >= 5 and h % G == 1:
                        mix1(v * GH + h // G - 1)
                    if h >= 6 and h % G == 2:
                        heads_hi(h // G - 1, v * GH + h // G - 1)
                    if h == 4 and first:
                        act.wait_ge(wo_in, 16 * f + 16)
                        act.activation(wo[0][:, :, :].bitcast(FP32R), wo_rows[:, :, :], ACT.Copy).then_inc(wo_hi, 1)
                    if not last and h:
                        if h == 2:
                            take(*tokens(), use + 3)
                        square(h, n + HH)

            def lead_out(f, v):
                probs_hi(HH - 1, v * HH + HH - 1)
                mix1(v * GH + GH - 1)
                heads_hi(GH - 1, v * GH + GH - 1)

            halves(act, lead_in, step, lead_out)

        @block.vector
        def _(dve):
            link = Links(dve, vl, 0)
            tnorm.statistics(dve, x_all)
            for t in keysT:
                dve.wait_ge(constants, 1)
                dve.tensor_scalar(t[:, :, KV:KE].bitcast(FP32R), eps[:, 0:1].unsqueeze(1).broadcast_to([P, HH, 1]), 0.0, None, ALU.mult)
            dve.wait_ge(params, 32)
            link(dve.tensor_tensor(g_col[:, :], gq[:, :], gk[:, :], ALU.mult))
            dve.tensor_scalar(g_col[:, :], g_col[:, :], SCALE, None, ALU.mult).then_inc(gcol_ready, 1)
            dve.wait_ge(gcol_ready, 1)

            def scale(n, m, wait):
                rows = unit_rows(n)
                dve.wait_ge(roots, m + 1)
                if wait is not None:
                    dve.wait_ge(trs, wait)
                dve.tensor_tensor(kn[0:rows, n % 2, :].rearrange("p (h d) -> p h d", h=G),
                                  proj[n % 2][0:rows, :].rearrange("p (h d) -> p h d", h=G),
                                  root[0:rows, n % 2, :].unsqueeze(2).broadcast_to([rows, G, HD1]), ALU.mult).then_inc(scaled, 1)

            def rest(pair, src, use):
                dve.wait_ge(t_hi, use + 1)
                dve.tensor_tensor(pair[1].bitcast(FP32R), src, pair[0], ALU.subtract).then_inc(t_out, 1)

            def context_lo(v):
                for c in range(CT):
                    dve.wait_ge(ctxT_hi, v * 2 + c + 1)
                    dve.tensor_tensor(ctxT[1][:, c, :].bitcast(FP32R), mbank[c][:, 0:KV], ctxT[0][:, c, :], ALU.subtract).then_inc(ctxT_out, 1)

            def tokens_lo(use):
                rest([t[:, :, :] for t in xnT], tbank[:, 0:DT * S].rearrange("p (t s) -> p t s", t=DT), use)

            def unit_lo(n, use):
                g, t = n // G, n % G
                if t < 3:
                    rest([k[:, g * G:g * G + G, t * KR:(t + 1) * KR] for k in keysT],
                         tbank[:, 0:G * KR].rearrange("p (h s) -> p h s", h=G), use)
                else:
                    dve.wait_ge(t_hi, use + 1)
                    dve.scalar_tensor_tensor(out=qT[1][:, g * G:g * G + G, :].bitcast(FP32R), in0=tbank[:, 0:G * S].rearrange("p (h s) -> p h s", h=G),
                                             scalar=g_col[:, :], in1=qT[0][:, g * G:g * G + G, :], op0=ALU.mult, op1=ALU.subtract).then_inc(t_out, 1)

            def max_(h, n):
                dve.wait_ge(scores, n + 1)
                dve.tensor_reduce(nmax[:, h % 4:h % 4 + 1], sbank[h % 2][0:S, 0:KV], AXX, ALU.max, negate=True).then_inc(maxes, 1)

            def probs_lo(h, n):
                dve.wait_ge(pt_hi, n + 1)
                dve.tensor_tensor(probsT[1][:, :, h % G, :].bitcast(FP32R), ptbank[0:KR, 0:KT * S].rearrange("p (t s) -> p t s", t=KT),
                                  probsT[0][:, :, h % G, :], ALU.subtract).then_inc(pt_out, 1)

            def mix0(m):
                dve.wait_ge(mixes, m + 1)
                dve.tensor_copy(mixT[:, 0, :], mbank[0][:, 0:G * S]).then_inc(mix0_out, 1)

            def heads_lo(g, m):
                dve.wait_ge(o_hi, m + 1)
                dve.tensor_tensor(oT[1][:, g * G:g * G + G, :].bitcast(FP32R), mbank[0][:, 0:G * S].rearrange("p (h s) -> p h s", h=G),
                                  oT[0][:, g * G:g * G + G, :], ALU.subtract).then_inc(o_out, 1)

            def x_out(f, v, b):
                dve.wait_ge(wos, v + 1)
                if f:
                    dve.wait_ge(part_used, b + 1)
                    dve.tensor_tensor(x_all[:, b, :], mbank[1][0:S, :], x_all[:, b, :], ALU.add).then_inc(x_done, 1)
                else:
                    dve.wait_ge(part_out, b * 16 + 16)
                    dve.tensor_copy(part[:, :], mbank[1][0:S, :]).then_inc(x_done, 1)

            def weights_lo(f, g):
                for i, (loaded, w) in enumerate(((wk_rows, wk), (wq_rows, wq))):
                    dve.wait_ge(w_hi, 2 * GH * f + 2 * g + i + 1)
                    dve.tensor_tensor(w[1][:, :, g * W:(g + 1) * W].bitcast(FP32R), loaded[:, :, g * W:(g + 1) * W], w[0][:, :, g * W:(g + 1) * W],
                                      ALU.subtract).then_inc(w_split, 1)

            def lead_in(f, v0):
                use = TB * v0
                if not f:
                    dve.wait_ge(tnorm.roots, 1)
                tnorm.apply(dve, 0, x_all[:, 0, :], xn[:, :]).then_inc(xn_ready, 1)
                weights_lo(f, 0)
                context_lo(v0)
                tokens_lo(use)
                for n in range(HH):
                    if n == 2:
                        weights_lo(f, 1)
                    if n >= 1:
                        scale(n - 1, HH * v0 + n - 1, use + n - 1 if n >= 3 else None)
                    if n >= 2:
                        unit_lo(n - 2, use + n - 1)
                max_(0, HH * v0)

            def step(f, v, b, first, last):
                use = TP + TB * v
                for h in range(HH):
                    n = v * HH + h
                    if h == 0 and not last:
                        context_lo(v + 1)
                    if h < HH - 1 or not last:
                        max_((h + 1) % HH, n + 1)
                    dve.wait_ge(exps, n + 1)
                    dve.reciprocal(rsum[:, h % 4:h % 4 + 1], sums[:, h % 4:h % 4 + 1]).then_inc(rsums, 1)
                    dve.wait_ge(rsums, n + 1)
                    dve.tensor_scalar(probs[:, h % 4, :], probs[:, h % 4, :], rsum[:, h % 4:h % 4 + 1], None, ALU.mult).then_inc(pnorms, 1)
                    if h == 0:
                        scale(HH - 1, v * HH + HH - 1, use)
                    if h == 5 and not first:
                        x_out(f, v - 1, b - 1)
                    if h < 2:
                        unit_lo(HH - 2 + h, use + h)
                    elif not last:
                        unit_lo(h - 2, use + (2 if h == 2 else h + 1))
                    if h or not first:
                        probs_lo((h - 1) % HH, n - 1)
                    if h == 1 and not last:
                        tnorm.apply(dve, b + 1, x_all[:, b + 1, :], xn[:, :]).then_inc(xn_ready, 1)
                    if not last and h >= 1:
                        scale(h - 1, n + HH - 1, use + (h if h < 3 else 3 if h == 3 else h + 1))
                    if not first:
                        if h == 1:
                            mix0(v * GH - 1)
                        if h == 2:
                            heads_lo(GH - 1, v * GH - 1)
                    if not last and h == 2:
                        tokens_lo(use + 3)
                    if h >= 5 and h % G == 1:
                        mix0(v * GH + h // G - 1)
                    if h >= 6 and h % G == 2:
                        heads_lo(h // G - 1, v * GH + h // G - 1)
                    if h == 4 and first:
                        dve.wait_ge(wo_hi, f + 1)
                        dve.tensor_tensor(wo[1][:, :, :].bitcast(FP32R), wo_rows[:, :, :], wo[0][:, :, :], ALU.subtract).then_inc(wo_split, 1)

            def lead_out(f, v):
                probs_lo(HH - 1, v * HH + HH - 1)
                mix0(v * GH + GH - 1)
                heads_lo(GH - 1, v * GH + GH - 1)
                x_out(f, v, B - 1)

            halves(dve, lead_in, step, lead_out)
            dve.wait_ge(x_done, LAST + 1)

        @block.tensor
        def _(pe):
            def product(out, pairs):
                parts = [(a[i].bitcast(FP32R), b[j].bitcast(FP32R)) for a, b in pairs for i, j in ((0, 0), (0, 1), (1, 0))]
                for k, (a, b) in enumerate(parts):
                    ins = pe.matmul(out, a, b, start=k == 0, stop=k == len(parts) - 1)
                return ins

            def bank_free(use):
                if not (isinstance(use, int) and use == 0):
                    pe.wait_ge(t_out, use)

            def context(v, contents):
                pe.wait_ge(ctx_in, v * 16 + 16)
                for c, (signal, count) in enumerate(contents):
                    if count is not None:
                        pe.wait_ge(signal, count)
                    for t in range(KT):
                        ins = pe.transpose(mbank[c][:, t * KR:(t + 1) * KR], ctxin[:, t, c * P:(c + 1) * P], ident[0:KR, 0:KR])
                    ins.then_inc(ctx_T, 1)

            def tokens(use):
                bank_free(use)
                for t in range(DT):
                    ins = pe.transpose(tbank[:, t * S:(t + 1) * S], xn[:, t * P:(t + 1) * P], ident[0:S, 0:S])
                ins.then_inc(trs, 1)

            def unit(n, m):
                g, t = n // G, n % G
                cols = slice(g * W, (g + 1) * W)
                if not (isinstance(m, int) and m < 2):
                    pe.wait_ge(scaled, m - 1)
                if t == 3:
                    pairs = [([x[:, k, :] for x in xnT], [w[:, k, cols] for w in wq]) for k in range(DT)]
                else:
                    pairs = [([c[:, k, t * KR:(t + 1) * KR] for c in ctxT], [w[:, k, cols] for w in wk]) for k in range(CT)]
                product(proj[n % 2][0:unit_rows(n), :], pairs).then_inc(units, 1)

            def unit_T(n, m, use):
                rows = unit_rows(n)
                pe.wait_ge(scaled, m + 1)
                bank_free(use)
                for j in range(G):
                    ins = pe.transpose(tbank[:, j * rows:(j + 1) * rows], kn[0:rows, n % 2, j * P:(j + 1) * P], ident[0:rows, 0:rows])
                ins.then_inc(trs, 1)

            def score(h, n, v):
                if not (isinstance(n, int) and n < 2):
                    pe.wait_ge(exps, n - 1)
                if h % G == 0:
                    c = h // G
                    pe.wait_ge(t_out, TP - TB + TB * v + G * c + 7 if c < GH - 1 else TP + TB * v + 2)
                product(sbank[h % 2][0:S, 0:KE], [([q[:, h, :] for q in qT], [k[:, h, :] for k in keysT])]).then_inc(scores, 1)

            def pt(h, n, v):
                pe.wait_ge(pnorms, n + 1)
                if not (isinstance(n, int) and n == 0):
                    pe.wait_ge(pt_out, n)
                for t in range(KT):
                    ins = pe.transpose(ptbank[0:KR, t * S:(t + 1) * S], probs[:, h % 4, t * KR:(t + 1) * KR], ident[0:S, 0:S])
                ins.then_inc(pts, 1)

            def mix(g, v):
                m = v * GH + g
                pe.wait_ge(pt_out, v * HH + G * g + G)
                if not (isinstance(m, int) and m == 0):
                    pe.wait_ge(o_out, m)
                    pe.wait_ge(mix1_out, m)
                if g == 0:
                    pe.wait_ge(ctx_split, v + 1)
                for c in range(CT):
                    if c and g == 0 and not (isinstance(v, int) and v == 0):
                        pe.wait_ge(x_done, v)
                    ins = product(mbank[c][:, 0:G * S], [([x[:, t, c * P:(c + 1) * P] for x in ctx_tok],
                                                         [p[:, t, :, :].rearrange("p g s -> p (g s)") for p in probsT]) for t in range(KT)])
                ins.then_inc(mixes, 1)

            def head_values(g, v):
                m = v * GH + g
                pe.wait_ge(mix0_out, m + 1)
                pe.wait_ge(mix1_out, m + 1)
                for j in range(G):
                    h = g * G + j
                    for c in range(CT):
                        ins = pe.matmul(mbank[0][:, j * S:(j + 1) * S], wv[:, c, h * HD1:(h + 1) * HD1],
                                        mixT[:, c, j * S:(j + 1) * S], start=c == 0, stop=c == CT - 1)
                ins.then_inc(heads_out, 1)

            def out(v):
                pe.wait_ge(o_out, v * GH + GH)
                product(mbank[1][0:S, :], [([o[:, h, :] for o in oT], [w[:, h, :] for w in wo]) for h in range(HH)]).then_inc(wos, 1)

            def lead_in(f, v0):
                use = TB * v0
                context(v0, ((o_out, GH * v0), (x_done, v0)) if f else ((None, None), (None, None)))
                pe.wait_ge(xn_ready, v0 + 1)
                tokens(use)
                pe.wait_ge(w_split, 2 * GH * f + 2)
                pe.wait_ge(ctxT_out, 2 * v0 + 2)
                pe.wait_ge(t_out, use + 1)
                for n in range(HH):
                    if n == G:
                        pe.wait_ge(w_split, 2 * GH * f + 4)
                    unit(n, HH * v0 + n)
                    if n >= 2:
                        unit_T(n - 2, HH * v0 + n - 2, use + n - 1)
                score(0, HH * v0, v0)
                pe.wait_ge(wv_in, 16 * f + 16)

            def step(f, v, b, first, last):
                use = TP + TB * v
                if not first:
                    pe.wait_ge(wo_split, f + 1)
                for h in range(HH):
                    n = v * HH + h
                    if h == 0 and not last:
                        if first:
                            context(v + 1, ((ctxT_out, 2 * v + 1), (ctxT_out, 2 * v + 2)))
                        else:
                            context(v + 1, ((o_out, v * GH - 1), (mix1_out, v * GH - 1)))
                    if h < HH - 1:
                        score(h + 1, n + 1, v)
                    elif not last:
                        score(0, n + 1, v + 1)
                    if h == 1 and not last:
                        pe.wait_ge(ctxT_out, v * 2 + 4)
                        unit(0, v * HH + HH)
                    if h < 2:
                        unit_T(HH - 2 + h, v * HH + HH - 2 + h, use + h)
                    elif not last:
                        unit_T(h - 2, n + HH - 2, use + (2 if h == 2 else h + 1))
                    if h or not first:
                        pt((h - 1) % HH, n - 1, v)
                    if not first:
                        if h == 1:
                            mix(GH - 1, v - 1)
                        if h == 2:
                            head_values(GH - 1, v - 1)
                        if h == 3:
                            out(v - 1)
                    if h >= 5 and h % G == 1:
                        mix(h // G - 1, v)
                    if h >= 6 and h % G == 2:
                        head_values(h // G - 1, v)
                    if not last and h:
                        if h == 2:
                            pe.wait_ge(xn_ready, v + 2)
                            tokens(use + 3)
                        if h == 3:
                            pe.wait_ge(t_out, use + 4)
                        unit(h, n + HH)

            def lead_out(f, v):
                pt(HH - 1, v * HH + HH - 1, v)
                mix(GH - 1, v)
                head_values(GH - 1, v)
                out(v)

            halves(pe, lead_in, step, lead_out)


def phase_experts(nc, A, ident, neg_half, x_all, out):
    E, R, F = 8, 8, A["L1_ffn_W_gate"].shape[1]
    L = (E + 1) * R
    FC = -(-F // P)
    FR = F - (FC - 1) * P
    SG = 4
    T, J = SG * S, B // SG
    with ExitStack() as ctx:
        sb, bank, sem = tools(nc, ctx, "f1")
        w_gate, w_up, w_down = sb("w_gate", [P, DT, F]), sb("w_up", [P, DT, F]), sb("w_down", [P, FC, D])
        a_gate, a_up, a_down = sb("a_gate", [P, DT, L]), sb("a_up", [P, DT, L]), sb("a_down", [P, FC, L])
        b_gate, b_up, b_down = sb("b_gate", [L, F]), sb("b_up", [L, F]), sb("b_down", [L, D])
        w_router, bias, rank = sb("w_router", [P, DT, E]), sb("bias", [P, E]), sb("rank", [P, E])
        xn, xs, xnT = sb("xn", [S, 2, D]), sb("xs", [P, 2, DT * S]), sb("xnT", [P, DT, B * S])
        score, biased = sb("score", [S, B, E]), sb("biased", [S, B, E])
        hot, hot2, best, keys = sb("hot", [S, B, E]), sb("hot2", [S, B, E]), sb("best", [S, B]), sb("keys", [S, B])
        wexp, wexp2, wexpT = sb("wexp", [S, B, L]), sb("wexp2", [S, 2, L]), sb("wexpT", [L, B * S])
        ug, uu, vT = sb("ug", [L, B * S]), sb("uu", [L, B * S]), sb("vT", [L, T])
        sg, hT = sb("sg", [P, 2, T]), sb("hT", [P, FC, T])
        gb, upb = [bank("g0"), bank("g1")], [bank("u0"), bank("u1")]
        tb, ob = [bank("t0"), bank("t1")], [bank("o0"), bank("o1")]
        lb, mb = ob, gb[0]

        l_router, l_small, l_gate, l_down = sem("l_router"), sem("l_small"), sem("l_gate"), sem("l_down")
        rank_set, vl = sem("rank_set"), sem("vl")
        tnorm = AllTokensNorm(sb, sem, neg_half)
        xn_ready, xT_done, xs_out, xnT_out, logits, logits_out = (sem(n) for n in (
            "xn_ready", "xT_done", "xs_out", "xnT_out", "logits", "logits_out"))
        w_at, wT_done, wT_out, uls, us_out = (sem(n) for n in (
            "w_at", "wT_done", "wT_out", "uls", "us_out"))
        gates, ups, sigs, gs_done, h_ready, vs, v_ready, outs, res_done = (sem(n) for n in (
            "gates", "ups", "sigs", "gs_done", "h_ready", "vs", "v_ready", "outs", "res_done"))
        stored = sem("stored")
        block = ctx.enter_context(nc.Block())
        N_SMALL = 1 + 2 * (E + 3) + 2 * (E + 1) + 2

        @block.sync
        def _(sp):
            def rows(name):
                return A[f"L1_ffn_{name}"]

            sp.dma_start(w_router[:, :, :], rows("W_router").rearrange("(t p) e -> p t e", p=P)).then_inc(l_router, 16)
            sp.dma_start(bias[:, :], rows("expert_bias").partition_broadcast(P)).then_inc(l_small, 16)
            for kind, a, b_ in (("gate", a_gate, b_gate), ("up", a_up, b_up)):
                for e in range(E):
                    sp.dma_start(a[:, :, e * R:(e + 1) * R], rows(f"A_{kind}")[e].rearrange("(t p) r -> p t r", p=P)).then_inc(l_small, 16)
                sp.dma_start(a[:, :, E * R:L], rows(f"sA_{kind}").rearrange("(t p) r -> p t r", p=P)).then_inc(l_small, 16)
                sp.dma_start(b_[0:E * R, :], rows(f"B_{kind}").rearrange("e r f -> (e r) f")).then_inc(l_small, 16)
                sp.dma_start(b_[E * R:L, :], rows(f"sB_{kind}")).then_inc(l_small, 16)
            sp.dma_start(w_gate[:, :, :], rows("W_gate").rearrange("(t p) f -> p t f", p=P)).then_inc(l_gate, 16)
            sp.dma_start(w_up[:, :, :], rows("W_up").rearrange("(t p) f -> p t f", p=P)).then_inc(l_gate, 16)
            full = (FC - 1) * P
            for e in range(E + 1):
                src = rows("A_down")[e] if e < E else rows("sA_down")
                sp.dma_start(a_down[:, 0:FC - 1, e * R:(e + 1) * R], src[0:full, :].rearrange("(c p) r -> p c r", p=P)).then_inc(l_small, 16)
                sp.dma_start(a_down[0:FR, FC - 1, e * R:(e + 1) * R], src[full:F, :]).then_inc(l_small, 16)
            sp.dma_start(b_down[0:E * R, :], rows("B_down").rearrange("e r d -> (e r) d")).then_inc(l_small, 16)
            sp.dma_start(b_down[E * R:L, :], rows("sB_down")).then_inc(l_small, 16)
            sp.dma_start(w_down[:, 0:FC - 1, :], rows("W_down")[0:full, :].rearrange("(c p) d -> p c d", p=P)).then_inc(l_down, 16)
            sp.dma_start(w_down[0:FR, FC - 1, :], rows("W_down")[full:F, :]).then_inc(l_down, 16)
            with sp.Fori(0, J) as j:
                for i in range(SG):
                    sp.wait_ge(res_done, j * SG + i + 1)
                    sp.dma_start(out[j * SG + i], x_all[:, j * SG + i, :]).then_inc(stored, 16)
            sp.wait_ge(stored, 16 * B)

        @block.gpsimd
        def _(pool):
            for e in range(E):
                pool.memset(rank[:, e:e + 1], float(E - e)).then_inc(rank_set, 1)
            pool.memset(wexp[:, :, E * R:L], 1.0 / R).then_inc(rank_set, 1)

            tnorm.root_of(pool)

        @block.scalar
        def _(act):

            def step(b, u):
                act.wait_ge(xT_done, b + 1)
                if not (isinstance(b, int) and b < 2):
                    act.wait_ge(xnT_out, b - 1)
                act.activation(xs[:, u, :], tb[u][:, 0:DT * S], ACT.Copy).then_inc(xs_out, 1)
                act.wait_ge(logits, b + 1)
                act.activation(score[:, b, :], lb[u][0:S, 0:E], ACT.Sigmoid).then_inc(logits_out, 1)

            for b in (0, 1):
                step(b, b)
            with act.Fori(1, B // 2) as i:
                for u in range(2):
                    step(i * 2 + u, u)
            with act.Fori(0, J) as j:
                act.wait_ge(wT_done, j * SG + SG)
                act.activation(wexpT[:, bass.ds(j * T, T)], mb[0:L, 0:T], ACT.Copy).then_inc(wT_out, 1)
            with act.Fori(0, J) as j:
                for c in range(FC):
                    rows = P if c < FC - 1 else FR
                    act.wait_ge(gates, j * FC + c + 1)
                    act.activation(sg[0:rows, c % 2, :], gb[c % 2][0:rows, 0:T], ACT.Sigmoid).then_inc(sigs, 1)

        @block.tensor
        def _(pe):
            pe.wait_ge(l_router, 16)

            def transposes(b, u):
                pe.wait_ge(xn_ready, b + 1)
                for t in range(DT):
                    ins = pe.transpose(tb[u][:, t * S:(t + 1) * S], xn[:, u, t * P:(t + 1) * P], ident[0:S, 0:S])
                ins.then_inc(xT_done, 1)

            def router(b, u):
                pe.wait_ge(xs_out, b + 1)
                if not (isinstance(b, int) and b < 2):
                    pe.wait_ge(logits_out, b - 1)
                for t in range(DT):
                    ins = pe.matmul(lb[u][0:S, 0:E], xs[:, u, t * S:(t + 1) * S], w_router[:, t, :], start=t == 0, stop=t == DT - 1)
                ins.then_inc(logits, 1)

            transposes(0, 0)
            for b in (0, 1):
                transposes(b + 1, 1 - b)
                router(b, b)
            with pe.Fori(1, B // 2 - 1) as i:
                for u in range(2):
                    transposes(i * 2 + u + 1, 1 - u)
                    router(i * 2 + u, u)
            transposes(B - 1, 1)
            router(B - 2, 0)
            router(B - 1, 1)

            def weights_T(j, first):
                for i in range(SG):
                    pe.wait_ge(w_at, j * SG + i + 1)
                    if i == 0 and not first:
                        pe.wait_ge(wT_out, j)
                    ins = pe.transpose(mb[0:L, i * S:(i + 1) * S], wexp2[:, i % 2, :], ident[0:S, 0:S])
                    ins.then_inc(wT_done, 1)

            weights_T(0, True)
            with pe.Fori(1, J) as j:
                weights_T(j, False)
            pe.wait_ge(l_small, 16 * N_SMALL)

            def lora_in(j, first):
                for k, a in enumerate((a_gate, a_up)):
                    if not first:
                        pe.wait_ge(us_out, j * 2 + k - 1)
                    for t in range(DT):
                        ins = pe.matmul(tb[k][0:L, 0:T], a[:, t, :], xnT[:, t, bass.ds(j * T, T)], start=t == 0, stop=t == DT - 1)
                    ins.then_inc(uls, 1)

            pe.wait_ge(xnT_out, B)
            lora_in(0, True)
            with pe.Fori(1, J) as j:
                lora_in(j, False)
            pe.wait_ge(l_gate, 32)
            pe.wait_ge(us_out, 2 * J)

            def one_pass(j, first):
                for c in range(FC):
                    rows = P if c < FC - 1 else FR
                    if c >= 2:
                        pe.wait_ge(h_ready, j * FC + c - 1)
                    elif c == 0 and not first:
                        pe.wait_ge(h_ready, j * FC)
                    for dst, w, b_, u_, done in ((gb, w_gate, b_gate, ug, gates), (upb, w_up, b_up, uu, ups)):
                        for t in range(DT):
                            pe.matmul(dst[c % 2][0:rows, 0:T], w[:, t, c * P:c * P + rows], xnT[:, t, bass.ds(j * T, T)], start=t == 0, stop=False)
                        pe.matmul(dst[c % 2][0:rows, 0:T], b_[:, c * P:c * P + rows], u_[:, bass.ds(j * T, T)], start=False, stop=True).then_inc(done, 1)
                if first:
                    pe.wait_ge(l_down, 32)
                pe.wait_ge(h_ready, j * FC + FC)
                for c in range(FC):
                    rows = P if c < FC - 1 else FR
                    ins = pe.matmul(tb[0][0:L, 0:T], a_down[0:rows, c, :], hT[0:rows, c, :], start=c == 0, stop=c == FC - 1)
                ins.then_inc(vs, 1)
                for i in range(SG):
                    if i >= 2:
                        pe.wait_ge(res_done, j * SG + i - 1)
                    for c in range(FC):
                        rows = P if c < FC - 1 else FR
                        pe.matmul(ob[i % 2][0:S, :], hT[0:rows, c, i * S:(i + 1) * S], w_down[0:rows, c, :], start=c == 0, stop=False)
                    if i == 0:
                        pe.wait_ge(v_ready, j + 1)
                    pe.matmul(ob[i % 2][0:S, :], vT[:, i * S:(i + 1) * S], b_down[:, :], start=False, stop=True).then_inc(outs, 1)

            one_pass(0, True)
            with pe.Fori(1, J) as j:
                one_pass(j, False)

        @block.vector
        def _(dve):
            link = Links(dve, vl, 0)

            def step(b, u, first, last):
                if not last:
                    tnorm.apply(dve, b, x_all[:, b, :], xn[:, u, :]).then_inc(xn_ready, 1)
                if not first:
                    dve.wait_ge(xs_out, b)
                    dve.tensor_scalar(xnT[:, :, bass.ds((b - 1) * S, S)], xs[:, 1 - u, :].rearrange("p (t s) -> p t s", t=DT), 1.0, None, ALU.mult).then_inc(xnT_out, 1)

            tnorm.statistics(dve, x_all)
            dve.wait_ge(tnorm.roots, 1)
            step(0, 0, True, False)
            step(1, 1, False, False)
            with dve.Fori(1, B // 2) as i:
                for u in range(2):
                    step(i * 2 + u, u, False, False)
            step(B, 0, False, True)
            dve.wait_ge(logits_out, B)
            dve.wait_ge(l_small, 16 * N_SMALL)
            dve.wait_ge(rank_set, E + 1)
            per = [S, B, E]
            link(dve.tensor_tensor(biased[:, :, :], score[:, :, :], bias[0:S, :].unsqueeze(1).broadcast_to(per), ALU.add))
            one_hot_first_max(dve, link, biased[:, :, :], best[:, :], rank[0:S, :], keys[:, :], hot[:, :, :])
            link(dve.tensor_scalar(hot2[:, :, :], hot[:, :, :], -1e30, None, ALU.mult))
            link(dve.tensor_tensor(biased[:, :, :], biased[:, :, :], hot2[:, :, :], ALU.add))
            one_hot_first_max(dve, link, biased[:, :, :], best[:, :], rank[0:S, :], keys[:, :], hot2[:, :, :])
            link(dve.tensor_tensor(hot[:, :, :], hot[:, :, :], hot2[:, :, :], ALU.add))
            link(dve.tensor_tensor(hot[:, :, :], hot[:, :, :], score[:, :, :], ALU.mult))
            link(dve.tensor_reduce(best[:, :], hot[:, :, :], AXX, ALU.add))
            link(dve.tensor_scalar(best[:, :], best[:, :], 1e-8, None, ALU.add))
            link(dve.reciprocal(best[:, :], best[:, :]))
            link(dve.tensor_scalar(best[:, :], best[:, :], 1.0 / R, None, ALU.mult))
            link(dve.tensor_tensor(hot[:, :, :], hot[:, :, :], best[:, :].unsqueeze(2).broadcast_to(per), ALU.mult))
            for e in range(E):
                link(dve.tensor_copy(wexp[:, :, e * R:(e + 1) * R], hot[:, :, e:e + 1].broadcast_to([S, B, R])))

            def hand_over(b, u, wait):
                if wait:
                    dve.wait_ge(wT_done, b - 1)
                dve.tensor_scalar(wexp2[:, u, :], wexp[:, b, :], 1.0, None, ALU.mult).then_inc(w_at, 1)

            hand_over(0, 0, False)
            hand_over(1, 1, False)
            with dve.Fori(1, B // 2) as i:
                for u in range(2):
                    hand_over(i * 2 + u, u, True)
            with dve.Fori(0, J) as j:
                cols = bass.ds(j * T, T)
                dve.wait_ge(wT_out, j + 1)
                for k, u_ in enumerate((ug, uu)):
                    dve.wait_ge(uls, j * 2 + k + 1)
                    dve.tensor_tensor(u_[:, cols], tb[k][0:L, 0:T], wexpT[:, cols], ALU.mult).then_inc(us_out, 1)

            def one_pass(j, first):
                for c in range(FC):
                    rows = P if c < FC - 1 else FR
                    m = j * FC + c
                    dve.wait_ge(sigs, m + 1)
                    dve.tensor_tensor(sg[0:rows, c % 2, :], gb[c % 2][0:rows, 0:T], sg[0:rows, c % 2, :], ALU.mult).then_inc(gs_done, 1)
                    dve.wait_ge(gs_done, m + 1)
                    dve.wait_ge(ups, m + 1)
                    dve.tensor_tensor(hT[0:rows, c, :], upb[c % 2][0:rows, 0:T], sg[0:rows, c % 2, :], ALU.mult).then_inc(h_ready, 1)
                dve.wait_ge(vs, j + 1)
                dve.tensor_tensor(vT[:, :], tb[0][0:L, 0:T], wexpT[:, bass.ds(j * T, T)], ALU.mult).then_inc(v_ready, 1)
                for i in range(SG):
                    dve.wait_ge(outs, j * SG + i + 1)
                    dve.tensor_tensor(x_all[:, j * SG + i, :], ob[i % 2][0:S, :], x_all[:, j * SG + i, :], ALU.add).then_inc(res_done, 1)

            one_pass(0, True)
            with dve.Fori(1, J) as j:
                one_pass(j, False)


def build(nc, A, out):
    with ExitStack() as ctx:
        x_all = ctx.enter_context(nc.sbuf_tensor("x_all", [S, B, D], FP32))
        ident = ctx.enter_context(nc.sbuf_tensor("ident", [P, P], FP32))
        neg_half = ctx.enter_context(nc.sbuf_tensor("neg_half", [P, 1], FP32))
        vd_dram = nc.dram_tensor("vd_rows", [B * ND, D], FP32, kind="Internal").ap()
        part_dram = nc.dram_tensor("first_half", [B, S, D], FP32, kind="Internal").ap()
        phase_constants(nc, ident, neg_half)
        phase_attention0(nc, A, ident, neg_half, x_all, vd_dram)
        phase_select(nc, A, ident, neg_half, x_all)
        phase_attention1(nc, A, ident, neg_half, x_all, part_dram)
        phase_experts(nc, A, ident, neg_half, x_all, out)


def kernel(**inputs):
    import numpy as _np
    import concourse.bacc as _bacc
    from concourse.bass_utils import run_bass_kernel_spmd as _run

    nc = _bacc.Bacc("TRN2", target_bir_lowering=False, num_devices=1)
    arrays, A = {}, {}
    for name, a in inputs.items():
        a = _np.ascontiguousarray(a)
        arrays[f"in_{name}"] = a
        A[name] = nc.dram_tensor(f"in_{name}", a.shape, FP32, kind="ExternalInput").ap()
    out = nc.dram_tensor("out", (B, S, D), FP32, kind="ExternalOutput").ap()
    build(nc, A, out)
    r = _run(nc, [arrays], core_ids=[0])
    return r.results[0]["out"]
```
